# Optimizing a Trainium2 kernel written in Bass

```python
import numpy as np
import jax
import jax.numpy as jnp

def _softmax(x, axis=-1):
    return jax.nn.softmax(x, axis=axis)

def _gelu(x):
    return jax.nn.gelu(x, approximate=True)

def _silu(x):
    return jax.nn.silu(x)

def _sigmoid(x):
    return jax.nn.sigmoid(x)

def _layernorm(x, axis=-1, eps=1e-05):
    m = jnp.mean(x, axis=axis, keepdims=True)
    v = jnp.var(x, axis=axis, keepdims=True)
    return (x - m) / jnp.sqrt(v + eps)

def _scatter_add(tgt, idx, src, axis=0):
    return tgt.at[idx].add(src)

def _segment_sum(src, seg, n):
    return jax.ops.segment_sum(src, seg, n)
kernel_name = 'mk_decoder_preln_d1_seqx_r8_f7c2c1'

def setup_inputs(seed: int=0):
    np.random.seed(seed)
    _w = jnp.asarray

    def _rec_inputs():
        import jax
        import jax.numpy as jnp
        _rk = jax.random.key(seed)
        x = -0.0003929 + 0.9999 * jax.random.normal(jax.random.fold_in(_rk, 1), (16, 64, 256), jnp.float32)
        _lenS = 64 - jax.random.randint(jax.random.fold_in(_rk, 7), (16,), 0, max(1, 64 // 4) + 1, jnp.int32)
        _lenS2 = 64 - jax.random.randint(jax.random.fold_in(_rk, 8), (16,), 0, max(1, 64 // 4) + 1, jnp.int32)
        _ctx_2048P = jax.random.normal(jax.random.fold_in(_rk, 11), (16, 16, 256), jnp.float32)
        _ctx_2048c = jax.random.dirichlet(jax.random.fold_in(_rk, 511), 0.3 * jnp.ones((16,), jnp.float32), (16, 64))
        _ctx_2048t = jnp.einsum('bsk,bkd->bsd', _ctx_2048c, _ctx_2048P)
        _ctx_2048t = _ctx_2048t * jax.lax.rsqrt(jnp.mean(jnp.square(_ctx_2048t)) + 1e-12) * 0.953939
        ctx_2048 = 2.81802e-05 + 1.00001 * (_ctx_2048t + 0.3 * jax.random.normal(jax.random.fold_in(_rk, 611), (16, 64, 256), jnp.float32))
        return (x, ctx_2048)
    x, ctx_2048 = _rec_inputs()

    def _L0_attn_setup():
        import jax, jax.numpy as jnp
        import numpy as np
        HQ, HKV, HD = (32, 8, 64)
        G = HQ // HKV
        SCALE = HD ** (-0.5)

        def _rope(x, offset=0):
            B, L, H, hd = x.shape
            inv = 1.0 / 10000.0 ** (jnp.arange(0, hd, 2, dtype=jnp.float32) / hd)
            pos = jnp.arange(offset, offset + L, dtype=jnp.float32)
            f = pos[:, None] * inv[None, :]
            c = jnp.cos(f)[None, :, None, :]
            s = jnp.sin(f)[None, :, None, :]
            x1, x2 = (x[..., 0::2], x[..., 1::2])
            out = jnp.stack([x1 * c - x2 * s, x1 * s + x2 * c], axis=-1)
            return out.reshape(x.shape)
        key = jax.random.key(seed)
        ks = jax.random.split(key, 5)
        B, L, D = (2, 256, 256)
        w = 0.02
        return {'x': jax.random.normal(ks[0], (B, L, D), dtype=jnp.float32), 'Wq': jax.random.normal(ks[1], (HQ * HD, D), dtype=jnp.float32) * w, 'Wk': jax.random.normal(ks[2], (HKV * HD, D), dtype=jnp.float32) * w, 'Wv': jax.random.normal(ks[3], (HKV * HD, D), dtype=jnp.float32) * w, 'Wo': jax.random.normal(ks[4], (D, HQ * HD), dtype=jnp.float32) * w}
    _L0_attn_all = _L0_attn_setup()
    _L0_attn_in = {k: v for k, v in _L0_attn_all.items() if k in ('Wq', 'Wk', 'Wv', 'Wo')}
    del _L0_attn_all

    def _L0_xattn_setup():
        import jax, jax.numpy as jnp
        import numpy as np
        NUM_HEADS = 8

        def _proj(W, x):
            return jnp.einsum('oi,bin->bon', W, x)

        def _split_heads(x, h):
            B, D, N = x.shape
            return x.reshape(B, D, h, N // h).transpose(2, 0, 1, 3)

        def _mha(XQ, XK, XV, Wq, Wk, Wv, Wo):
            B, D, N = XQ.shape
            h = NUM_HEADS
            Nh = N // h
            q = _split_heads(_proj(Wq, XQ), h)
            k = _split_heads(_proj(Wk, XK), h)
            v = _split_heads(_proj(Wv, XV), h)
            scores = jnp.einsum('hbdn,hben->hbde', q, k) / jnp.sqrt(jnp.asarray(Nh, q.dtype))
            p = jax.nn.softmax(scores, axis=-1)
            out = jnp.einsum('hbde,hben->hbdn', p, v)
            attn_heads = out.transpose(1, 2, 0, 3).reshape(B, D, N)
            return _proj(Wo, XQ - attn_heads)
        key = jax.random.key(seed)
        ks = jax.random.split(key, 7)
        B, D, N = (16, 64, 256)
        sc = 1.0 / np.sqrt(D)
        return {'X_Query': jax.random.normal(ks[0], (B, D, N), jnp.float32), 'X_Key': jax.random.normal(ks[1], (B, D, N), jnp.float32), 'X_Value': jax.random.normal(ks[2], (B, D, N), jnp.float32), 'W_q': jax.random.normal(ks[3], (D, D), jnp.float32) * sc, 'W_k': jax.random.normal(ks[4], (D, D), jnp.float32) * sc, 'W_v': jax.random.normal(ks[5], (D, D), jnp.float32) * sc, 'W_o': jax.random.normal(ks[6], (D, D), jnp.float32) * sc}
    _L0_xattn_all = _L0_xattn_setup()
    _L0_xattn_in = {k: v for k, v in _L0_xattn_all.items() if k in ('W_q', 'W_k', 'W_v', 'W_o')}
    del _L0_xattn_all

    def _L0_ffn_setup():
        import jax, jax.numpy as jnp
        import numpy as np
        DIM = 256
        INTER = 176
        E = 16
        TOPK = 4
        G = 4
        TOPK_G = 2
        N_SHARED = 2
        ROUTE_SCALE = 1.0
        INIT_STD = 0.02
        B, S = (1, 256)
        key = jax.random.key(seed)
        ks = jax.random.split(key, 9)
        std = INIT_STD
        x = jax.random.normal(ks[0], (B, S, DIM), jnp.float32)
        gate_w = jax.random.normal(ks[1], (E, DIM), jnp.float32) * std
        expert_bias = jnp.zeros((E,), jnp.float32)
        w1 = jax.random.normal(ks[2], (E, DIM, INTER), jnp.float32) * std
        w3 = jax.random.normal(ks[3], (E, DIM, INTER), jnp.float32) * std
        w2 = jax.random.normal(ks[4], (E, INTER, DIM), jnp.float32) * std
        sh = N_SHARED * INTER
        sw1 = jax.random.normal(ks[5], (DIM, sh), jnp.float32) * std
        sw3 = jax.random.normal(ks[6], (DIM, sh), jnp.float32) * std
        sw2 = jax.random.normal(ks[7], (sh, DIM), jnp.float32) * std
        return {'x': x, 'gate_w': gate_w, 'expert_bias': expert_bias, 'w1': w1, 'w2': w2, 'w3': w3, 'sw1': sw1, 'sw2': sw2, 'sw3': sw3}
    _L0_ffn_all = _L0_ffn_setup()
    _L0_ffn_in = {k: v for k, v in _L0_ffn_all.items() if k in ('gate_w', 'expert_bias', 'w1', 'w2', 'w3', 'sw1', 'sw2', 'sw3')}
    del _L0_ffn_all
    return {'x': x, 'ctx_2048': ctx_2048, 'L0_attn_Wq': _L0_attn_in['Wq'], 'L0_attn_Wk': _L0_attn_in['Wk'], 'L0_attn_Wv': _L0_attn_in['Wv'], 'L0_attn_Wo': _L0_attn_in['Wo'], 'L0_xattn_W_q': _L0_xattn_in['W_q'], 'L0_xattn_W_k': _L0_xattn_in['W_k'], 'L0_xattn_W_v': _L0_xattn_in['W_v'], 'L0_xattn_W_o': _L0_xattn_in['W_o'], 'L0_ffn_gate_w': _L0_ffn_in['gate_w'], 'L0_ffn_expert_bias': _L0_ffn_in['expert_bias'], 'L0_ffn_w1': _L0_ffn_in['w1'], 'L0_ffn_w2': _L0_ffn_in['w2'], 'L0_ffn_w3': _L0_ffn_in['w3'], 'L0_ffn_sw1': _L0_ffn_in['sw1'], 'L0_ffn_sw2': _L0_ffn_in['sw2'], 'L0_ffn_sw3': _L0_ffn_in['sw3']}

def reference(x, ctx_2048, L0_attn_Wq, L0_attn_Wk, L0_attn_Wv, L0_attn_Wo, L0_xattn_W_q, L0_xattn_W_k, L0_xattn_W_v, L0_xattn_W_o, L0_ffn_gate_w, L0_ffn_expert_bias, L0_ffn_w1, L0_ffn_w2, L0_ffn_w3, L0_ffn_sw1, L0_ffn_sw2, L0_ffn_sw3):
    import jax
    import jax.numpy as jnp

    def _L0_attn_ref(x, Wq, Wk, Wv, Wo):
        import jax, jax.numpy as jnp
        import numpy as np
        HQ, HKV, HD = (32, 8, 64)
        G = HQ // HKV
        SCALE = HD ** (-0.5)

        def _rope(x, offset=0):
            B, L, H, hd = x.shape
            inv = 1.0 / 10000.0 ** (jnp.arange(0, hd, 2, dtype=jnp.float32) / hd)
            pos = jnp.arange(offset, offset + L, dtype=jnp.float32)
            f = pos[:, None] * inv[None, :]
            c = jnp.cos(f)[None, :, None, :]
            s = jnp.sin(f)[None, :, None, :]
            x1, x2 = (x[..., 0::2], x[..., 1::2])
            out = jnp.stack([x1 * c - x2 * s, x1 * s + x2 * c], axis=-1)
            return out.reshape(x.shape)
        B, L, D = x.shape
        q = (x @ Wq.T).reshape(B, L, HQ, HD)
        k = (x @ Wk.T).reshape(B, L, HKV, HD)
        v = (x @ Wv.T).reshape(B, L, HKV, HD)
        q = _rope(q)
        k = _rope(k)
        qh = q.transpose(0, 2, 1, 3).reshape(B, HKV, G, L, HD)
        kh = k.transpose(0, 2, 1, 3)
        vh = v.transpose(0, 2, 1, 3)
        attn = jnp.einsum('bkgqd,bkld->bkgql', qh, kh) * SCALE
        causal = jnp.arange(L)[:, None] >= jnp.arange(L)[None, :]
        attn = jnp.where(causal[None, None, None], attn, -jnp.inf)
        p = jax.nn.softmax(attn, axis=-1)
        out = jnp.einsum('bkgql,bkld->bkgqd', p, vh)
        out = out.reshape(B, HQ, L, HD).transpose(0, 2, 1, 3).reshape(B, L, HQ * HD)
        return out @ Wo.T

    def _L0_xattn_ref(X_Query, X_Key, X_Value, W_q, W_k, W_v, W_o):
        import jax, jax.numpy as jnp
        import numpy as np
        NUM_HEADS = 8

        def _proj(W, x):
            return jnp.einsum('oi,bin->bon', W, x)

        def _split_heads(x, h):
            B, D, N = x.shape
            return x.reshape(B, D, h, N // h).transpose(2, 0, 1, 3)

        def _mha(XQ, XK, XV, Wq, Wk, Wv, Wo):
            B, D, N = XQ.shape
            h = NUM_HEADS
            Nh = N // h
            q = _split_heads(_proj(Wq, XQ), h)
            k = _split_heads(_proj(Wk, XK), h)
            v = _split_heads(_proj(Wv, XV), h)
            scores = jnp.einsum('hbdn,hben->hbde', q, k) / jnp.sqrt(jnp.asarray(Nh, q.dtype))
            p = jax.nn.softmax(scores, axis=-1)
            out = jnp.einsum('hbde,hben->hbdn', p, v)
            attn_heads = out.transpose(1, 2, 0, 3).reshape(B, D, N)
            return _proj(Wo, XQ - attn_heads)
        return _mha(X_Query, X_Key, X_Value, W_q, W_k, W_v, W_o)

    def _L0_ffn_ref(x, gate_w, expert_bias, w1, w2, w3, sw1, sw2, sw3):
        import jax, jax.numpy as jnp
        import numpy as np
        DIM = 256
        INTER = 176
        E = 16
        TOPK = 4
        G = 4
        TOPK_G = 2
        N_SHARED = 2
        ROUTE_SCALE = 1.0
        INIT_STD = 0.02
        B, S = (1, 256)
        b, s, d = x.shape
        T = b * s
        xf = x.reshape(T, d)
        scores = jax.nn.sigmoid(xf @ gate_w.T)
        original_scores = scores
        scores = scores + expert_bias
        sg = scores.reshape(T, G, E // G)
        group_scores = sg.max(axis=-1)
        _, gidx = jax.lax.top_k(group_scores, TOPK_G)
        gmask = jnp.zeros((T, G), bool).at[jnp.arange(T)[:, None], gidx].set(True)
        masked = jnp.where(gmask[:, :, None], sg, -jnp.inf).reshape(T, E)
        _, idx = jax.lax.top_k(masked, TOPK)
        w = jnp.take_along_axis(original_scores, idx, axis=1)
        w = w / jnp.sum(w, axis=-1, keepdims=True)
        w = w * ROUTE_SCALE
        cw = jnp.zeros((T, E), x.dtype).at[jnp.arange(T)[:, None], idx].add(w)
        h = jax.nn.silu(jnp.einsum('td,edh->teh', xf, w1)) * jnp.einsum('td,edh->teh', xf, w3)
        y = jnp.einsum('teh,ehd,te->td', h, w2, cw)
        z = jax.nn.silu(xf @ sw1) * (xf @ sw3) @ sw2
        return (y + z).reshape(b, s, d)
    x = x + _L0_attn_ref(_layernorm(x, axis=-1), L0_attn_Wq, L0_attn_Wk, L0_attn_Wv, L0_attn_Wo)
    x = x + _L0_xattn_ref(_layernorm(x, axis=-1), ctx_2048, ctx_2048, L0_xattn_W_q, L0_xattn_W_k, L0_xattn_W_v, L0_xattn_W_o)
    x = x + _L0_ffn_ref(_layernorm(x, axis=-1), L0_ffn_gate_w, L0_ffn_expert_bias, L0_ffn_w1, L0_ffn_w2, L0_ffn_w3, L0_ffn_sw1, L0_ffn_sw2, L0_ffn_sw3)
    return x

_drawn_inputs = setup_inputs


def setup_inputs(seed=0):
    import zlib

    import numpy as np

    out = dict(_drawn_inputs(seed))
    spreads = {'L0_ffn_expert_bias': (0.0, 0.8)}
    factors = {'L0_attn_Wq': 8.0,
     'L0_attn_Wk': 7.993,
     'L0_ffn_gate_w': 8.0,
     'L0_ffn_w1': 8.0,
     'L0_ffn_w2': 8.0,
     'L0_ffn_w3': 8.0,
     'L0_ffn_sw1': 4.104,
     'L0_ffn_sw2': 4.058,
     'L0_ffn_sw3': 4.05}
    for name, (base, spread) in spreads.items():
        noise = np.random.default_rng([zlib.crc32(name.encode()), seed]).standard_normal(out[name].shape)
        drawn = base * np.exp(spread * noise) if base else spread * noise
        out[name] = jnp.asarray(drawn.astype(out[name].dtype))
    for name, factor in factors.items():
        out[name] = (out[name] * factor).astype(out[name].dtype)
    return out
```

```python
from contextlib import ExitStack

import numpy as np

import concourse.bass as bass
from concourse import mybir

F32 = mybir.dt.float32
F32R = mybir.dt.float32r
BF16 = mybir.dt.bfloat16
ALU = mybir.AluOpType
ACT = mybir.ActivationFunctionType
AX = mybir.AxisListType

P = 128
B, SEQ, D = 16, 64, 256
T = B * SEQ
NT = T // P
KC = D // P
HALF = 512
NHALF = T // HALF
EPS = 1e-5

HQ, HKV, HD = 32, 8, 64
G = HQ // HKV
F = HD // 2
SCALE = float(HD) ** -0.5
NPAIR = 2 * G + 2
MASKED = -1e30

XH = 8
XN = D // XH
XSCALE = float(XN) ** -0.5

E = 16
INTER = 176
GE = 4
TOPK, TOPG = 4, 2
EG = 8
UNIT = P // EG
NU = INTER // UNIT
NEC = (E // EG) * NU
SH = 2 * INTER
NSC = (SH + P - 1) // P
NC = NEC + NSC


def as_f32(ap):
    return ap.bitcast(F32)


def bc(ap, axis, n):
    a = ap.unsqueeze(axis)
    shape = list(a.shape)
    shape[axis] = n
    return a.broadcast_to(shape)


class Steps:

    def __init__(self, total, lag):
        self.total, self.lag = total, lag

    def run(self, eng, step):
        for r in range(8):
            step(0, r)
        if self.total > 8:
            with eng.Fori(1, self.total // 8) as i:
                for r in range(8):
                    step(i, r)
        for r in range(self.lag):
            step(self.total // 8, r)

    def live(self, i, q):
        return not isinstance(i, int) or 0 <= 8 * i + q < self.total

    def later(self, i, q, n):
        return not isinstance(i, int) or 8 * i + q >= n


class Kit:

    def __init__(self, nc, ctx):
        self.nc, self.ctx = nc, ctx

    def sb(self, name, shape, dt=F32):
        return self.ctx.enter_context(self.nc.sbuf_tensor(name, shape, dt))

    def bank(self, name, n=1):
        shape = [P, HALF] if n == 1 else [P, n, HALF]
        return self.ctx.enter_context(self.nc.psum_tensor(name, shape, F32))

    def sem(self, name):
        return self.ctx.enter_context(self.nc.semaphore(name))


def split3(pe, out, w, x, w_sl, x_sl, first, last):
    pe.matmul(out, w[0][w_sl], x[0][x_sl], start=first, stop=False)
    pe.matmul(out, w[0][w_sl], x[1][x_sl], start=False, stop=False)
    return pe.matmul(out, w[1][w_sl], x[0][x_sl], start=False, stop=last)


def norm_stats(nc, dve, X, st, mv, s_stat, s_x=None):
    for t in range(NT):
        if s_x and t % 2 == 0:
            dve.wait_ge(s_x[t // 2], 16)
        nc.vector.bn_stats(st[:, t, :], X[:, t, :]).then_inc(s_stat, 1)
    for t in range(NT):
        dve.wait_ge(s_stat, t + 1)
        last = nc.vector.bn_aggr(mv[:, t, :], st[:, t, :])
    last.then_inc(s_stat, 1)
    dve.wait_ge(s_stat, NT + 1)


def norm_rstd(nc, dve, mv, std, rstd, tmp, s_var, s_std, s_stat, n0, between=None):
    nc.vector.tensor_scalar(tmp[:, 0, :], mv[:, :, 1], EPS, None, ALU.add).then_inc(s_var, 1)
    if between:
        between()
    dve.wait_ge(s_std, 1)
    nc.vector.reciprocal(rstd[:, 0, :], std[:]).then_inc(s_stat, 1)
    dve.wait_ge(s_stat, n0 + 1)
    nc.vector.tensor_tensor(tmp[:, 1, :], rstd[:, 0, :], rstd[:, 0, :], ALU.mult).then_inc(s_stat, 1)
    dve.wait_ge(s_stat, n0 + 2)
    nc.vector.tensor_tensor(tmp[:, 2, :], tmp[:, 1, :], tmp[:, 0, :], ALU.mult).then_inc(s_stat, 1)
    dve.wait_ge(s_stat, n0 + 3)
    nc.vector.tensor_scalar(tmp[:, 3, :], tmp[:, 2, :], -0.5, 1.5, ALU.mult, ALU.add).then_inc(s_stat, 1)
    dve.wait_ge(s_stat, n0 + 4)
    nc.vector.tensor_tensor(rstd[:, 1, :], rstd[:, 0, :], tmp[:, 3, :], ALU.mult).then_inc(s_stat, 1)
    dve.wait_ge(s_stat, n0 + 5)


def qkv_phase(nc, X, QR, KR, V, WO, ident, x_d, wqk_d, wv_d, wo_d, cs_d, ident_d):
    NW = NPAIR + KC
    NWO = 16 * D // HALF
    with ExitStack() as ctx:
        k = Kit(nc, ctx)
        raw = [k.sb(f"w_raw{i}", [P, HALF]) for i in range(2)]
        raw_o = [k.sb(f"wo_raw{i}", [P, HALF]) for i in range(2)]
        w = [[k.sb(f"w_{n}{i}", [P, HALF], F32R) for n in ("hi", "lo")] for i in range(2)]
        xnT = [k.sb(f"xnT_{n}", [P, KC, T], F32R) for n in ("hi", "lo")]
        prod = k.sb("rope_products", [P, 2, 4, HALF])
        xn = prod[:].rearrange("p a b c -> p (a b c)")[:, 0:NT * D].rearrange("p (t d) -> p t d", t=NT)
        cs = k.sb("cos_sin", [P, 2, SEQ])
        st = k.sb("stats", [P, NT, 6])
        mv = k.sb("mean_var", [P, NT, 2])
        std = k.sb("std", [P, NT])
        rstd = k.sb("rstd", [P, 2, NT])
        tmp = k.sb("norm_tmp", [P, 4, NT])
        ps_t = k.bank("ps_transposed", 4)
        ps_v = [k.bank(f"ps_v{i}") for i in range(2)]
        proj = [ps_t[:, 2 * i:2 * i + 2, :] for i in range(2)]

        s_x = [k.sem(f"p1_x{i}") for i in range(4)]
        s_const = k.sem("p1_const")
        s_raw = [k.sem(f"p1_raw{i}") for i in range(2)]
        s_raw_o = [k.sem(f"p1_raw_o{i}") for i in range(2)]
        s_hi = k.sem("p1_w_hi")
        s_lo = k.sem("p1_w_lo")
        s_hi_o = k.sem("p1_wo_hi")
        s_lo_o = k.sem("p1_wo_lo")
        s_stat = k.sem("p1_stat")
        s_var = k.sem("p1_var")
        s_std = k.sem("p1_std")
        s_xn = k.sem("p1_xn")
        s_tr = k.sem("p1_transposed")
        s_xhi = k.sem("p1_xnT_hi")
        s_xlo = k.sem("p1_xnT_lo")
        s_vps = k.sem("p1_v_psum")
        s_vsb = k.sem("p1_v_copied")
        s_proj = k.sem("p1_projected")
        s_prod = k.sem("p1_products")
        s_rot = k.sem("p1_rotated")
        block = ctx.enter_context(nc.Block())

        def wo_dst(c):
            return [o[:, 2 * c:2 * c + 2, :].rearrange("p c n -> p (c n)") for o in WO]

        @block.sync
        def _(sp):
            for q in range(4):
                sp.dma_start(X[:, 2 * q:2 * q + 2, :], x_d[:, 2 * q:2 * q + 2, :]).then_inc(s_x[q], 16)
            sp.dma_start(ident[:], ident_d).then_inc(s_const, 16)
            for c in range(2):
                sp.dma_start(raw[c][:], wqk_d[c]).then_inc(s_raw[c], 16)
            sp.dma_start(cs[:], cs_d).then_inc(s_const, 16)
            for c in range(NWO):
                if c >= 2:
                    sp.wait_ge(s_lo_o, c - 1)
                sp.dma_start(raw_o[c % 2][:], wo_d[c]).then_inc(s_raw_o[c % 2], 16)
            for c in range(2, NW):
                sp.wait_ge(s_lo, c - 1)
                sp.dma_start(raw[c % 2][:], wqk_d[c] if c < NPAIR else wv_d[:, c - NPAIR, :]
                             ).then_inc(s_raw[c % 2], 16)

        @block.gpsimd
        def _(pool):
            for c in range(NWO):
                hi, lo = wo_dst(c)
                pool.wait_ge(s_hi_o, c + 1)
                nc.gpsimd.tensor_tensor(lo, raw_o[c % 2][:], as_f32(hi), ALU.subtract).then_inc(s_lo_o, 1)
            for m in range(NPAIR):
                for h in range(2):
                    pool.wait_ge(s_prod, 2 * m + h + 1)
                    pr = prod[:, h, :, :]
                    if m < 2 * G:
                        dst = [QR[:, a, 4 * h:4 * h + 4, :].rearrange(
                            "p t (b m s) -> p (t b) m s", b=2, s=SEQ)[:, :, m, :] for a in range(2)]
                        pr = pr.rearrange("p n (t s) -> p n t s", s=SEQ)
                    else:
                        dst = [KR[:, a, 4 * h:4 * h + 4, m - 2 * G, :] for a in range(2)]
                        pr = pr.rearrange("p n (t c) -> p n t c", c=P)
                    nc.gpsimd.tensor_tensor(dst[0], pr[:, 0], pr[:, 3], ALU.subtract)
                    nc.gpsimd.tensor_tensor(dst[1], pr[:, 1], pr[:, 2], ALU.add).then_inc(s_rot, 1)

        @block.scalar
        def _(act):
            def high_half(c):
                act.wait_ge(s_raw[c % 2], 16 * (c // 2 + 1))
                nc.scalar.copy(w[c % 2][0][:], raw[c % 2][:]).then_inc(s_hi, 1)

            def high_half_o(c):
                act.wait_ge(s_raw_o[c % 2], 16 * (c // 2 + 1))
                nc.scalar.copy(wo_dst(c)[0], raw_o[c % 2][:]).then_inc(s_hi_o, 1)

            high_half(0)
            high_half(1)
            act.wait_ge(s_var, 1)
            nc.scalar.activation(std[:], tmp[:, 0, :], ACT.Sqrt).then_inc(s_std, 1)
            for c in range(4):
                high_half_o(c)
            for n in range(KC * NHALF):
                kc, h = n % KC, n // KC
                act.wait_ge(s_tr, n + 1)
                nc.scalar.copy(xnT[0][:, kc, h * HALF:(h + 1) * HALF], ps_t[:, n, :]).then_inc(s_xhi, 1)
            for c in range(4, NWO):
                high_half_o(c)
            for c in range(2, NW):
                act.wait_ge(s_proj, 4 * (c - 1))
                high_half(c)
            for t in range(NT):
                act.wait_ge(s_vps, t + 1)
                nc.scalar.copy(V[:, t, :], ps_v[t % 2][:]).then_inc(s_vsb, 1)

        @block.vector
        def _(dve):
            def low_half(i, r):
                dve.wait_ge(s_hi, 2 * i + r + 1)
                nc.vector.tensor_tensor(w[r % 2][1][:], raw[r % 2][:], as_f32(w[r % 2][0][:]),
                                        ALU.subtract).then_inc(s_lo, 1)

            norm_stats(nc, dve, X, st, mv, s_stat, s_x)
            norm_rstd(nc, dve, mv, std, rstd, tmp, s_var, s_std, s_stat, NT + 1)
            for t in range(NT):
                nc.vector.tensor_scalar(xn[:, t, :], X[:, t, :], mv[:, t, 0:1], rstd[:, 1, t:t + 1],
                                        ALU.subtract, ALU.mult).then_inc(s_xn, 1)
            low_half(0, 0)
            low_half(0, 1)
            for n in range(KC * NHALF):
                kc, h = n % KC, n // KC
                tok = slice(h * HALF, (h + 1) * HALF)
                dve.wait_ge(s_xhi, n + 1)
                nc.vector.tensor_tensor(xnT[1][:, kc, tok], ps_t[:, n, :], as_f32(xnT[0][:, kc, tok]),
                                        ALU.subtract).then_inc(s_xlo, 1)
            dve.wait_ge(s_const, 32)

            def products(i, r):
                ps, pr = proj[r % 2], prod[:, r % 2, :, :]
                if not isinstance(i, int) or r >= 2:
                    dve.wait_ge(s_rot, 4 * i + r - 1)
                for a in range(2):
                    dve.wait_ge(s_proj, 8 * i + 2 * r + a + 1)
                    src = ps[:, a, :].rearrange("p (b s) -> p b s", s=SEQ)
                    for m in range(2):
                        last = nc.vector.tensor_tensor(
                            pr[:, 2 * a + m, :].rearrange("p (b s) -> p b s", s=SEQ), src,
                            bc(cs[:, m, :], 1, HALF // SEQ), ALU.mult)
                last.then_inc(s_prod, 1)

            def two_pairs(i):
                for r in range(4):
                    products(i, r)
                    if r % 2:
                        low_half(i, 2 + r // 2)

            two_pairs(0)
            with dve.Fori(1, NPAIR // 2) as i:
                two_pairs(i)

        @block.tensor
        def _(pe):
            pe.wait_ge(s_const, 32)
            for h in range(NHALF):
                for kc in range(KC):
                    for q in range(4):
                        t = 4 * h + q
                        pe.wait_ge(s_xn, t + 1)
                        last = nc.tensor.transpose(ps_t[:, 2 * h + kc, q * P:(q + 1) * P],
                                                   xn[:, t, kc * P:(kc + 1) * P], ident[:])
                    last.then_inc(s_tr, 1)

            def project(i, r):
                h = r % 2
                wv = [x[:].rearrange("p (k a m) -> p k a m", k=KC, a=2) for x in w[r // 2]]
                if h == 0:
                    pe.wait_ge(s_lo, 2 * i + r // 2 + 1)
                if isinstance(i, int) and r < 2:
                    pe.wait_ge(s_xlo, 4)
                else:
                    pe.wait_ge(s_prod, 4 * i + r - 1)
                for a in range(2):
                    for kc in range(KC):
                        last = split3(nc.tensor, proj[r % 2][:, a, :], wv, xnT, (slice(None), kc, a),
                                      (slice(None), kc, slice(h * HALF, (h + 1) * HALF)), kc == 0, kc == KC - 1)
                    last.then_inc(s_proj, 1)

            for r in range(4):
                project(0, r)
            with pe.Fori(1, NPAIR // 2) as i:
                for r in range(4):
                    project(i, r)
            pe.wait_ge(s_lo, NW)
            for t in range(NT):
                if t >= 2:
                    pe.wait_ge(s_vsb, t - 1)
                for kc in range(KC):
                    last = split3(nc.tensor, ps_v[t % 2][:], xnT, w[kc], (slice(None), kc, slice(t * P, (t + 1) * P)),
                                  (slice(None),), kc == 0, kc == KC - 1)
                last.then_inc(s_vps, 1)


def attention_phase(nc, X, QR, KR, V, WO, ident, mask_d):
    NUN = 4 * NT
    steps = Steps(NUN, 7)
    with ExitStack() as ctx:
        k = Kit(nc, ctx)
        Q = [k.sb(f"q_tile{i}", [P, 2, 2 * 2 * G * SEQ]) for i in range(2)]
        KB = [k.sb(f"k_blocks{i}", [P, 2, 2, 2, P]) for i in range(2)]
        VB = [k.sb(f"v_blocks{i}", [P, 2, 4, P]) for i in range(2)]
        EX = k.sb("probabilities", [P, 4, 4, P])
        PT = k.sb("probs_T", [P, 2, 2, 2 * P])
        OT = [[k.sb(f"out_T_{n}{i}", [P, 2 * G, P], F32R) for n in ("hi", "lo")] for i in range(2)]
        mask_f = k.sb("mask_f", [P, P])
        mask = k.sb("mask", [P, 4, P], BF16)
        ident_b = k.sb("ident_b", [P, P], BF16)
        mx = k.sb("row_max", [P, 2, 8])
        sm = k.sb("row_sum", [P, 2, 8])
        ri = k.sb("row_inv", [P, 4, 8])
        ps_s = [k.bank(f"ps_scores{i}") for i in range(2)]
        ps_p = [k.bank(f"ps_probsT{i}") for i in range(2)]
        ps_o = [k.bank(f"ps_outT{i}") for i in range(2)]
        ps_y = [k.bank(f"ps_y{i}") for i in range(2)]

        s_mask = k.sem("p2_mask")
        s_zero = k.sem("p2_zero")
        s_mb = k.sem("p2_mask_ready")
        s_qk = [k.sem(f"p2_qk_staged{i}") for i in range(2)]
        s_vb = [k.sem(f"p2_v_staged{i}") for i in range(2)]
        s_scores = k.sem("p2_scores")
        s_max = k.sem("p2_max")
        s_shift = k.sem("p2_shifted")
        s_exp = k.sem("p2_exp")
        s_sum = k.sem("p2_sum")
        s_inv = k.sem("p2_inverse")
        s_norm = k.sem("p2_normalised")
        s_pT = k.sem("p2_probs_transposed")
        s_pTc = k.sem("p2_probsT_copied")
        s_pv = k.sem("p2_values_mixed")
        s_ohi = k.sem("p2_outT_hi")
        s_olo = k.sem("p2_outT_lo")
        s_y = k.sem("p2_out_projected")
        s_res = k.sem("p2_residual")
        N_QK, N_V = 16, 4
        block = ctx.enter_context(nc.Block())

        def stage_qk(sp, t, r):
            for gl in range(2):
                for a in range(2):
                    for g2 in range(2):
                        src = slice((2 * gl + g2) * F, (2 * gl + g2 + 1) * F)
                        dst = slice(g2 * HD + a * F, g2 * HD + (a + 1) * F)
                        sp.dma_start(Q[r][dst, gl, :], QR[src, a, bass.ds(t, 1), :].rearrange("p o n -> p (o n)")
                                     ).then_inc(s_qk[r], 16)
                        sp.dma_start(
                            KB[r][dst, gl, :, :, g2 * HD:(g2 + 1) * HD].rearrange("p s b t -> p (s b) t"),
                            KR[src, a, bass.ds(t, 1), :, :].rearrange("p o s (b t) -> p (o s b) t", b=2),
                        ).then_inc(s_qk[r], 16)

        def stage_v(sp, t, r):
            for b in range(2):
                for g2 in range(2):
                    sp.dma_start(
                        VB[r][g2 * HD:(g2 + 1) * HD, b, :, g2 * HD:(g2 + 1) * HD],
                        V[b * SEQ:(b + 1) * SEQ, bass.ds(t, 1), :].rearrange(
                            "p o (gp g d) -> p (o gp) g d", gp=4, g=2)[:, :, g2, :],
                    ).then_inc(s_vb[r], 16)

        @block.sync
        def _(sp):
            sp.dma_start(mask_f[:], mask_d).then_inc(s_mask, 16)
            sp.wait_ge(s_zero, 2)
            for r in range(2):
                stage_qk(sp, r, r)
                stage_v(sp, r, r)
            with sp.Fori(1, NT // 2) as i:
                for r in range(2):
                    sp.wait_ge(s_scores, 8 * i + 4 * r - 4)
                    stage_qk(sp, 2 * i + r, r)
                    sp.wait_ge(s_pv, 8 * i + 4 * r - 4)
                    stage_v(sp, 2 * i + r, r)

        @block.gpsimd
        def _(pool):
            for r in range(2):
                nc.gpsimd.memset(KB[r][:], 0.0)
                nc.gpsimd.memset(VB[r][:], 0.0).then_inc(s_zero, 1)

            def step(i, r):
                q = r - 1
                if steps.live(i, q):
                    pool.wait_ge(s_inv, 8 * i + q + 1)
                    e = EX[:, q % 4, :, :].rearrange("p x (g s) -> p (x g) s", g=2)
                    nc.gpsimd.tensor_tensor(e, e, bc(ri[:, q % 4, :], 2, SEQ), ALU.mult).then_inc(s_norm, 1)

            steps.run(pool, step)

        @block.scalar
        def _(act):
            def step(i, r):
                if steps.live(i, r):
                    act.wait_ge(s_shift, 8 * i + r + 1)
                    nc.scalar.activation(EX[:, r % 4, :, :], EX[:, r % 4, :, :], ACT.Exp,
                                         scale=SCALE).then_inc(s_exp, 1)
                q = r - 2
                if steps.live(i, q):
                    act.wait_ge(s_pT, 8 * i + q + 1)
                    if steps.later(i, q, 2):
                        act.wait_ge(s_pv, 8 * i + q - 1)
                    nc.scalar.copy(PT[:, q % 2, :, :].rearrange("p a n -> p (a n)"),
                                   ps_p[q % 2][:]).then_inc(s_pTc, 1)
                q = r - 3
                if steps.live(i, q):
                    act.wait_ge(s_pv, 8 * i + q + 1)
                    if steps.later(i, q, 4):
                        act.wait_ge(s_y, 8 * i + 2 * (q // 2) - 2)
                    b = q % 2
                    nc.scalar.copy(OT[(q // 2) % 2][0][:, :, b * SEQ:(b + 1) * SEQ],
                                   ps_o[q % 2][:].rearrange("p (c s) -> p c s", s=SEQ)).then_inc(s_ohi, 1)

            steps.run(act, step)

        @block.vector
        def _(dve):
            dve.wait_ge(s_mask, 16)
            nc.vector.tensor_copy(mask[:], bc(mask_f[:], 1, 4)).then_inc(s_mb, 1)
            nc.vector.tensor_copy(ident_b[:], ident[:]).then_inc(s_mb, 1)

            def step(i, r):
                if steps.live(i, r):
                    rows = ps_s[r % 2][:].rearrange("p (x s) -> p x s", s=SEQ)
                    dve.wait_ge(s_scores, 8 * i + r + 1)
                    nc.vector.tensor_reduce(mx[:, r % 2, :], rows, AX.X, ALU.max).then_inc(s_max, 1)
                    dve.wait_ge(s_max, 8 * i + r + 1)
                    if steps.later(i, r, 4):
                        dve.wait_ge(s_pT, 8 * i + r - 3)
                    nc.vector.tensor_tensor(EX[:, r % 4, :, :].rearrange("p x (g s) -> p (x g) s", g=2), rows,
                                            bc(mx[:, r % 2, :], 2, SEQ), ALU.subtract).then_inc(s_shift, 1)
                q = r - 4
                if steps.live(i, q):
                    b, ot = q % 2, OT[(q // 2) % 2]
                    dve.wait_ge(s_ohi, 8 * i + q + 1)
                    hi, lo = (o[:, :, b * SEQ:(b + 1) * SEQ] for o in ot)
                    nc.vector.tensor_tensor(lo, ps_o[q % 2][:].rearrange("p (c s) -> p c s", s=SEQ), as_f32(hi),
                                            ALU.subtract).then_inc(s_olo, 1)
                q = r - 1
                if steps.live(i, q):
                    dve.wait_ge(s_exp, 8 * i + q + 1)
                    nc.vector.tensor_reduce(sm[:, q % 2, :], EX[:, q % 4, :, :].rearrange("p x (g s) -> p (x g) s", g=2),
                                            AX.X, ALU.add).then_inc(s_sum, 1)
                    dve.wait_ge(s_sum, 8 * i + q + 1)
                    nc.vector.reciprocal(ri[:, q % 4, :], sm[:, q % 2, :]).then_inc(s_inv, 1)
                q = r - 6
                if steps.live(i, q) and q % 4 == 3:
                    t = 2 * i + q // 4
                    dve.wait_ge(s_y, 8 * i + q + 1)
                    x = X[:, bass.ds(t, 1), :].rearrange("p o d -> p (o d)")
                    nc.vector.tensor_tensor(x, ps_y[(q // 4) % 2][:, 0:D], x, ALU.add).then_inc(s_res, 1)

            steps.run(dve, step)

        @block.tensor
        def _(pe):
            pe.wait_ge(s_mb, 2)

            def step(i, r):
                if steps.live(i, r):
                    ring, gh, b = (r // 4) % 2, (r // 2) % 2, r % 2
                    if r % 4 == 0:
                        pe.wait_ge(s_qk[ring], 16 * N_QK * i + 16 * N_QK)
                    if steps.later(i, r, 2):
                        pe.wait_ge(s_shift, 8 * i + r - 1)
                    nc.tensor.matmul(ps_s[r % 2][:], ident_b[:], mask[:].rearrange("p x n -> p (x n)"),
                                     start=True, stop=False)
                    for x in range(4):
                        s, m0 = x // 2, (2 * G * b + 2 * x) * SEQ
                        last = nc.tensor.matmul(ps_s[r % 2][:, x * P:(x + 1) * P],
                                                Q[ring][:, gh, m0:m0 + P],
                                                KB[ring][:, gh, s, b, :], start=False, stop=x == 3)
                    last.then_inc(s_scores, 1)
                q = r - 2
                if steps.live(i, q):
                    pe.wait_ge(s_norm, 8 * i + q + 1)
                    if steps.later(i, q, 2):
                        pe.wait_ge(s_pTc, 8 * i + q - 1)
                    for x in range(4):
                        last = nc.tensor.transpose(ps_p[q % 2][:, x * P:(x + 1) * P], EX[:, q % 4, x, :], ident[:])
                    last.then_inc(s_pT, 1)
                q = r - 3
                if steps.live(i, q):
                    ring, gh, b = (q // 4) % 2, (q // 2) % 2, q % 2
                    if q % 4 == 0:
                        j = i + q // 8
                        pe.wait_ge(s_vb[ring], 16 * N_V * j + 16 * N_V)
                    pe.wait_ge(s_pTc, 8 * i + q + 1)
                    if steps.later(i, q, 2):
                        pe.wait_ge(s_olo, 8 * i + q - 1)
                    for x in range(2):
                        last = nc.tensor.matmul(ps_o[q % 2][:, x * 2 * P:(x + 1) * 2 * P],
                                                VB[ring][:, b, 2 * x + gh, :], PT[:, q % 2, x, :],
                                                start=True, stop=True)
                    last.then_inc(s_pv, 1)
                q = r - 6
                if steps.live(i, q):
                    v, part = q // 2, q % 2
                    if part == 0:
                        pe.wait_ge(s_olo, 8 * i + 2 * v + 2)
                    if q % 4 == 0 and steps.later(i, q, 8):
                        pe.wait_ge(s_res, 2 * i + q // 4 - 1)
                    for c in range(4 * part, 4 * part + 4):
                        last = split3(nc.tensor, ps_y[(q // 4) % 2][:, 0:D], OT[v % 2], WO,
                                      (slice(None), c), (slice(None), 8 * (v % 2) + c),
                                      q % 4 == 0 and c == 0, q % 4 == 3 and c == 7)
                    last.then_inc(s_y, 1)

            steps.run(pe, step)


def cross_phase(nc, X, ident, ctx_d, wx_d):
    NJOB = 3 * NT // 2
    with ExitStack() as ctx:
        k = Kit(nc, ctx)
        C = k.sb("context", [P, NT, D])
        WX = k.sb("wx", [P, 4, P])
        XQ = k.sb("xq", [P, NT, D])
        QT = k.sb("qT", [P, NT, 2, P])
        KB = k.sb("kT_blocks", [P, NT, 2, 2, 4, SEQ])
        VB = k.sb("v_blocks", [P, NT, 4, 2, 2, XN])
        EX = k.sb("xprobs", [P, 4, XH, SEQ])
        PT = k.sb("xprobsT", [P, 2, 4, P])
        DF = k.sb("diff", [P, 2, D])
        st = k.sb("xstats", [P, NT, 6])
        mv = k.sb("xmean_var", [P, NT, 2])
        std = k.sb("xstd", [P, NT])
        rstd = k.sb("xrstd", [P, 2, NT])
        tmp = k.sb("xnorm_tmp", [P, 4, NT])
        mx = k.sb("xrow_max", [P, 2, XH])
        sm = k.sb("xrow_sum", [P, 2, XH])
        ri = k.sb("xrow_inv", [P, 4, XH])
        ps_j = [k.bank(f"xps_job{i}") for i in range(2)]
        ps_s = [k.bank(f"xps_scores{i}") for i in range(2)]
        ps_p = [k.bank(f"xps_probsT{i}") for i in range(2)]
        ps_o = k.bank("xps_out")
        ps_y = k.bank("xps_y")

        s_c = [k.sem(f"p3_context{i}") for i in range(2)]
        s_w = k.sem("p3_weights")
        s_zero = k.sem("p3_zero")
        s_stat = k.sem("p3_stat")
        s_var = k.sem("p3_var")
        s_std = k.sem("p3_std")
        s_xq = k.sem("p3_xq")
        s_job = k.sem("p3_job")
        s_ja = k.sem("p3_job_act")
        s_jd = k.sem("p3_job_dve")
        s_scores = k.sem("p3_scores")
        s_max = k.sem("p3_max")
        s_shift = k.sem("p3_shifted")
        s_exp = k.sem("p3_exp")
        s_sum = k.sem("p3_sum")
        s_inv = k.sem("p3_inverse")
        s_norm = k.sem("p3_normalised")
        s_pT = k.sem("p3_probs_transposed")
        s_pTc = k.sem("p3_probsT_copied")
        s_pv = k.sem("p3_values_mixed")
        s_diff = k.sem("p3_diff")
        s_y = k.sem("p3_projected")
        s_res = k.sem("p3_residual")
        block = ctx.enter_context(nc.Block())
        LAG = 5

        @block.sync
        def _(sp):
            sp.dma_start(WX[:], wx_d).then_inc(s_w, 16)
            sp.dma_start(C[:, 0:4, :], ctx_d[:, 0:4, :]).then_inc(s_c[0], 16)
            sp.dma_start(C[:, 4:8, :], ctx_d[:, 4:8, :]).then_inc(s_c[1], 16)

        @block.gpsimd
        def _(pool):
            nc.gpsimd.memset(KB[:], 0.0).then_inc(s_zero, 1)
            nc.gpsimd.memset(VB[:], 0.0).then_inc(s_zero, 1)
            for t in range(NT):
                pool.wait_ge(s_inv, t + 1)
                e = EX[:, t % 4, :, :]
                nc.gpsimd.tensor_tensor(e, e, bc(ri[:, t % 4, :], 2, SEQ), ALU.mult).then_inc(s_norm, 1)

        def spread_keys(copy, j, h4):
            rows = slice(h4 * XN, (h4 + 1) * XN)
            return copy(KB[rows, 2 * j:2 * j + 2, :, :, h4, :].rearrange("p t c b s -> p (t c b) s"),
                        ps_j[j % 2][rows, :].rearrange("p (m s) -> p m s", s=SEQ))

        def spread_values(copy, j, b, h2):
            src = ps_j[j % 2][b * SEQ:(b + 1) * SEQ, :].rearrange("p (m g n) -> p m g n", g=2, n=XN)[:, :, h2, :]
            return copy(VB[h2 * SEQ:(h2 + 1) * SEQ, 2 * j:2 * j + 2, :, b, h2, :].rearrange("p t h n -> p (t h) n"),
                        src)

        @block.scalar
        def _(act):
            act.wait_ge(s_zero, 2)
            for j in range(4):
                act.wait_ge(s_job, j + 1)
                spread_keys(nc.scalar.copy, j, 0)
                spread_keys(nc.scalar.copy, j, 1).then_inc(s_ja, 1)
            act.wait_ge(s_var, 1)
            nc.scalar.activation(std[:], tmp[:, 0, :], ACT.Sqrt).then_inc(s_std, 1)
            for j in range(4):
                act.wait_ge(s_job, 4 + j + 1)
                for h2 in range(2):
                    last = spread_values(nc.scalar.copy, j, 0, h2)
                last.then_inc(s_ja, 1)
            for j in range(4):
                act.wait_ge(s_job, 8 + j + 1)
                nc.scalar.copy(QT[:, 2 * j:2 * j + 2, :, :].rearrange("p t c m -> p (t c m)"),
                               ps_j[j % 2][:]).then_inc(s_ja, 1)
            for k_ in range(NT + LAG):
                if k_ < NT:
                    act.wait_ge(s_shift, k_ + 1)
                    nc.scalar.activation(EX[:, k_ % 4, :, :], EX[:, k_ % 4, :, :], ACT.Exp,
                                         scale=XSCALE).then_inc(s_exp, 1)
                t = k_ - 2
                if 0 <= t < NT:
                    act.wait_ge(s_pT, t + 1)
                    if t >= 2:
                        act.wait_ge(s_pv, t - 1)
                    nc.scalar.copy(PT[:, t % 2, :, :].rearrange("p h m -> p (h m)"), ps_p[t % 2][:]).then_inc(s_pTc, 1)

        def other_keys(dve):
            dve.wait_ge(s_zero, 2)
            for j in range(4):
                dve.wait_ge(s_job, j + 1)
                spread_keys(nc.vector.tensor_copy, j, 2)
                spread_keys(nc.vector.tensor_copy, j, 3).then_inc(s_jd, 1)

        @block.vector
        def _(dve):
            norm_stats(nc, dve, X, st, mv, s_stat)
            norm_rstd(nc, dve, mv, std, rstd, tmp, s_var, s_std, s_stat, NT + 1,
                      between=lambda: other_keys(dve))
            for t in range(NT):
                nc.vector.tensor_scalar(XQ[:, t, :], X[:, t, :], mv[:, t, 0:1], rstd[:, 1, t:t + 1],
                                        ALU.subtract, ALU.mult).then_inc(s_xq, 1)
            for j in range(4):
                dve.wait_ge(s_job, 4 + j + 1)
                for h2 in range(2):
                    last = spread_values(nc.vector.tensor_copy, j, 1, h2)
                last.then_inc(s_jd, 1)
            for k_ in range(NT + LAG):
                if k_ < NT:
                    rows = ps_s[k_ % 2][:].rearrange("p (x s) -> p x s", s=SEQ)
                    dve.wait_ge(s_scores, k_ + 1)
                    nc.vector.tensor_reduce(mx[:, k_ % 2, :], rows, AX.X, ALU.max).then_inc(s_max, 1)
                    dve.wait_ge(s_max, k_ + 1)
                    if k_ >= 4:
                        dve.wait_ge(s_pT, k_ - 3)
                    nc.vector.tensor_tensor(EX[:, k_ % 4, :, :], rows, bc(mx[:, k_ % 2, :], 2, SEQ),
                                            ALU.subtract).then_inc(s_shift, 1)
                t = k_ - 4
                if 0 <= t < NT:
                    dve.wait_ge(s_pv, t + 1)
                    if t >= 2:
                        dve.wait_ge(s_y, t - 1)
                    for b in range(2):
                        rows = slice(b * SEQ, (b + 1) * SEQ)
                        last = nc.vector.tensor_tensor(
                            DF[rows, t % 2, :].rearrange("p (h n) -> p h n", h=4),
                            XQ[rows, t, :].rearrange("p (h n) -> p h n", h=4),
                            ps_o[rows, :].rearrange("p (h b n) -> p h b n", h=4, b=2)[:, :, b, :], ALU.subtract)
                    last.then_inc(s_diff, 1)
                t = k_ - 1
                if 0 <= t < NT:
                    dve.wait_ge(s_exp, t + 1)
                    nc.vector.tensor_reduce(sm[:, t % 2, :], EX[:, t % 4, :, :], AX.X, ALU.add).then_inc(s_sum, 1)
                    dve.wait_ge(s_sum, t + 1)
                    nc.vector.reciprocal(ri[:, t % 4, :], sm[:, t % 2, :]).then_inc(s_inv, 1)
                t = k_ - 5
                if 0 <= t < NT:
                    dve.wait_ge(s_y, t + 1)
                    nc.vector.tensor_tensor(X[:, t, :], ps_y[:, 0:D], X[:, t, :], ALU.add).then_inc(s_res, 1)

        @block.tensor
        def _(pe):
            pe.wait_ge(s_w, 16)
            for n in range(NJOB):
                kind, j = n // 4, n % 4
                out = ps_j[j % 2]
                if n >= 2:
                    pe.wait_ge(s_ja, n - 1)
                    pe.wait_ge(s_jd, min(n - 1, 8))
                if kind < 2:
                    pe.wait_ge(s_c[j // 2], 16)
                if kind == 1:
                    last = nc.tensor.matmul(out[:], WX[:, 2, :], C[:, 2 * j:2 * j + 2, :].rearrange("p t d -> p (t d)"),
                                            start=True, stop=True)
                else:
                    src = C if kind == 0 else XQ
                    for x in range(4):
                        t, c = 2 * j + x // 2, x % 2
                        if kind == 2:
                            pe.wait_ge(s_xq, t + 1)
                        last = nc.tensor.matmul(out[:, x * P:(x + 1) * P], src[:, t, c * P:(c + 1) * P],
                                                WX[:, 1 if kind == 0 else 0, :], start=True, stop=True)
                last.then_inc(s_job, 1)
            for k_ in range(NT + LAG):
                t = k_
                if t < NT:
                    pe.wait_ge(s_ja, 8 + t // 2 + 1)
                    if t >= 2:
                        pe.wait_ge(s_shift, t - 1)
                    for b in range(2):
                        for c in range(2):
                            last = nc.tensor.matmul(ps_s[t % 2][b * SEQ:(b + 1) * SEQ, c * 4 * SEQ:(c + 1) * 4 * SEQ],
                                                    QT[:, t, c, b * SEQ:(b + 1) * SEQ],
                                                    KB[:, t, c, b, :, :].rearrange("p h s -> p (h s)"),
                                                    start=True, stop=True)
                    last.then_inc(s_scores, 1)
                t = k_ - 2
                if 0 <= t < NT:
                    pe.wait_ge(s_norm, t + 1)
                    if t >= 2:
                        pe.wait_ge(s_pTc, t - 1)
                    for hp in range(4):
                        last = nc.tensor.transpose(ps_p[t % 2][:, hp * P:(hp + 1) * P],
                                                   EX[:, t % 4, 2 * hp:2 * hp + 2, :].rearrange("p h s -> p (h s)"),
                                                   ident[:])
                    last.then_inc(s_pT, 1)
                t = k_ - 3
                if 0 <= t < NT:
                    pe.wait_ge(s_pTc, t + 1)
                    if t >= 1:
                        pe.wait_ge(s_diff, t)
                    for hp in range(4):
                        last = nc.tensor.matmul(ps_o[:, hp * P:(hp + 1) * P], PT[:, t % 2, hp, :],
                                                VB[:, t, hp, :, :, :].rearrange("p b h n -> p (b h n)"),
                                                start=True, stop=True)
                    last.then_inc(s_pv, 1)
                t = k_ - 4
                if 0 <= t < NT:
                    pe.wait_ge(s_diff, t + 1)
                    if t >= 1:
                        pe.wait_ge(s_res, t)
                    nc.tensor.matmul(ps_y[:, 0:D], WX[:, 3, :], DF[:, t % 2, :], start=True, stop=True).then_inc(s_y, 1)


def expert_phase(nc, X, ident, d, out_d):
    LAG = 2
    UP = 2 * D
    with ExitStack() as ctx:
        k = Kit(nc, ctx)
        raw13 = [k.sb(f"raw13_{i}", [P, UP]) for i in range(2)]
        raw2 = [k.sb(f"raw2_{i}", [P, D]) for i in range(2)]
        w13 = [[k.sb(f"w13_{n}{i}", [P, UP], F32R) for n in ("hi", "lo")] for i in range(2)]
        w2 = [[k.sb(f"w2_{n}{i}", [P, D], F32R) for n in ("hi", "lo")] for i in range(2)]
        xnT = [k.sb(f"f_xnT_{n}", [P, KC, T], F32R) for n in ("hi", "lo")]
        xn = k.sb("f_xn", [P, NT, D])
        gate = k.sb("gate", [P, KC, E])
        gw = [k.sb(f"gate_{n}", [P, KC, E], F32R) for n in ("hi", "lo")]
        bias = k.sb("bias", [P, E])
        lower = k.sb("lower", [P, E, E])
        sg = k.sb("silu", [P, 2, HALF])
        hu = k.sb("gated", [P, 2, HALF])
        hw = k.sb("weighted", [P, 2, HALF])
        H = [[k.sb(f"h_{n}{i}", [P, HALF], F32R) for n in ("hi", "lo")] for i in range(2)]
        CW = k.sb("cw_rows", [P, 2, T])
        cwr = k.sb("cw_repeated", [P, NT, 2, EG, UNIT])
        yT = k.sb("yT", [P, KC, T])
        st = k.sb("fstats", [P, NT, 6])
        mv = k.sb("fmean_var", [P, NT, 2])
        std = k.sb("fstd", [P, NT])
        rstd = k.sb("frstd", [P, 2, NT])
        tmp = k.sb("fnorm_tmp", [P, 4, NT])
        ex = k.sb("g_exp", [P, NT, E])
        den = k.sb("g_den", [P, NT, E])
        sc = k.sb("g_scores", [P, NT, E])
        biased = k.sb("g_biased", [P, NT, E])
        gm = k.sb("g_group_max", [P, NT, GE])
        gbeat = k.sb("g_gbeat", [P, 3, NT, GE, GE])
        gcnt = k.sb("g_gcount", [P, NT, GE])
        gsel = k.sb("g_group_sel", [P, NT, GE])
        goff = k.sb("g_group_off", [P, NT, GE])
        kept = k.sb("g_kept", [P, NT, E])
        msk = k.sb("g_masked", [P, NT, E])
        beat = k.sb("g_beat", [P, NT, E, E])
        tie = k.sb("g_tie", [P, NT, E, E])
        cnt = k.sb("g_count", [P, NT, E])
        sel = k.sb("g_selected", [P, NT, E])
        picked = k.sb("g_picked", [P, NT, E])
        wsum = k.sb("g_sum", [P, 2, NT])
        cw = k.sb("g_weight", [P, NT, E])
        acc = [[k.bank(f"acc{dc}{h}") for h in range(NHALF)] for dc in range(KC)]
        up = [[k.bank(f"up{n}{i}") for n in range(2)] for i in range(2)]

        s_gate = k.sem("p4_gate")
        s_bias = k.sem("p4_bias")
        s_r13 = [k.sem(f"p4_raw13_{i}") for i in range(2)]
        s_r2 = [k.sem(f"p4_raw2_{i}") for i in range(2)]
        s_stat = k.sem("p4_stat")
        s_var = k.sem("p4_var")
        s_std = k.sem("p4_std")
        s_xn = k.sem("p4_xn")
        s_tr = k.sem("p4_transposed")
        s_xhi = k.sem("p4_xnT_hi")
        s_xlo = k.sem("p4_xnT_lo")
        s_ghi = k.sem("p4_gate_hi")
        s_glo = k.sem("p4_gate_lo")
        s_log = k.sem("p4_logits")
        s_gexp = k.sem("p4_gate_exp")
        s_g = k.sem("p4_gating")
        s_masked = k.sem("p4_masked")
        s_equal = k.sem("p4_equal")
        s_tie = k.sem("p4_ties")
        s_cwr = k.sem("p4_cw_repeated")
        s_cwt = k.sem("p4_cw_transposed")
        s_cw = k.sem("p4_cw_rows")
        s_13hi = k.sem("p4_w13_hi")
        s_13lo = k.sem("p4_w13_lo")
        s_2hi = k.sem("p4_w2_hi")
        s_2lo = k.sem("p4_w2_lo")
        s_up = k.sem("p4_up")
        s_silu = k.sem("p4_silu")
        s_gated = k.sem("p4_gated")
        s_wtd = k.sem("p4_weighted")
        s_hhi = k.sem("p4_h_hi")
        s_hlo = k.sem("p4_h_lo")
        s_down = k.sem("p4_down")
        s_yT = k.sem("p4_yT")
        s_yt = k.sem("p4_y_transposed")
        s_y = k.sem("p4_y")
        s_out = k.sem("p4_out")
        block = ctx.enter_context(nc.Block())

        N0 = 2 * NSC

        def run_units(eng, step, lag):
            for n in range(N0 + 4):
                step((n - N0) // 4, (n - N0) % 4)
            with eng.Fori(1, NU - 1) as u:
                for r in range(4):
                    step(u, r)
            for r in range(4 + lag):
                step(NU - 1, r)

        def live(u, q):
            return not isinstance(u, int) or 0 <= 4 * u + N0 + q < 2 * NC

        def after(u, q, n):
            return not isinstance(u, int) or 4 * u + N0 + q >= n

        def shared(u, q):
            return isinstance(u, int) and 4 * u + q < 0

        def place(q):
            return (NSC + q // 2) % 2

        @block.sync
        def _(sp):
            sp.dma_start(gate[:], d["gate"]).then_inc(s_gate, 16)

            def load13(u, q):
                c, i = 2 * u + NSC + q // 2, place(q)
                if after(u, q, 4):
                    sp.wait_ge(s_13lo, c - 1)
                sp.dma_start(raw13[i][:], d["wch"][bass.ds(c, 1), :, 0:UP].rearrange("o p n -> (o p) n")
                             ).then_inc(s_r13[i], 16)

            def load2(u, q):
                c, i = 2 * u + NSC + q // 2, place(q)
                if after(u, q, 4):
                    sp.wait_ge(s_2lo, c - 1)
                sp.dma_start(raw2[i][:], d["wch"][bass.ds(c, 1), :, UP:UP + D].rearrange("o p n -> (o p) n")
                             ).then_inc(s_r2[i], 16)

            load13(-2, 2)
            load13(-1, 0)
            load2(-2, 2)
            sp.dma_start(bias[:], d["bias"].partition_broadcast(P)).then_inc(s_bias, 16)
            sp.dma_start(lower[:], d["lower"].partition_broadcast(P)).then_inc(s_bias, 16)

            def step(u, r):
                if r % 2 == 0:
                    if live(u, r + 4):
                        load13(u, r + 4)
                    if live(u, r + 2):
                        load2(u, r + 2)

            run_units(sp, step, 0)
            for q in range(2):
                sp.wait_ge(s_y, 4 * (q + 1))
                sp.dma_start(out_d[:, 4 * q:4 * q + 4, :], xn[:, 4 * q:4 * q + 4, :]).then_inc(s_out, 16)
            sp.wait_ge(s_out, 32)

        @block.gpsimd
        def _(pool):
            def low13(u, q):
                c, i = 2 * u + NSC + q // 2, place(q)
                pool.wait_ge(s_13hi, c + 1)
                nc.gpsimd.tensor_tensor(w13[i][1][:], raw13[i][:], as_f32(w13[i][0][:]), ALU.subtract).then_inc(s_13lo, 1)

            def low2(u, q):
                c, i = 2 * u + NSC + q // 2, place(q)
                pool.wait_ge(s_2hi, c + 1)
                nc.gpsimd.tensor_tensor(w2[i][1][:], raw2[i][:], as_f32(w2[i][0][:]), ALU.subtract).then_inc(s_2lo, 1)

            low13(-2, 2)

            def step(u, r):
                if r % 2 == 0:
                    if live(u, r + 2):
                        low13(u, r + 2)
                    if live(u, r):
                        low2(u, r)
                if isinstance(u, int) and 4 * u + r == -2:
                    pool.wait_ge(s_equal, 1)
                    nc.gpsimd.tensor_tensor(tie[:], tie[:], bc(lower[:], 1, NT), ALU.mult).then_inc(s_tie, 1)
                if live(u, r) and not shared(u, r):
                    if isinstance(u, int) and u == 0 and r == 0:
                        pool.wait_ge(s_cw, 4)
                    pool.wait_ge(s_gated, 4 * u + N0 + r + 1)
                    if not isinstance(u, int) or 4 * u + r >= 2:
                        pool.wait_ge(s_hlo, 4 * u + N0 + r - 1)
                    h = r % 2
                    nc.gpsimd.tensor_tensor(hw[:, h, :], hu[:, h, :], CW[:, r // 2, h * HALF:(h + 1) * HALF],
                                            ALU.mult).then_inc(s_wtd, 1)

            run_units(pool, step, 0)

        @block.scalar
        def _(act):
            def high13(u, q):
                c, i = 2 * u + NSC + q // 2, place(q)
                act.wait_ge(s_r13[i], 16 * (u + (NSC + q // 2) // 2 + 1))
                if after(u, q, 4):
                    act.wait_ge(s_up, 2 * c - 2)
                nc.scalar.copy(w13[i][0][:], raw13[i][:]).then_inc(s_13hi, 1)

            def high2(u, q):
                c, i = 2 * u + NSC + q // 2, place(q)
                act.wait_ge(s_r2[i], 16 * (u + (NSC + q // 2) // 2 + 1))
                if after(u, q, 4):
                    act.wait_ge(s_down, 2 * c - 2)
                nc.scalar.copy(w2[i][0][:], raw2[i][:]).then_inc(s_2hi, 1)

            act.wait_ge(s_gate, 16)
            nc.scalar.copy(gw[0][:], gate[:]).then_inc(s_ghi, 1)
            high13(-2, 2)
            act.wait_ge(s_var, 1)
            nc.scalar.activation(std[:], tmp[:, 0, :], ACT.Sqrt).then_inc(s_std, 1)
            for n in range(KC * NHALF):
                kc, h = n % KC, n // KC
                act.wait_ge(s_tr, n + 1)
                nc.scalar.copy(xnT[0][:, kc, h * HALF:(h + 1) * HALF], up[h][kc][:]).then_inc(s_xhi, 1)
            act.wait_ge(s_log, 1)
            nc.scalar.activation(ex[:].rearrange("p t e -> p (t e)"), acc[0][0][:, 0:NT * E], ACT.Exp,
                                 scale=-1.0).then_inc(s_gexp, 1)

            def step(u, r):
                if r % 2 == 0:
                    if live(u, r):
                        high2(u, r)
                    if live(u, r + 2):
                        high13(u, r + 2)
                if isinstance(u, int) and u == 0 and r == 0:
                    for n in range(4):
                        h, g = n // 2, n % 2
                        act.wait_ge(s_cwt, n + 1)
                        nc.scalar.copy(CW[:, g, h * HALF:(h + 1) * HALF], up[h][g][:]).then_inc(s_cw, 1)
                if live(u, r):
                    act.wait_ge(s_up, 4 * u + N0 + r + 1)
                    if after(u, r, 2):
                        act.wait_ge(s_gated, 4 * u + N0 + r - 1)
                    nc.scalar.activation(sg[:, r % 2, :], up[r % 2][0][:], ACT.Silu).then_inc(s_silu, 1)
                q = r - 1
                if live(u, q):
                    if shared(u, q):
                        act.wait_ge(s_gated, 4 * u + N0 + q + 1)
                    else:
                        act.wait_ge(s_wtd, 4 * u + q + 1)
                    if after(u, q, 2):
                        act.wait_ge(s_down, 4 * u + N0 + q - 1)
                    src = hu if shared(u, q) else hw
                    nc.scalar.copy(H[q % 2][0][:], src[:, q % 2, :]).then_inc(s_hhi, 1)

            run_units(act, step, 1)
            for n in range(4):
                dc, h = n % 2, n // 2
                act.wait_ge(s_down, 2 * NC - 1 + h)
                nc.scalar.copy(yT[:, dc, h * HALF:(h + 1) * HALF], acc[dc][h][:]).then_inc(s_yT, 1)

        @block.vector
        def _(dve):
            done = [0]

            def then(ins):
                ins.then_inc(s_g, 1)
                done[0] += 1
                dve.wait_ge(s_g, done[0])

            dve.wait_ge(s_ghi, 1)
            nc.vector.tensor_tensor(gw[1][:], gate[:], as_f32(gw[0][:]), ALU.subtract).then_inc(s_glo, 1)
            norm_stats(nc, dve, X, st, mv, s_stat)
            norm_rstd(nc, dve, mv, std, rstd, tmp, s_var, s_std, s_stat, NT + 1)
            for t in range(NT):
                nc.vector.tensor_scalar(xn[:, t, :], X[:, t, :], mv[:, t, 0:1], rstd[:, 1, t:t + 1],
                                        ALU.subtract, ALU.mult).then_inc(s_xn, 1)
            for n in range(KC * NHALF):
                kc, h = n % KC, n // KC
                tok = slice(h * HALF, (h + 1) * HALF)
                dve.wait_ge(s_xhi, n + 1)
                nc.vector.tensor_tensor(xnT[1][:, kc, tok], up[h][kc][:], as_f32(xnT[0][:, kc, tok]),
                                        ALU.subtract).then_inc(s_xlo, 1)

            def choose_groups():
                dve.wait_ge(s_bias, 32)
                dve.wait_ge(s_gexp, 1)
                then(nc.vector.tensor_scalar(den[:], ex[:], 1.0, None, ALU.add))
                then(nc.vector.reciprocal(sc[:], den[:]))
                then(nc.vector.tensor_tensor(biased[:], sc[:], bc(bias[:], 1, NT), ALU.add))
                grouped = biased[:].rearrange("p t (g e) -> p t g e", g=GE)
                then(nc.vector.tensor_reduce(gm[:], grouped, AX.X, ALU.max))
                other, own = bc(gm[:], 2, GE), bc(gm[:], 3, GE)
                nc.vector.tensor_tensor(gbeat[:, 0], other, own, ALU.is_gt)
                then(nc.vector.tensor_tensor(gbeat[:, 1], other, own, ALU.is_equal))
                then(nc.vector.tensor_tensor(gbeat[:, 2], gbeat[:, 1], bc(lower[:, 0:GE, 0:GE], 1, NT), ALU.mult))
                then(nc.vector.tensor_tensor(gbeat[:, 1], gbeat[:, 0], gbeat[:, 2], ALU.add))
                then(nc.vector.tensor_reduce(gcnt[:], gbeat[:, 1], AX.X, ALU.add))
                then(nc.vector.tensor_scalar(gsel[:], gcnt[:], TOPG - 0.5, None, ALU.is_lt))
                nc.vector.tensor_scalar(goff[:], gsel[:], 1.0, -MASKED, ALU.subtract, ALU.mult)
                then(nc.vector.tensor_tensor(kept[:].rearrange("p t (g e) -> p t g e", g=GE), grouped,
                                             bc(gsel[:], 3, E // GE), ALU.mult))
                nc.vector.tensor_tensor(msk[:].rearrange("p t (g e) -> p t g e", g=GE),
                                        kept[:].rearrange("p t (g e) -> p t g e", g=GE),
                                        bc(goff[:], 3, E // GE), ALU.add).then_inc(s_masked, 1)

            def rank_experts():
                dve.wait_ge(s_masked, 1)
                other, own = bc(msk[:], 2, E), bc(msk[:], 3, E)
                nc.vector.tensor_tensor(tie[:], other, own, ALU.is_equal).then_inc(s_equal, 1)

            def rank_experts_2():
                other, own = bc(msk[:], 2, E), bc(msk[:], 3, E)
                then(nc.vector.tensor_tensor(beat[:], other, own, ALU.is_gt))

            def add_ties():
                dve.wait_ge(s_tie, 1)
                then(nc.vector.tensor_tensor(beat[:], beat[:], tie[:], ALU.add))

            def weights():
                then(nc.vector.tensor_reduce(cnt[:], beat[:], AX.X, ALU.add))
                then(nc.vector.tensor_scalar(sel[:], cnt[:], TOPK - 0.5, None, ALU.is_lt))
                then(nc.vector.tensor_tensor(picked[:], sc[:], sel[:], ALU.mult))
                then(nc.vector.tensor_reduce(wsum[:, 0, :], picked[:], AX.X, ALU.add))
                then(nc.vector.reciprocal(wsum[:, 1, :], wsum[:, 0, :]))
                then(nc.vector.tensor_tensor(cw[:], picked[:], bc(wsum[:, 1, :], 2, E), ALU.mult))
                nc.vector.tensor_copy(cwr[:].rearrange("p t g e i -> p (t g e) i"),
                                      bc(cw[:].rearrange("p t e -> p (t e)"), 2, UNIT)).then_inc(s_cwr, 1)

            routing = {-6: choose_groups, -5: rank_experts, -4: rank_experts_2, -2: add_ties, -1: weights}

            def step(u, r):
                if live(u, r):
                    dve.wait_ge(s_silu, 4 * u + N0 + r + 1)
                    if shared(u, r):
                        if after(u, r, 2):
                            dve.wait_ge(s_hlo, 4 * u + N0 + r - 1)
                    elif not isinstance(u, int) or 4 * u + r >= 2:
                        dve.wait_ge(s_wtd, 4 * u + r - 1)
                    else:
                        dve.wait_ge(s_hlo, 4 * u + N0 + r - 1)
                    nc.vector.tensor_tensor(hu[:, r % 2, :], up[r % 2][1][:], sg[:, r % 2, :],
                                            ALU.mult).then_inc(s_gated, 1)
                q = r - 1
                if live(u, q):
                    dve.wait_ge(s_hhi, 4 * u + N0 + q + 1)
                    src = hu if shared(u, q) else hw
                    nc.vector.tensor_tensor(H[q % 2][1][:], src[:, q % 2, :], as_f32(H[q % 2][0][:]),
                                            ALU.subtract).then_inc(s_hlo, 1)
                if isinstance(u, int) and 4 * u + r in routing:
                    routing[4 * u + r]()

            run_units(dve, step, 1)
            for t in range(NT):
                dve.wait_ge(s_yt, t + 1)
                nc.vector.tensor_tensor(xn[:, t, :], up[(t // 2) % 2][t % 2][:, 0:D], X[:, t, :], ALU.add).then_inc(s_y, 1)

        @block.tensor
        def _(pe):
            for h in range(NHALF):
                for kc in range(KC):
                    for q in range(4):
                        t = 4 * h + q
                        pe.wait_ge(s_xn, t + 1)
                        last = nc.tensor.transpose(up[h][kc][:, q * P:(q + 1) * P], xn[:, t, kc * P:(kc + 1) * P],
                                                   ident[:])
                    last.then_inc(s_tr, 1)
            pe.wait_ge(s_glo, 1)
            pe.wait_ge(s_xlo, 4)
            for t in range(NT):
                for kc in range(KC):
                    last = split3(nc.tensor, acc[0][0][:, t * E:(t + 1) * E], xnT, gw,
                                  (slice(None), kc, slice(t * P, (t + 1) * P)), (slice(None), kc), kc == 0, kc == KC - 1)
            last.then_inc(s_log, 1)

            def step(u, r):
                if isinstance(u, int) and u == 0 and r == 0:
                    pe.wait_ge(s_cwr, 1)
                    pe.wait_ge(s_gated, N0)
                    for n in range(4):
                        h, g = n // 2, n % 2
                        for x in range(4):
                            last = nc.tensor.transpose(up[h][g][:, x * P:(x + 1) * P],
                                                       cwr[:, 4 * h + x, g, :, :].rearrange("p e i -> p (e i)"), ident[:])
                        last.then_inc(s_cwt, 1)
                    pe.wait_ge(s_cw, 4)
                if live(u, r):
                    w = [x[:].rearrange("p (a k m) -> p a k m", a=2, k=KC) for x in w13[place(r)]]
                    c, h = 2 * u + NSC + r // 2, r % 2
                    if h == 0:
                        pe.wait_ge(s_13lo, c + 1)
                    if after(u, r, 2):
                        pe.wait_ge(s_gated, 4 * u + N0 + r - 1)
                    for m in range(2):
                        for kc in range(KC):
                            last = split3(nc.tensor, up[r % 2][m][:], w, xnT, (slice(None), m, kc),
                                          (slice(None), kc, slice(h * HALF, (h + 1) * HALF)), kc == 0, kc == KC - 1)
                    last.then_inc(s_up, 1)
                q = r - LAG
                if live(u, q):
                    c, h = 2 * u + NSC + q // 2, q % 2
                    if h == 0:
                        pe.wait_ge(s_2lo, c + 1)
                        if isinstance(u, int) and 4 * u + q == -N0:
                            pe.wait_ge(s_gexp, 1)
                    pe.wait_ge(s_hlo, 4 * u + N0 + q + 1)
                    first = isinstance(u, int) and 4 * u + N0 + q < 2
                    end = isinstance(u, int) and 4 * u + N0 + q >= 2 * NC - 2
                    for dc in range(KC):
                        last = split3(nc.tensor, acc[dc][h][:], w2[place(q)], H[q % 2],
                                      (slice(None), slice(dc * P, (dc + 1) * P)), (slice(None),), first, end)
                    last.then_inc(s_down, 1)

            run_units(pe, step, LAG)
            for t in range(NT):
                pe.wait_ge(s_yT, 2 * (t // 4) + 2)
                if t >= 4:
                    pe.wait_ge(s_y, t - 3)
                for dc in range(KC):
                    last = nc.tensor.transpose(up[(t // 2) % 2][t % 2][:, dc * P:(dc + 1) * P],
                                               yT[:, dc, t * P:(t + 1) * P], ident[:])
                last.then_inc(s_yt, 1)


def decoder_layer(nc, d, out):
    with ExitStack() as ctx:
        k = Kit(nc, ctx)
        X = k.sb("x", [P, NT, D])
        ident = k.sb("ident", [P, P])
        x_d = d["x"].rearrange("(t p) c -> p t c", p=P)
        out_d = out.rearrange("(t p) c -> p t c", p=P)
        with ExitStack() as c1:
            k1 = Kit(nc, c1)
            QR = k1.sb("q_rotated", [P, 2, NT, 2 * 2 * G * SEQ])
            KR = k1.sb("k_rotated", [P, 2, NT, 2, P])
            V = k1.sb("v", [P, NT, HKV * HD])
            WO = [k1.sb(f"wo_{n}", [P, 16, D], F32R) for n in ("hi", "lo")]
            qkv_phase(nc, X, QR, KR, V, WO, ident, x_d, d["wqk"], d["wv"], d["wo"], d["cos_sin"], d["ident"])
            attention_phase(nc, X, QR, KR, V, WO, ident, d["mask"])
        cross_phase(nc, X, ident, d["ctx"].rearrange("(t p) c -> p t c", p=P), d["wx"])
        expert_phase(nc, X, ident, d, out_d)



def layout(x, ctx_2048, L0_attn_Wq, L0_attn_Wk, L0_attn_Wv, L0_attn_Wo, L0_xattn_W_q, L0_xattn_W_k,
           L0_xattn_W_v, L0_xattn_W_o, L0_ffn_gate_w, L0_ffn_expert_bias, L0_ffn_w1, L0_ffn_w2, L0_ffn_w3,
           L0_ffn_sw1, L0_ffn_sw2, L0_ffn_sw3):
    a = np.ascontiguousarray
    f4 = np.float32

    def pairs(w, heads):
        w = np.asarray(w).reshape(2, 4, heads, F, 2, KC, P)
        return w.transpose(0, 2, 6, 5, 4, 1, 3).reshape(2 * heads, P, KC * 2 * P)

    wqk = np.concatenate([pairs(L0_attn_Wq, G), pairs(L0_attn_Wk, 1)], 0)
    wv = np.asarray(L0_attn_Wv).reshape(HKV * HD, KC, P).transpose(2, 1, 0)
    wo = np.asarray(L0_attn_Wo).reshape(D, 2, 2, 2, G, HD).transpose(3, 5, 2, 1, 4, 0)
    wo = wo.reshape(P, 8, 2 * D).transpose(1, 0, 2)
    inv = (f4(1.0) / f4(10000.0) ** (np.arange(0, HD, 2, dtype=f4) / f4(HD))).astype(f4)
    ang = (np.arange(SEQ, dtype=f4)[None, :] * inv[:, None]).astype(f4)
    cs = np.stack([np.cos(ang), np.sin(ang)], 1).astype(f4)
    cs = np.tile(cs, (4, 1, 1))
    q, kk = np.arange(P)[:, None] % SEQ, np.arange(P)[None, :] % SEQ
    mask = np.where(q >= kk, 0.0, MASKED).astype(f4)
    wx = np.zeros((P, 4, P), f4)
    for n, w in enumerate((L0_xattn_W_q, L0_xattn_W_k, L0_xattn_W_v, L0_xattn_W_o)):
        for b in range(2):
            wx[b * SEQ:(b + 1) * SEQ, n, b * SEQ:(b + 1) * SEQ] = np.asarray(w).T
    def up_chunks(shared, routed):
        sh = np.zeros((D, NSC * P), f4)
        sh[:, 0:SH] = np.asarray(shared)
        sh = sh.reshape(KC, P, NSC, P).transpose(2, 1, 0, 3)
        ro = np.asarray(routed).reshape(2, EG, KC, P, NU, UNIT).transpose(4, 0, 3, 2, 1, 5)
        return np.concatenate([sh, ro.reshape(NEC, P, KC, P)], 0)

    sh2 = np.zeros((NSC * P, D), f4)
    sh2[0:SH] = np.asarray(L0_ffn_sw2)
    ro2 = np.asarray(L0_ffn_w2).reshape(2, EG, NU, UNIT, D).transpose(2, 0, 1, 3, 4).reshape(NEC, P, D)
    w2 = np.concatenate([sh2.reshape(NSC, P, D), ro2], 0)
    w13 = np.stack([up_chunks(L0_ffn_sw1, L0_ffn_w1), up_chunks(L0_ffn_sw3, L0_ffn_w3)], 2)
    wch = np.concatenate([w13.reshape(NC, P, 2 * D), w2], 2)
    gate = np.asarray(L0_ffn_gate_w).reshape(E, KC, P).transpose(2, 1, 0)
    lower = (np.arange(E)[None, :] < np.arange(E)[:, None]).astype(f4)
    return {
        "wch": a(wch), "gate": a(gate), "bias": a(np.asarray(L0_ffn_expert_bias)), "lower": lower,
        "ctx": a(np.asarray(ctx_2048).reshape(T, D)), "wx": wx,
        "x": a(np.asarray(x).reshape(T, D)), "wqk": a(wqk), "wv": a(wv), "wo": a(wo),
        "cos_sin": a(cs), "mask": a(mask), "ident": np.eye(P, dtype=f4),
    }


def kernel(**inputs):
    import concourse.bacc as _bacc
    from concourse.bass_utils import run_bass_kernel_spmd as _run

    nc = _bacc.Bacc("TRN2", target_bir_lowering=False, num_devices=1)
    arrays = {f"in_{n}": v for n, v in layout(**inputs).items()}
    d = {n[3:]: nc.dram_tensor(n, v.shape, mybir.dt.from_np(v.dtype), kind="ExternalInput").ap()
         for n, v in arrays.items()}
    out = nc.dram_tensor("out", (T, D), F32, kind="ExternalOutput").ap()
    decoder_layer(nc, d, out)
    r = _run(nc, [arrays], core_ids=[0])
    return r.results[0]["out"].reshape(B, SEQ, D)
```

```python
from contextlib import ExitStack

import numpy as np

import concourse.bass as bass
from concourse import mybir

F32 = mybir.dt.float32
F32R = mybir.dt.float32r
BF16 = mybir.dt.bfloat16
ALU = mybir.AluOpType
ACT = mybir.ActivationFunctionType
AX = mybir.AxisListType

P = 128
B, SEQ, D = 16, 64, 256
T = B * SEQ
NT = T // P
KC = D // P
HALF = 512
NHALF = T // HALF
EPS = 1e-5

HQ, HKV, HD = 32, 8, 64
G = HQ // HKV
F = HD // 2
SCALE = float(HD) ** -0.5
NPAIR = 2 * G + 2
MASKED = -1e30

XH = 8
XN = D // XH
XSCALE = float(XN) ** -0.5

E = 16
INTER = 176
GE = 4
TOPK, TOPG = 4, 2
EG = 8
UNIT = P // EG
NU = INTER // UNIT
NEC = (E // EG) * NU
SH = 2 * INTER
NSC = (SH + P - 1) // P
NC = NEC + NSC


def as_f32(ap):
    return ap.bitcast(F32)


def bc(ap, axis, n):
    a = ap.unsqueeze(axis)
    shape = list(a.shape)
    shape[axis] = n
    return a.broadcast_to(shape)


class Steps:

    def __init__(self, total, lag, head):
        self.total, self.lag, self.head = total, lag, head

    def run(self, eng, step):
        for k in range(8 * self.head):
            step(k // 8, k % 8)
        with eng.Fori(self.head, self.total // 8) as i:
            for r in range(8):
                step(i, r)
        for k in range(self.total, self.total + self.lag):
            step(k // 8, k % 8)

    def live(self, i, q):
        return not isinstance(i, int) or 0 <= 8 * i + q < self.total

    def later(self, i, q, n):
        return not isinstance(i, int) or 8 * i + q >= n


class Kit:

    def __init__(self, nc, ctx):
        self.nc, self.ctx = nc, ctx

    def sb(self, name, shape, dt=F32):
        return self.ctx.enter_context(self.nc.sbuf_tensor(name, shape, dt))

    def bank(self, name, n=1):
        shape = [P, HALF] if n == 1 else [P, n, HALF]
        return self.ctx.enter_context(self.nc.psum_tensor(name, shape, F32))

    def sem(self, name):
        return self.ctx.enter_context(self.nc.semaphore(name))


def split3(pe, out, w, x, w_sl, x_sl, first, last):
    pe.matmul(out, w[0][w_sl], x[0][x_sl], start=first, stop=False)
    pe.matmul(out, w[0][w_sl], x[1][x_sl], start=False, stop=False)
    return pe.matmul(out, w[1][w_sl], x[0][x_sl], start=False, stop=last)


class Common:

    def __init__(self, k):
        self.WO = [k.sb(f"wo_{n}", [P, 16, D], F32R) for n in ("hi", "lo")]
        flat = [x[:].rearrange("p c n -> p (c n)") for x in self.WO]
        a, b = KC * T, KC * T + 2 * D
        self.xnT = [x[:, 0:a].rearrange("p (k t) -> p k t", k=KC) for x in flat]
        self.w13 = [x[:, a:b] for x in flat]
        self.gw = [x[:, b:b + KC * E].rearrange("p (k e) -> p k e", k=KC) for x in flat]
        self.mhalf = k.sb("minus_half", [P, NT // 2])
        self.st = k.sb("f_stats", [P, NT, 6])
        self.mv = k.sb("f_mean_var", [P, NT, 2])
        self.tmp = k.sb("f_norm_tmp", [P, 6, NT])
        self.s_var = k.sem("f_var")
        self.s_pow = k.sem("f_pow")
        self.s_r13 = k.sem("f_raw13_0")
        self.s_13hi = k.sem("f_w13_hi")
        self.s_13lo = k.sem("f_w13_lo")


class Chain:

    def __init__(self, eng, sem):
        self.eng, self.sem, self.n = eng, sem, 0

    def then(self, ins):
        ins.then_inc(self.sem, 1)
        self.n += 1
        self.eng.wait_ge(self.sem, self.n)


def norm_stats(nc, chain, X, h, st, mv, tmp, s_var, s_x=None, have=0):
    tiles = range(h * NT // 2, (h + 1) * NT // 2)
    for t in range(max(have, tiles.start), tiles.stop):
        if s_x and t % 2 == 0:
            chain.eng.wait_ge(s_x[t // 2], 16)
        last = nc.vector.bn_stats(st[:, t, :], X[:, t, :])
    chain.then(last)
    for t in tiles:
        last = nc.vector.bn_aggr(mv[:, t, :], st[:, t, :])
    chain.then(last)
    nc.vector.tensor_scalar(tmp[:, 0, tiles.start:tiles.stop], mv[:, tiles.start:tiles.stop, 1], EPS, None,
                            ALU.add).then_inc(s_var, 1)


def norm_power(nc, pool, h, mhalf, tmp, s_var, s_pow):
    half = slice(h * NT // 2, (h + 1) * NT // 2)
    pool.wait_ge(s_var, h + 1)
    nc.gpsimd.tensor_tensor(tmp[:, 1, half], tmp[:, 0, half], mhalf[:], ALU.pow).then_inc(s_pow, 1)


def norm_apply(nc, chain, X, xn, h, mv, tmp, s_pow, s_xn):
    half = slice(h * NT // 2, (h + 1) * NT // 2)
    v, r, a, b, c, rstd = (tmp[:, n, half] for n in range(6))
    chain.eng.wait_ge(s_pow, h + 1)
    chain.then(nc.vector.tensor_tensor(a, r, r, ALU.mult))
    chain.then(nc.vector.tensor_tensor(b, a, v, ALU.mult))
    chain.then(nc.vector.tensor_scalar(c, b, -0.5, 1.5, ALU.mult, ALU.add))
    chain.then(nc.vector.tensor_tensor(rstd, r, c, ALU.mult))
    for t in range(half.start, half.stop):
        nc.vector.tensor_scalar(xn[:, t, :], X[:, t, :], mv[:, t, 0:1], tmp[:, 5, t:t + 1],
                                ALU.subtract, ALU.mult).then_inc(s_xn, 1)


N_Q, N_K, N_V = 8, 8, 4


def stage_q(sp, QR, Q, t, sem):
    for gl in range(2):
        for a in range(2):
            for g2 in range(2):
                src = slice((2 * gl + g2) * F, (2 * gl + g2 + 1) * F)
                dst = slice(g2 * HD + a * F, g2 * HD + (a + 1) * F)
                sp.dma_start(Q[dst, gl, :], QR[src, a, bass.ds(t, 1), :].rearrange("p o n -> p (o n)")
                             ).then_inc(sem, 16)


def stage_k(sp, KR, KB, t, sem):
    for gl in range(2):
        for a in range(2):
            for g2 in range(2):
                src = slice((2 * gl + g2) * F, (2 * gl + g2 + 1) * F)
                dst = slice(g2 * HD + a * F, g2 * HD + (a + 1) * F)
                sp.dma_start(
                    KB[dst, gl, :, :, g2 * HD:(g2 + 1) * HD].rearrange("p s b t -> p (s b) t"),
                    KR[src, a, bass.ds(t, 1), :, :].rearrange("p o s (b t) -> p (o s b) t", b=2),
                ).then_inc(sem, 16)


def stage_v(sp, V, VB, t, sem):
    for b in range(2):
        for g2 in range(2):
            sp.dma_start(
                VB[g2 * HD:(g2 + 1) * HD, b, :, g2 * HD:(g2 + 1) * HD],
                V[b * SEQ:(b + 1) * SEQ, bass.ds(t, 1), :].rearrange(
                    "p o (gp g d) -> p (o gp) g d", gp=4, g=2)[:, :, g2, :],
            ).then_inc(sem, 16)


def qkv_phase(nc, com, X, QR, KR, V, ident, staged, s_qk, s_vb, mask, ident_b, x_d, wqk_d, wv_d, wo_d, cs_d, ident_d, mask_d):
    NW = NPAIR + KC
    NWO = 16 * D // HALF
    WO_LOADS = 2
    assert NWO == NT and HKV * HD == HALF
    with ExitStack() as ctx:
        k = Kit(nc, ctx)
        raw = [k.sb(f"w_raw{i}", [P, HALF]) for i in range(2)]
        w = [[k.sb(f"w_{n}{i}", [P, HALF], F32R) for n in ("hi", "lo")] for i in range(2)]
        xnT = [k.sb(f"xnT_{n}", [P, KC, T], F32R) for n in ("hi", "lo")]
        WO, mhalf = com.WO, com.mhalf
        Q, KV, KB, VB = staged
        prod = [x[:].rearrange("p (n m) -> p n m", n=4) for x in (Q[1], KV[1])]
        xn = Q[1][:].rearrange("p (t d) -> p t d", t=NT)
        cs = k.sb("cos_sin", [P, 2, SEQ])
        mask_f = k.sb("mask_f", [P, P])
        st = k.sb("stats", [P, NT, 6])
        mv = k.sb("mean_var", [P, NT, 2])
        tmp = k.sb("norm_tmp", [P, 6, NT])
        ps_t = k.bank("ps_transposed", 4)
        ps_v = [k.bank(f"ps_v{i}") for i in range(2)]
        proj = [ps_t[:, 2 * i:2 * i + 2, :] for i in range(2)]

        s_x = [k.sem(f"p1_x{i}") for i in range(4)]
        s_const = k.sem("p1_const")
        s_raw = [k.sem(f"p1_raw{i}") for i in range(2)]
        s_raw_o = [k.sem(f"p1_raw_o{i}") for i in range(WO_LOADS)]
        s_hi = k.sem("p1_w_hi")
        s_lo = k.sem("p1_w_lo")
        s_hi_o = k.sem("p1_wo_hi")
        s_lo_o = k.sem("p1_wo_lo")
        s_stat = k.sem("p1_stat")
        s_var = k.sem("p1_var")
        s_pow = k.sem("p1_pow")
        s_xn = k.sem("p1_xn")
        s_tr = k.sem("p1_transposed")
        s_xhi = k.sem("p1_xnT_hi")
        s_xlo = k.sem("p1_xnT_lo")
        s_vps = k.sem("p1_v_psum")
        s_vsb = k.sem("p1_v_copied")
        s_proj = k.sem("p1_projected")
        s_prod = k.sem("p1_products")
        s_rot = k.sem("p1_rotated")
        s_mask = k.sem("p1_mask")
        s_zero = k.sem("p1_zero")
        s_half = k.sem("p1_half")
        block = ctx.enter_context(nc.Block())

        def wo_dst(c):
            return [o[:, 2 * c:2 * c + 2, :].rearrange("p c n -> p (c n)") for o in WO]

        @block.sync
        def _(sp):
            for q in range(4):
                sp.dma_start(X[:, 2 * q:2 * q + 2, :], x_d[:, 2 * q:2 * q + 2, :]).then_inc(s_x[q], 16)
            sp.dma_start(ident[:], ident_d).then_inc(s_const, 16)
            for c in range(2):
                sp.dma_start(raw[c][:], wqk_d[c]).then_inc(s_raw[c], 16)
            sp.dma_start(cs[:], cs_d).then_inc(s_const, 16)
            for c in range(2, NW):
                sp.wait_ge(s_lo, c - 1)
                sp.dma_start(raw[c % 2][:], wqk_d[c] if c < NPAIR else wv_d[:, c - NPAIR, :]
                             ).then_inc(s_raw[c % 2], 16)
                if 3 <= c < 3 + WO_LOADS:
                    n = NWO // WO_LOADS
                    part = slice((c - 3) * n, (c - 2) * n)
                    sp.dma_start(V[:, part, :], wo_d[:, part, :]).then_inc(s_raw_o[c - 3], 16)
                if c == 6:
                    sp.wait_ge(s_zero, 1)
                    sp.wait_ge(s_rot, 4)
                    stage_k(sp, KR, KB[0], 0, s_qk[0])
            sp.dma_start(mask_f[:], mask_d).then_inc(s_mask, 16)
            sp.wait_ge(s_rot, 2 * NPAIR)
            stage_q(sp, QR, Q[0][:].rearrange("p (a n) -> p a n", a=2), 0, s_qk[0])
            sp.wait_ge(s_vsb, 1)
            stage_v(sp, V, VB[0], 0, s_vb[0])
            stage_q(sp, QR, Q[1][:].rearrange("p (a n) -> p a n", a=2), 1, s_qk[1])

        @block.gpsimd
        def _(pool):
            nc.gpsimd.memset(mhalf[:], -0.5).then_inc(s_half, 1)
            pool.wait_ge(s_half, 1)
            for h in range(2):
                norm_power(nc, pool, h, mhalf, tmp, s_var, s_pow)
            nc.gpsimd.memset(KV[0][:], 0.0).then_inc(s_zero, 1)
            for m in range(NPAIR):
                for h in range(2):
                    pool.wait_ge(s_prod, 2 * m + h + 1)
                    pr = prod[h]
                    if m >= 2:
                        dst = [QR[:, a, 4 * h:4 * h + 4, :].rearrange(
                            "p t (b m s) -> p (t b) m s", b=2, s=SEQ)[:, :, m - 2, :] for a in range(2)]
                        pr = pr.rearrange("p n (t s) -> p n t s", s=SEQ)
                    else:
                        dst = [KR[:, a, 4 * h:4 * h + 4, m, :] for a in range(2)]
                        pr = pr.rearrange("p n (t c) -> p n t c", c=P)
                    nc.gpsimd.tensor_tensor(dst[0], pr[:, 0], pr[:, 3], ALU.subtract)
                    nc.gpsimd.tensor_tensor(dst[1], pr[:, 1], pr[:, 2], ALU.add).then_inc(s_rot, 1)
            pool.wait_ge(s_rot, 2 * NPAIR)
            nc.gpsimd.memset(KV[1][:], 0.0)

        @block.scalar
        def _(act):
            def high_half(c):
                act.wait_ge(s_raw[c % 2], 16 * (c // 2 + 1))
                nc.scalar.copy(w[c % 2][0][:], raw[c % 2][:]).then_inc(s_hi, 1)

            def high_half_o(c):
                hi, _ = wo_dst(c)
                act.wait_ge(s_raw_o[c * WO_LOADS // NWO], 16)
                nc.scalar.copy(hi, V[:, c, :]).then_inc(s_hi_o, 1)

            high_half(0)
            high_half(1)
            for n in range(KC * NHALF):
                kc, h = n % KC, n // KC
                act.wait_ge(s_tr, n + 1)
                nc.scalar.copy(xnT[0][:, kc, h * HALF:(h + 1) * HALF], ps_t[:, n, :]).then_inc(s_xhi, 1)
            for c in range(2, NW):
                act.wait_ge(s_proj, 4 * (c - 1))
                high_half(c)
                if 4 <= c < NW:
                    high_half_o(c - 4)
            for t in range(NT):
                act.wait_ge(s_vps, t + 1)
                act.wait_ge(s_lo_o, t + 1)
                nc.scalar.copy(V[:, t, :], ps_v[t % 2][:]).then_inc(s_vsb, 1)

        @block.vector
        def _(dve):
            def low_half(i, r):
                dve.wait_ge(s_hi, 2 * i + r + 1)
                nc.vector.tensor_tensor(w[r % 2][1][:], raw[r % 2][:], as_f32(w[r % 2][0][:]),
                                        ALU.subtract).then_inc(s_lo, 1)

            chain = Chain(dve, s_stat)
            for h in range(2):
                norm_stats(nc, chain, X, h, st, mv, tmp, s_var, s_x)
            norm_apply(nc, chain, X, xn, 0, mv, tmp, s_pow, s_xn)
            low_half(0, 0)
            norm_apply(nc, chain, X, xn, 1, mv, tmp, s_pow, s_xn)
            for n in range(KC * NHALF):
                kc, h = n % KC, n // KC
                tok = slice(h * HALF, (h + 1) * HALF)
                dve.wait_ge(s_xhi, n + 1)
                nc.vector.tensor_tensor(xnT[1][:, kc, tok], ps_t[:, n, :], as_f32(xnT[0][:, kc, tok]),
                                        ALU.subtract).then_inc(s_xlo, 1)
            low_half(0, 1)
            dve.wait_ge(s_const, 32)

            def products(i, r):
                ps, pr = proj[r % 2], prod[r % 2]
                if not isinstance(i, int) or r >= 2:
                    dve.wait_ge(s_rot, 4 * i + r - 1)
                for a in range(2):
                    dve.wait_ge(s_proj, 8 * i + 2 * r + a + 1)
                    src = ps[:, a, :].rearrange("p (b s) -> p b s", s=SEQ)
                    for m in range(2):
                        last = nc.vector.tensor_tensor(
                            pr[:, 2 * a + m, :].rearrange("p (b s) -> p b s", s=SEQ), src,
                            bc(cs[:, m, :], 1, HALF // SEQ), ALU.mult)
                last.then_inc(s_prod, 1)

            def two_pairs(i):
                for r in range(4):
                    products(i, r)
                    if r % 2:
                        low_half(i, 2 + r // 2)

            two_pairs(0)
            with dve.Fori(1, NPAIR // 2) as i:
                two_pairs(i)
            dve.wait_ge(s_mask, 16)
            nc.vector.tensor_copy(mask[:], bc(mask_f[:], 1, 4))
            nc.vector.tensor_copy(ident_b[:], ident[:])
            for c in range(NWO):
                hi, lo = wo_dst(c)
                dve.wait_ge(s_hi_o, c + 1)
                nc.vector.tensor_tensor(lo, V[:, c, :], as_f32(hi), ALU.subtract).then_inc(s_lo_o, 1)

        @block.tensor
        def _(pe):
            pe.wait_ge(s_const, 32)
            for h in range(NHALF):
                for kc in range(KC):
                    for q in range(4):
                        t = 4 * h + q
                        pe.wait_ge(s_xn, t + 1)
                        last = nc.tensor.transpose(ps_t[:, 2 * h + kc, q * P:(q + 1) * P],
                                                   xn[:, t, kc * P:(kc + 1) * P], ident[:])
                    last.then_inc(s_tr, 1)

            def project(i, r):
                h = r % 2
                wv = [x[:].rearrange("p (k a m) -> p k a m", k=KC, a=2) for x in w[r // 2]]
                if h == 0:
                    pe.wait_ge(s_lo, 2 * i + r // 2 + 1)
                if isinstance(i, int) and r < 2:
                    pe.wait_ge(s_xlo, 2 * r + 2)
                else:
                    pe.wait_ge(s_prod, 4 * i + r - 1)
                for a in range(2):
                    for kc in range(KC):
                        last = split3(nc.tensor, proj[r % 2][:, a, :], wv, xnT, (slice(None), kc, a),
                                      (slice(None), kc, slice(h * HALF, (h + 1) * HALF)), kc == 0, kc == KC - 1)
                    last.then_inc(s_proj, 1)

            for r in range(4):
                project(0, r)
            with pe.Fori(1, NPAIR // 2) as i:
                for r in range(4):
                    project(i, r)
            pe.wait_ge(s_lo, NW)
            for t in range(NT):
                if t >= 2:
                    pe.wait_ge(s_vsb, t - 1)
                for kc in range(KC):
                    last = split3(nc.tensor, ps_v[t % 2][:], xnT, w[kc], (slice(None), kc, slice(t * P, (t + 1) * P)),
                                  (slice(None),), kc == 0, kc == KC - 1)
                last.then_inc(s_vps, 1)


def attention_phase(nc, com, X, QR, KR, V, ident, staged, s_qk, s_vb, mask, ident_b, ctx_d, wx_d,
                    gate_d, wch_d):
    NUN = 4 * NT
    S_T, S_PV, S_LO, S_Y, S_ADD = 2, 3, 4, 5, 6
    X_MEAN, X_VAR, X_KV, X_NORM, X_Q, X_S, X_SUM, X_T, X_PV, X_DIFF, X_ADD = 10, 11, 11, 12, 13, 14, 15, 16, 17, 18, 19
    steps = Steps(NUN, X_ADD - 3, 2)
    with ExitStack() as ctx:
        k = Kit(nc, ctx)
        Q, _, KB, VB = staged
        Q = [x[:].rearrange("p (a n) -> p a n", a=2) for x in Q]
        EX = k.sb("probabilities", [P, 4, 4, P])
        PT = k.sb("probs_T", [P, 2, 2, 2 * P])
        OT = [[k.sb(f"out_T_{n}{i}", [P, 2 * G, P], F32R) for n in ("hi", "lo")] for i in range(2)]
        mx = k.sb("row_max", [P, 2, 8])
        sm = k.sb("row_sum", [P, 2, 8])
        ri = k.sb("row_inv", [P, 4, 8])
        WX = k.sb("wx", [P, 4, P])
        XQ = k.sb("xq", [P, 2, D])
        rs = k.sb("xrstd", [P, 9])
        xmx = k.sb("xrow_max", [P, XH])
        xsm = k.sb("xrow_sum", [P, XH])
        xri = k.sb("xrow_inv", [P, XH])
        kbx = QR[:, 0, 0, :].rearrange("p (c b h s) -> p c b h s", c=2, b=2, h=4)
        vbx = QR[:, 0, 1, :].rearrange("p (r h b g n) -> p r h b g n", r=2, h=4, b=2, g=2)
        C = QR[:, 1, 0, 0:2 * D].rearrange("p (r d) -> p r d", r=2)
        DF = QR[:, 1, 0, 2 * D:3 * D]
        XC = KR[:, 1, 0, :, :].rearrange("p s c -> p (s c)")
        SQ = KR[:, 0, 0, :, :].rearrange("p s c -> p (s c)")
        QT = QR[:, 1, 0, 3 * D:4 * D].rearrange("p (c m) -> p c m", c=2)
        XE = QR[:, 1, 1, 0:HALF].rearrange("p (h s) -> p h s", h=XH)
        XPT = QR[:, 1, 1, HALF:2 * HALF].rearrange("p (h m) -> p h m", h=4)
        WO = com.WO
        XN3 = QR[:, 0, 2, :].rearrange("p (t d) -> p t d", t=NT // 2)
        raw13 = QR[:, 0, 3, 0:2 * D]
        gate = QR[:, 1, 3, 0:KC * E].rearrange("p (k e) -> p k e", k=KC)
        ps_s = [k.bank(f"ps_scores{i}") for i in range(2)]
        ps_p = k.bank("ps_probsT")
        ps_o = k.bank("ps_outT")
        ps_y = k.bank("ps_y")
        ps_xq = k.bank("ps_x_queries")
        ps_xs = k.bank("ps_x_scores")
        ps_xo = k.bank("ps_x_out")

        s_scores = k.sem("p2_scores")
        s_max = k.sem("p2_max")
        s_shift = k.sem("p2_shifted")
        s_exp = k.sem("p2_exp")
        s_sum = k.sem("p2_sum")
        s_inv = k.sem("p2_inverse")
        s_norm = k.sem("p2_normalised")
        s_pT = k.sem("p2_probs_transposed")
        s_pTc = k.sem("p2_probsT_copied")
        s_pv = k.sem("p2_values_mixed")
        s_ohi = k.sem("p2_outT_hi")
        s_olo = k.sem("p2_outT_lo")
        s_y = k.sem("p2_out_projected")
        s_res = k.sem("p2_residual")
        x_w = k.sem("x_weights")
        x_c = [k.sem(f"x_context{i}") for i in range(2)]
        x_zero = k.sem("x_zero")
        x_kv = k.sem("x_keys_values")
        x_k = k.sem("x_keys_copied")
        x_v = k.sem("x_values_copied")
        x_stat = k.sem("x_stat")
        x_tok = k.sem("x_tokens")
        x_cent = k.sem("x_centred")
        x_sq = k.sem("x_squares")
        x_var = k.sem("x_var")
        x_pow = k.sem("x_pow")
        x_norm = k.sem("x_normed")
        x_q = k.sem("x_queries")
        x_qc = k.sem("x_queries_copied")
        x_scores = k.sem("x_scores")
        x_max = k.sem("x_max")
        x_shift = k.sem("x_shifted")
        x_exp = k.sem("x_exp")
        x_sum = k.sem("x_sum")
        x_inv = k.sem("x_inverse")
        x_prob = k.sem("x_normalised")
        x_pT = k.sem("x_probs_transposed")
        x_pTc = k.sem("x_probsT_copied")
        x_pv = k.sem("x_values_mixed")
        x_diff = k.sem("x_diff")
        x_y = k.sem("x_projected")
        x_res = k.sem("x_residual")
        f_gate = k.sem("f_gate")
        f_ghi = k.sem("f_gate_hi")
        f_stat = k.sem("f_stat")
        f_xn = k.sem("f_normed")
        f_tr = k.sem("f_transposed")
        f_xhi = k.sem("f_xnT_hi")
        block = ctx.enter_context(nc.Block())

        def at(i, r, k_):
            return isinstance(i, int) and 8 * i + r == k_

        def cross(i, r, distance):
            n, rest = divmod(r - distance, 4)
            if rest or (isinstance(i, int) and not 0 <= 2 * i + n < NT):
                return None
            return n

        @block.sync
        def _(sp):
            stage_k(sp, KR, KB[1], 1, s_qk[1])
            stage_v(sp, V, VB[1], 1, s_vb[1])
            sp.dma_start(WX[:], wx_d).then_inc(x_w, 16)

            def context(t, r, n):
                if not isinstance(n, int) or n:
                    sp.wait_ge(x_kv, n)
                sp.dma_start(C[:, r, :], ctx_d[:, bass.ds(t, 1), :].rearrange("p o d -> p (o d)")
                             ).then_inc(x_c[r], 16)

            def two_tiles(i):
                for r in range(2):
                    sp.wait_ge(s_scores, 8 * i + 4 * r - 4)
                    stage_q(sp, QR, Q[r], 2 * i + r, s_qk[r])
                    stage_k(sp, KR, KB[r], 2 * i + r, s_qk[r])
                    context(2 * i + r - 2, r, 0 if isinstance(i, int) else 2 * i + r - 3)
                    sp.wait_ge(s_pv, 8 * i + 4 * r - 4)
                    stage_v(sp, V, VB[r], 2 * i + r, s_vb[r])

            two_tiles(1)
            with sp.Fori(2, NT // 2) as i:
                two_tiles(i)
            for t in (NT - 2, NT - 1):
                context(t, t % 2, t - 1)
            sp.dma_start(raw13, wch_d[0, :, 0:2 * D]).then_inc(com.s_r13, 16)
            sp.dma_start(gate, gate_d).then_inc(f_gate, 16)

        @block.gpsimd
        def _(pool):
            def step(i, r):
                if isinstance(i, int) and 8 * i + r == X_KV - 2:
                    nc.gpsimd.memset(kbx, 0.0).then_inc(x_zero, 1)
                    nc.gpsimd.memset(vbx, 0.0).then_inc(x_zero, 1)
                q = r - 1
                if steps.live(i, q):
                    pool.wait_ge(s_inv, 8 * i + q + 1)
                    e = EX[:, q % 4, :, :].rearrange("p x (g s) -> p (x g) s", g=2)
                    nc.gpsimd.tensor_tensor(e, e, bc(ri[:, q % 4, :], 2, SEQ), ALU.mult).then_inc(s_norm, 1)
                n = cross(i, r, X_SUM)
                if n is not None:
                    pool.wait_ge(x_inv, 2 * i + n + 1)
                    nc.gpsimd.tensor_tensor(XE, XE, bc(xri[:], 2, SEQ), ALU.mult).then_inc(x_prob, 1)
                n = cross(i, r, X_MEAN)
                if n is not None:
                    pool.wait_ge(x_cent, 2 * i + n + 1)
                    nc.gpsimd.tensor_tensor(SQ, XQ[:, n % 2, :], XQ[:, n % 2, :], ALU.mult).then_inc(x_sq, 1)
                n = cross(i, r, X_VAR)
                if n is not None:
                    pool.wait_ge(x_var, 2 * i + n + 1)
                    nc.gpsimd.tensor_tensor(rs[:, 1:2], rs[:, 0:1], com.mhalf[:, 0:1], ALU.pow).then_inc(x_pow, 1)

                if at(i, r, 34):
                    norm_power(nc, pool, 0, com.mhalf, com.tmp, com.s_var, com.s_pow)
                if at(i, r, 38):
                    pool.wait_ge(com.s_13hi, 1)
                    nc.gpsimd.tensor_tensor(com.w13[1][:], raw13, as_f32(com.w13[0][:]),
                                            ALU.subtract).then_inc(com.s_13lo, 1)

            steps.run(pool, step)

        @block.scalar
        def _(act):
            def step(i, r):
                if steps.live(i, r):
                    act.wait_ge(s_shift, 8 * i + r + 1)
                    nc.scalar.activation(EX[:, r % 4, :, :], EX[:, r % 4, :, :], ACT.Exp,
                                         scale=SCALE).then_inc(s_exp, 1)
                q = r - S_T
                if steps.live(i, q):
                    act.wait_ge(s_pT, 8 * i + q + 1)
                    if steps.later(i, q, 2):
                        act.wait_ge(s_pv, 8 * i + q - 1)
                    nc.scalar.copy(PT[:, q % 2, :, :].rearrange("p a n -> p (a n)"),
                                   ps_p[:]).then_inc(s_pTc, 1)
                q = r - S_PV
                if steps.live(i, q):
                    act.wait_ge(s_pv, 8 * i + q + 1)
                    if steps.later(i, q, 4):
                        act.wait_ge(s_y, 8 * i + 2 * (q // 2) - 2)
                    b = q % 2
                    nc.scalar.copy(OT[(q // 2) % 2][0][:, :, b * SEQ:(b + 1) * SEQ],
                                   ps_o[:].rearrange("p (c s) -> p c s", s=SEQ)).then_inc(s_ohi, 1)
                n = cross(i, r, X_Q)
                if n is not None:
                    act.wait_ge(x_q, 2 * i + n + 1)
                    nc.scalar.copy(QT.rearrange("p c m -> p (c m)"), ps_xq[:, 0:D]).then_inc(x_qc, 1)
                n = cross(i, r, X_S)
                if n is not None:
                    act.wait_ge(x_shift, 2 * i + n + 1)
                    nc.scalar.activation(XE, XE, ACT.Exp, scale=XSCALE).then_inc(x_exp, 1)
                n = cross(i, r, X_T)
                if n is not None:
                    act.wait_ge(x_pT, 2 * i + n + 1)
                    nc.scalar.copy(XPT.rearrange("p h m -> p (h m)"), ps_xs[:]).then_inc(x_pTc, 1)
                n = cross(i, r, X_KV)
                if n is not None:
                    if isinstance(i, int) and 2 * i + n == 0:
                        act.wait_ge(x_zero, 2)
                    act.wait_ge(x_kv, 2 * i + n + 1)
                    for h4 in range(4):
                        rows = slice(h4 * XN, (h4 + 1) * XN)
                        last = nc.scalar.copy(kbx[rows, :, :, h4, :].rearrange("p c b s -> p (c b) s"),
                                              ps_xo[rows, 0:D].rearrange("p (m s) -> p m s", s=SEQ))
                    last.then_inc(x_k, 1)
                if at(i, r, 38):
                    act.wait_ge(s_y, NUN)
                    act.wait_ge(f_gate, 16)
                    nc.scalar.copy(com.gw[0][:], gate).then_inc(f_ghi, 1)
                    act.wait_ge(com.s_r13, 16)
                    nc.scalar.copy(com.w13[0][:], raw13).then_inc(com.s_13hi, 1)
                if at(i, r, 37):
                    for kc in range(KC):
                        act.wait_ge(f_tr, kc + 1)
                        nc.scalar.copy(com.xnT[0][:, kc, 0:HALF], ps_s[kc][:]).then_inc(f_xhi, 1)

            steps.run(act, step)

        @block.vector
        def _(dve):
            def tile_of(t):
                return X[:, bass.ds(t, 1), :].rearrange("p o d -> p (o d)")

            half0 = Chain(dve, f_stat)

            def stat(i, n, j, ins):
                ins.then_inc(x_stat, 1)
                dve.wait_ge(x_stat, 7 * (2 * i + n) + j)

            def step(i, r):
                q = r - S_LO
                if steps.live(i, q):
                    b, ot = q % 2, OT[(q // 2) % 2]
                    dve.wait_ge(s_ohi, 8 * i + q + 1)
                    hi, lo = (o[:, :, b * SEQ:(b + 1) * SEQ] for o in ot)
                    nc.vector.tensor_tensor(lo, ps_o[:].rearrange("p (c s) -> p c s", s=SEQ), as_f32(hi),
                                            ALU.subtract).then_inc(s_olo, 1)
                q = r - S_ADD
                if steps.live(i, q) and q % 4 == 3:
                    t = 2 * i + q // 4
                    dve.wait_ge(s_y, 8 * i + q + 1)
                    nc.vector.tensor_tensor(XC, ps_y[:, 0:D], tile_of(t), ALU.add).then_inc(x_tok, 1)
                    nc.vector.tensor_tensor(tile_of(t), ps_y[:, 0:D], tile_of(t), ALU.add).then_inc(s_res, 1)
                n = cross(i, r, X_ADD)
                if n is not None:
                    t = 2 * i + n
                    dve.wait_ge(x_y, t + 1)
                    nc.vector.tensor_tensor(tile_of(t), ps_xq[:, 0:D], tile_of(t), ALU.add).then_inc(x_res, 1)
                if steps.live(i, r):
                    rows = ps_s[r % 2][:].rearrange("p (x s) -> p x s", s=SEQ)
                    dve.wait_ge(s_scores, 8 * i + r + 1)
                    nc.vector.tensor_reduce(mx[:, r % 2, :], rows, AX.X, ALU.max).then_inc(s_max, 1)
                    dve.wait_ge(s_max, 8 * i + r + 1)
                    if steps.later(i, r, 4):
                        dve.wait_ge(s_pT, 8 * i + r - 3)
                    nc.vector.tensor_tensor(EX[:, r % 4, :, :].rearrange("p x (g s) -> p (x g) s", g=2), rows,
                                            bc(mx[:, r % 2, :], 2, SEQ), ALU.subtract).then_inc(s_shift, 1)
                q = r - 1
                if steps.live(i, q):
                    dve.wait_ge(s_exp, 8 * i + q + 1)
                    nc.vector.tensor_reduce(sm[:, q % 2, :], EX[:, q % 4, :, :].rearrange("p x (g s) -> p (x g) s", g=2),
                                            AX.X, ALU.add).then_inc(s_sum, 1)
                    dve.wait_ge(s_sum, 8 * i + q + 1)
                    nc.vector.reciprocal(ri[:, q % 4, :], sm[:, q % 2, :]).then_inc(s_inv, 1)
                n = cross(i, r, X_DIFF)
                if n is not None:
                    dve.wait_ge(x_pv, 2 * i + n + 1)
                    for b in range(2):
                        rows = slice(b * SEQ, (b + 1) * SEQ)
                        last = nc.vector.tensor_tensor(
                            DF[rows, :].rearrange("p (h n) -> p h n", h=4),
                            XQ[rows, n % 2, :].rearrange("p (h n) -> p h n", h=4),
                            ps_xo[rows, :].rearrange("p (h b n) -> p h b n", h=4, b=2)[:, :, b, :], ALU.subtract)
                    last.then_inc(x_diff, 1)
                n = cross(i, r, X_S)
                if n is not None:
                    rows = ps_xs[:].rearrange("p (x s) -> p x s", s=SEQ)
                    dve.wait_ge(x_scores, 2 * i + n + 1)
                    nc.vector.tensor_reduce(xmx[:], rows, AX.X, ALU.max).then_inc(x_max, 1)
                    dve.wait_ge(x_max, 2 * i + n + 1)
                    nc.vector.tensor_tensor(XE, rows, bc(xmx[:], 2, SEQ), ALU.subtract).then_inc(x_shift, 1)
                n = cross(i, r, X_SUM)
                if n is not None:
                    dve.wait_ge(x_exp, 2 * i + n + 1)
                    nc.vector.tensor_reduce(xsm[:], XE, AX.X, ALU.add).then_inc(x_sum, 1)
                    dve.wait_ge(x_sum, 2 * i + n + 1)
                    nc.vector.reciprocal(xri[:], xsm[:]).then_inc(x_inv, 1)
                n = cross(i, r, X_MEAN)
                if n is not None:
                    dve.wait_ge(x_tok, 2 * i + n + 1)
                    stat(i, n, 1, nc.vector.tensor_reduce(rs[:, 6:7], XC, AX.X, ALU.add))
                    stat(i, n, 2, nc.vector.tensor_scalar(rs[:, 7:8], rs[:, 6:7], 1.0 / D, None, ALU.mult))
                    nc.vector.tensor_scalar(XQ[:, n % 2, :], XC, rs[:, 7:8], None,
                                            ALU.subtract).then_inc(x_cent, 1)
                n = cross(i, r, X_VAR)
                if n is not None:
                    dve.wait_ge(x_sq, 2 * i + n + 1)
                    stat(i, n, 3, nc.vector.tensor_reduce(rs[:, 8:9], SQ, AX.X, ALU.add))
                    nc.vector.tensor_scalar(rs[:, 0:1], rs[:, 8:9], 1.0 / D, EPS, ALU.mult, ALU.add
                                            ).then_inc(x_var, 1)
                n = cross(i, r, X_NORM)
                if n is not None:
                    dve.wait_ge(x_k, 2 * i + n + 1)
                    for b in range(2):
                        src = ps_xo[b * SEQ:(b + 1) * SEQ, D:2 * D].rearrange("p (m g n) -> p m g n", g=2, n=XN)
                        for h2 in range(2):
                            last = nc.vector.tensor_copy(vbx[h2 * SEQ:(h2 + 1) * SEQ, n % 2, :, b, h2, :], src[:, :, h2, :])
                    last.then_inc(x_v, 1)
                    dve.wait_ge(x_pow, 2 * i + n + 1)
                    stat(i, n, 4, nc.vector.tensor_tensor(rs[:, 2:3], rs[:, 1:2], rs[:, 1:2], ALU.mult))
                    stat(i, n, 5, nc.vector.tensor_tensor(rs[:, 3:4], rs[:, 2:3], rs[:, 0:1], ALU.mult))
                    stat(i, n, 6, nc.vector.tensor_scalar(rs[:, 4:5], rs[:, 3:4], -0.5, 1.5, ALU.mult, ALU.add))
                    stat(i, n, 7, nc.vector.tensor_tensor(rs[:, 5:6], rs[:, 1:2], rs[:, 4:5], ALU.mult))
                    nc.vector.tensor_scalar(XQ[:, n % 2, :], XQ[:, n % 2, :], rs[:, 5:6], None,
                                            ALU.mult).then_inc(x_norm, 1)
                if at(i, r, 33):
                    dve.wait_ge(x_res, NT // 2)
                    norm_stats(nc, half0, X, 0, com.st, com.mv, com.tmp, com.s_var)
                if at(i, r, 38):
                    dve.wait_ge(f_ghi, 1)
                    nc.vector.tensor_tensor(com.gw[1][:], gate, as_f32(com.gw[0][:]), ALU.subtract)
                if at(i, r, 35):
                    norm_apply(nc, half0, X, XN3, 0, com.mv, com.tmp, com.s_pow, f_xn)
                if at(i, r, 37):
                    for kc in range(KC):
                        dve.wait_ge(f_xhi, kc + 1)
                        nc.vector.tensor_tensor(com.xnT[1][:, kc, 0:HALF], ps_s[kc][:],
                                                as_f32(com.xnT[0][:, kc, 0:HALF]), ALU.subtract)
                for t in range(NT // 2, NT - 1):
                    if at(i, r, 4 * t + X_ADD + 1):
                        dve.wait_ge(x_res, t + 1)
                        nc.vector.bn_stats(com.st[:, t, :], X[:, t, :])

            steps.run(dve, step)

        @block.tensor
        def _(pe):
            def step(i, r):
                if steps.live(i, r):
                    ring, gh, b = (r // 4) % 2, (r // 2) % 2, r % 2
                    if r % 4 == 0:
                        pe.wait_ge(s_qk[ring], 16 * (N_Q + N_K) * i + 16 * (N_Q + N_K))
                    if steps.later(i, r, 2):
                        pe.wait_ge(s_shift, 8 * i + r - 1)
                    nc.tensor.matmul(ps_s[r % 2][:], ident_b[:], mask[:].rearrange("p x n -> p (x n)"),
                                     start=True, stop=False)
                    for x in range(4):
                        s, m0 = x // 2, (2 * G * b + 2 * x) * SEQ
                        last = nc.tensor.matmul(ps_s[r % 2][:, x * P:(x + 1) * P],
                                                Q[ring][:, gh, m0:m0 + P],
                                                KB[ring][:, gh, s, b, :], start=False, stop=x == 3)
                    last.then_inc(s_scores, 1)
                q = r - S_T
                if steps.live(i, q):
                    pe.wait_ge(s_norm, 8 * i + q + 1)
                    if steps.later(i, q, 1):
                        pe.wait_ge(s_pTc, 8 * i + q)
                    for x in range(4):
                        last = nc.tensor.transpose(ps_p[:, x * P:(x + 1) * P], EX[:, q % 4, x, :], ident[:])
                    last.then_inc(s_pT, 1)
                q = r - S_PV
                if steps.live(i, q):
                    ring, gh, b = (q // 4) % 2, (q // 2) % 2, q % 2
                    if q % 4 == 0:
                        j = i + q // 8
                        pe.wait_ge(s_vb[ring], 16 * N_V * j + 16 * N_V)
                    pe.wait_ge(s_pTc, 8 * i + q + 1)
                    if steps.later(i, q, 1):
                        pe.wait_ge(s_olo, 8 * i + q)
                    for x in range(2):
                        last = nc.tensor.matmul(ps_o[:, x * 2 * P:(x + 1) * 2 * P],
                                                VB[ring][:, b, 2 * x + gh, :], PT[:, q % 2, x, :],
                                                start=True, stop=True)
                    last.then_inc(s_pv, 1)

                n = cross(i, r, X_Q)
                if n is not None:
                    pe.wait_ge(x_norm, 2 * i + n + 1)
                    for c in range(2):
                        last = nc.tensor.matmul(ps_xq[:, c * P:(c + 1) * P], XQ[:, n % 2, c * P:(c + 1) * P],
                                                WX[:, 0, :], start=True, stop=True)
                    last.then_inc(x_q, 1)
                n = cross(i, r, X_PV)
                if n is not None:
                    pe.wait_ge(x_pTc, 2 * i + n + 1)
                    ahead = 2 * i + n + 2
                    if isinstance(i, int):
                        ahead = min(ahead, NT)
                    pe.wait_ge(x_v, ahead)
                    for hp in range(4):
                        last = nc.tensor.matmul(ps_xo[:, hp * P:(hp + 1) * P], XPT[:, hp, :],
                                                vbx[:, n % 2, hp, :, :, :].rearrange("p b h n -> p (b h n)"),
                                                start=True, stop=True)
                    last.then_inc(x_pv, 1)
                n = cross(i, r, X_S)
                if n is not None:
                    pe.wait_ge(x_qc, 2 * i + n + 1)
                    pe.wait_ge(x_k, 2 * i + n + 1)
                    if not isinstance(i, int) or 2 * i + n >= 1:
                        pe.wait_ge(x_pTc, 2 * i + n)
                    for b in range(2):
                        for c in range(2):
                            last = nc.tensor.matmul(ps_xs[b * SEQ:(b + 1) * SEQ, c * 4 * SEQ:(c + 1) * 4 * SEQ],
                                                    QT[:, c, b * SEQ:(b + 1) * SEQ],
                                                    kbx[:, c, b, :, :].rearrange("p h s -> p (h s)"),
                                                    start=True, stop=True)
                    last.then_inc(x_scores, 1)
                n = cross(i, r, X_T)
                if n is not None:
                    pe.wait_ge(x_prob, 2 * i + n + 1)
                    for hp in range(4):
                        last = nc.tensor.transpose(ps_xs[:, hp * P:(hp + 1) * P],
                                                   XE[:, 2 * hp:2 * hp + 2, :].rearrange("p h s -> p (h s)"), ident[:])
                    last.then_inc(x_pT, 1)
                n = cross(i, r, X_KV)
                if n is not None:
                    if isinstance(i, int) and 2 * i + n == 0:
                        pe.wait_ge(x_w, 16)
                    pe.wait_ge(x_c[n % 2], 16 * (i + n // 2 + 1))
                    if not isinstance(i, int) or 2 * i + n >= 2:
                        pe.wait_ge(x_diff, 2 * i + n - 1)
                    for c in range(2):
                        nc.tensor.matmul(ps_xo[:, c * P:(c + 1) * P], C[:, n % 2, c * P:(c + 1) * P], WX[:, 1, :],
                                         start=True, stop=True)
                    nc.tensor.matmul(ps_xo[:, D:2 * D], WX[:, 2, :], C[:, n % 2, :], start=True, stop=True
                                     ).then_inc(x_kv, 1)

                q = r - S_Y
                if steps.live(i, q):
                    v, part = q // 2, q % 2
                    if part == 0:
                        pe.wait_ge(s_olo, 8 * i + 2 * v + 2)
                    if q % 4 == 0 and steps.later(i, q, 4):
                        pe.wait_ge(s_res, 2 * i + q // 4)
                    for c in range(4 * part, 4 * part + 4):
                        last = split3(nc.tensor, ps_y[:, 0:D], OT[v % 2], WO,
                                      (slice(None), c), (slice(None), 8 * (v % 2) + c),
                                      q % 4 == 0 and c == 0, q % 4 == 3 and c == 7)
                    last.then_inc(s_y, 1)
                n = cross(i, r, X_DIFF)
                if n is not None:
                    pe.wait_ge(x_diff, 2 * i + n + 1)
                    nc.tensor.matmul(ps_xq[:, 0:D], WX[:, 3, :], DF, start=True, stop=True).then_inc(x_y, 1)
                if at(i, r, 36):
                    pe.wait_ge(s_shift, NUN)
                    for kc in range(KC):
                        for t in range(NT // 2):
                            pe.wait_ge(f_xn, t + 1)
                            last = nc.tensor.transpose(ps_s[kc][:, t * P:(t + 1) * P], XN3[:, t, kc * P:(kc + 1) * P],
                                                       ident[:])
                        last.then_inc(f_tr, 1)

            steps.run(pe, step)


def expert_phase(nc, com, X, ident, d, out_d):
    LAG = 2
    UP = 2 * D
    with ExitStack() as ctx:
        k = Kit(nc, ctx)
        raw13 = [k.sb(f"raw13_{i}", [P, UP]) for i in range(2)]
        raw2 = [k.sb(f"raw2_{i}", [P, D]) for i in range(2)]
        w13 = [com.w13, [k.sb(f"w13_{n}1", [P, UP], F32R) for n in ("hi", "lo")]]
        w2 = [[k.sb(f"w2_{n}{i}", [P, D], F32R) for n in ("hi", "lo")] for i in range(2)]
        xnT, gw = com.xnT, com.gw
        xn = k.sb("f_xn", [P, NT, D])
        lgT = k.sb("logits_T", [E, T])
        bias = k.sb("bias", [P, E])
        lower = k.sb("lower", [P, E, E])
        sg = k.sb("silu", [P, 2, HALF])
        hu = k.sb("gated", [P, 2, HALF])
        hw = k.sb("weighted", [P, 2, HALF])
        H = [[k.sb(f"h_{n}{i}", [P, HALF], F32R) for n in ("hi", "lo")] for i in range(2)]
        CW = k.sb("cw_rows", [P, 2, T])
        cwr = k.sb("cw_repeated", [P, NT, 2, EG, UNIT])
        yT = k.sb("yT", [P, KC, T])
        mhalf, st, mv, tmp = com.mhalf, com.st, com.mv, com.tmp
        ex = k.sb("g_exp", [P, NT, E])
        den = k.sb("g_den", [P, NT, E])
        sc = k.sb("g_scores", [P, NT, E])
        biased = k.sb("g_biased", [P, NT, E])
        gm = k.sb("g_group_max", [P, NT, GE])
        gbeat = k.sb("g_gbeat", [P, 3, NT, GE, GE])
        gcnt = k.sb("g_gcount", [P, NT, GE])
        gsel = k.sb("g_group_sel", [P, NT, GE])
        goff = k.sb("g_group_off", [P, NT, GE])
        kept = k.sb("g_kept", [P, NT, E])
        msk = k.sb("g_masked", [P, NT, E])
        beat = k.sb("g_beat", [P, NT, E, E])
        tie = k.sb("g_tie", [P, NT, E, E])
        cnt = k.sb("g_count", [P, NT, E])
        sel = k.sb("g_selected", [P, NT, E])
        picked = k.sb("g_picked", [P, NT, E])
        wsum = k.sb("g_sum", [P, 2, NT])
        cw = k.sb("g_weight", [P, NT, E])
        acc = [[k.bank(f"acc{dc}{h}") for h in range(NHALF)] for dc in range(KC)]
        up = [[k.bank(f"up{n}{i}") for n in range(2)] for i in range(2)]

        s_bias = k.sem("p4_bias")
        s_r13 = [com.s_r13, k.sem("p4_raw13_1")]
        s_r2 = [k.sem(f"p4_raw2_{i}") for i in range(2)]
        s_stat = k.sem("p4_stat")
        s_app = k.sem("p4_norm_steps")
        s_xn = k.sem("p4_xn")
        s_tr = k.sem("p4_transposed")
        s_xhi = k.sem("p4_xnT_hi")
        s_xlo = k.sem("p4_xnT_lo")
        s_logT = k.sem("p4_logits_T")
        s_lgT = k.sem("p4_logits_T_copied")
        s_log = k.sem("p4_logits")
        s_gexp = k.sem("p4_gate_exp")
        s_g = k.sem("p4_gating")
        s_masked = k.sem("p4_masked")
        s_equal = k.sem("p4_equal")
        s_tie = k.sem("p4_ties")
        s_cwr = k.sem("p4_cw_repeated")
        s_cwt = k.sem("p4_cw_transposed")
        s_cw = k.sem("p4_cw_rows")
        s_13hi, s_13lo = com.s_13hi, com.s_13lo
        s_2hi = k.sem("p4_w2_hi")
        s_2lo = k.sem("p4_w2_lo")
        s_up = k.sem("p4_up")
        s_silu = k.sem("p4_silu")
        s_gated = k.sem("p4_gated")
        s_wtd = k.sem("p4_weighted")
        s_hhi = k.sem("p4_h_hi")
        s_hlo = k.sem("p4_h_lo")
        s_down = k.sem("p4_down")
        s_yT = k.sem("p4_yT")
        s_yt = k.sem("p4_y_transposed")
        s_y = k.sem("p4_y")
        s_out = k.sem("p4_out")
        block = ctx.enter_context(nc.Block())

        N0 = 2 * NSC

        def run_units(eng, step, lag):
            for n in range(N0 + 4):
                step((n - N0) // 4, (n - N0) % 4)
            with eng.Fori(1, NU - 1) as u:
                for r in range(4):
                    step(u, r)
            for r in range(4 + lag):
                step(NU - 1, r)

        def live(u, q):
            return not isinstance(u, int) or 0 <= 4 * u + N0 + q < 2 * NC

        def after(u, q, n):
            return not isinstance(u, int) or 4 * u + N0 + q >= n

        def shared(u, q):
            return isinstance(u, int) and 4 * u + q < 0

        def place(q):
            return (NSC + q // 2) % 2

        @block.sync
        def _(sp):
            def load13(u, q):
                c, i = 2 * u + NSC + q // 2, place(q)
                if after(u, q, 4):
                    sp.wait_ge(s_13lo, c - 1)
                sp.dma_start(raw13[i][:], d["wch"][bass.ds(c, 1), :, 0:UP].rearrange("o p n -> (o p) n")
                             ).then_inc(s_r13[i], 16)

            def load2(u, q):
                c, i = 2 * u + NSC + q // 2, place(q)
                if after(u, q, 4):
                    sp.wait_ge(s_2lo, c - 1)
                sp.dma_start(raw2[i][:], d["wch"][bass.ds(c, 1), :, UP:UP + D].rearrange("o p n -> (o p) n")
                             ).then_inc(s_r2[i], 16)

            load13(-1, 0)
            load2(-2, 2)
            sp.dma_start(bias[:], d["bias"].partition_broadcast(P)).then_inc(s_bias, 16)
            sp.dma_start(lower[:], d["lower"].partition_broadcast(P)).then_inc(s_bias, 16)

            def step(u, r):
                if r % 2 == 0:
                    if live(u, r + 4):
                        load13(u, r + 4)
                    if live(u, r + 2):
                        load2(u, r + 2)

            run_units(sp, step, 0)
            for q in range(2):
                sp.wait_ge(s_y, 4 * (q + 1))
                sp.dma_start(out_d[:, 4 * q:4 * q + 4, :], xn[:, 4 * q:4 * q + 4, :]).then_inc(s_out, 16)
            sp.wait_ge(s_out, 32)

        @block.gpsimd
        def _(pool):
            def low13(u, q):
                c, i = 2 * u + NSC + q // 2, place(q)
                pool.wait_ge(s_13hi, c + 1)
                nc.gpsimd.tensor_tensor(w13[i][1][:], raw13[i][:], as_f32(w13[i][0][:]), ALU.subtract).then_inc(s_13lo, 1)

            def low2(u, q):
                c, i = 2 * u + NSC + q // 2, place(q)
                pool.wait_ge(s_2hi, c + 1)
                nc.gpsimd.tensor_tensor(w2[i][1][:], raw2[i][:], as_f32(w2[i][0][:]), ALU.subtract).then_inc(s_2lo, 1)

            norm_power(nc, pool, 1, mhalf, tmp, com.s_var, com.s_pow)

            def step(u, r):
                if r % 2 == 0:
                    if live(u, r + 2):
                        low13(u, r + 2)
                    if live(u, r):
                        low2(u, r)
                if isinstance(u, int) and 4 * u + r == -5:
                    pool.wait_ge(s_equal, 1)
                    nc.gpsimd.tensor_tensor(tie[:], tie[:], bc(lower[:], 1, NT), ALU.mult).then_inc(s_tie, 1)
                if live(u, r) and not shared(u, r):
                    if isinstance(u, int) and u == 0 and r == 0:
                        pool.wait_ge(s_cw, 4)
                    pool.wait_ge(s_gated, 4 * u + N0 + r + 1)
                    if not isinstance(u, int) or 4 * u + r >= 2:
                        pool.wait_ge(s_hlo, 4 * u + N0 + r - 1)
                    h = r % 2
                    nc.gpsimd.tensor_tensor(hw[:, h, :], hu[:, h, :], CW[:, r // 2, h * HALF:(h + 1) * HALF],
                                            ALU.mult).then_inc(s_wtd, 1)

            run_units(pool, step, 0)

        @block.scalar
        def _(act):
            def high13(u, q):
                c, i = 2 * u + NSC + q // 2, place(q)
                act.wait_ge(s_r13[i], 16 * (u + (NSC + q // 2) // 2 + 1))
                if after(u, q, 4):
                    act.wait_ge(s_up, 2 * c - 2)
                nc.scalar.copy(w13[i][0][:], raw13[i][:]).then_inc(s_13hi, 1)

            def high2(u, q):
                c, i = 2 * u + NSC + q // 2, place(q)
                act.wait_ge(s_r2[i], 16 * (u + (NSC + q // 2) // 2 + 1))
                if after(u, q, 4):
                    act.wait_ge(s_down, 2 * c - 2)
                nc.scalar.copy(w2[i][0][:], raw2[i][:]).then_inc(s_2hi, 1)

            def logits_out(h):
                act.wait_ge(s_logT, h + 1)
                nc.scalar.copy(lgT[:, h * HALF:(h + 1) * HALF], acc[0][h][0:E, :]).then_inc(s_lgT, 1)

            logits_out(0)
            for kc in range(KC):
                act.wait_ge(s_tr, kc + 1)
                nc.scalar.copy(xnT[0][:, kc, HALF:T], up[1][kc][:]).then_inc(s_xhi, 1)
            logits_out(1)
            act.wait_ge(s_log, 1)
            nc.scalar.activation(ex[:].rearrange("p t e -> p (t e)"), acc[1][0][:, 0:NT * E], ACT.Exp,
                                 scale=-1.0).then_inc(s_gexp, 1)

            def step(u, r):
                if r % 2 == 0:
                    if live(u, r):
                        high2(u, r)
                    if live(u, r + 2):
                        high13(u, r + 2)
                if isinstance(u, int) and u == 0 and r == 0:
                    for n in range(4):
                        h, g = n // 2, n % 2
                        act.wait_ge(s_cwt, n + 1)
                        nc.scalar.copy(CW[:, g, h * HALF:(h + 1) * HALF], up[h][g][:]).then_inc(s_cw, 1)
                if live(u, r):
                    act.wait_ge(s_up, 4 * u + N0 + r + 1)
                    if after(u, r, 2):
                        act.wait_ge(s_gated, 4 * u + N0 + r - 1)
                    nc.scalar.activation(sg[:, r % 2, :], up[r % 2][0][:], ACT.Silu).then_inc(s_silu, 1)
                q = r - 1
                if live(u, q):
                    if shared(u, q):
                        act.wait_ge(s_gated, 4 * u + N0 + q + 1)
                    else:
                        act.wait_ge(s_wtd, 4 * u + q + 1)
                    if after(u, q, 2):
                        act.wait_ge(s_down, 4 * u + N0 + q - 1)
                    src = hu if shared(u, q) else hw
                    nc.scalar.copy(H[q % 2][0][:], src[:, q % 2, :]).then_inc(s_hhi, 1)

            run_units(act, step, 1)
            for n in range(4):
                dc, h = n % 2, n // 2
                act.wait_ge(s_down, 2 * NC - 1 + h)
                nc.scalar.copy(yT[:, dc, h * HALF:(h + 1) * HALF], acc[dc][h][:]).then_inc(s_yT, 1)

        @block.vector
        def _(dve):
            routing_chain = Chain(dve, s_g)
            then = routing_chain.then
            norm_stats(nc, Chain(dve, s_stat), X, 1, st, mv, tmp, com.s_var, have=NT - 1)
            norm_apply(nc, Chain(dve, s_app), X, xn, 1, mv, tmp, com.s_pow, s_xn)
            for kc in range(KC):
                dve.wait_ge(s_xhi, kc + 1)
                nc.vector.tensor_tensor(xnT[1][:, kc, HALF:T], up[1][kc][:], as_f32(xnT[0][:, kc, HALF:T]),
                                        ALU.subtract).then_inc(s_xlo, 1)

            def choose_groups():
                dve.wait_ge(s_bias, 32)
                dve.wait_ge(s_gexp, 1)
                then(nc.vector.tensor_scalar(den[:], ex[:], 1.0, None, ALU.add))
                then(nc.vector.reciprocal(sc[:], den[:]))
                then(nc.vector.tensor_tensor(biased[:], sc[:], bc(bias[:], 1, NT), ALU.add))
                grouped = biased[:].rearrange("p t (g e) -> p t g e", g=GE)
                then(nc.vector.tensor_reduce(gm[:], grouped, AX.X, ALU.max))
                other, own = bc(gm[:], 2, GE), bc(gm[:], 3, GE)
                nc.vector.tensor_tensor(gbeat[:, 0], other, own, ALU.is_gt)
                then(nc.vector.tensor_tensor(gbeat[:, 1], other, own, ALU.is_equal))
                then(nc.vector.tensor_tensor(gbeat[:, 2], gbeat[:, 1], bc(lower[:, 0:GE, 0:GE], 1, NT), ALU.mult))
                then(nc.vector.tensor_tensor(gbeat[:, 1], gbeat[:, 0], gbeat[:, 2], ALU.add))
                then(nc.vector.tensor_reduce(gcnt[:], gbeat[:, 1], AX.X, ALU.add))
                then(nc.vector.tensor_scalar(gsel[:], gcnt[:], TOPG - 0.5, None, ALU.is_lt))
                nc.vector.tensor_scalar(goff[:], gsel[:], 1.0, -MASKED, ALU.subtract, ALU.mult)
                then(nc.vector.tensor_tensor(kept[:].rearrange("p t (g e) -> p t g e", g=GE), grouped,
                                             bc(gsel[:], 3, E // GE), ALU.mult))
                nc.vector.tensor_tensor(msk[:].rearrange("p t (g e) -> p t g e", g=GE),
                                        kept[:].rearrange("p t (g e) -> p t g e", g=GE),
                                        bc(goff[:], 3, E // GE), ALU.add).then_inc(s_masked, 1)

            def rank_experts():
                dve.wait_ge(s_masked, 1)
                other, own = bc(msk[:], 2, E), bc(msk[:], 3, E)
                nc.vector.tensor_tensor(tie[:], other, own, ALU.is_equal).then_inc(s_equal, 1)

            def rank_experts_2():
                other, own = bc(msk[:], 2, E), bc(msk[:], 3, E)
                then(nc.vector.tensor_tensor(beat[:], other, own, ALU.is_gt))

            def add_ties():
                dve.wait_ge(s_tie, 1)
                then(nc.vector.tensor_tensor(beat[:], beat[:], tie[:], ALU.add))

            def weights():
                then(nc.vector.tensor_reduce(cnt[:], beat[:], AX.X, ALU.add))
                then(nc.vector.tensor_scalar(sel[:], cnt[:], TOPK - 0.5, None, ALU.is_lt))
                then(nc.vector.tensor_tensor(picked[:], sc[:], sel[:], ALU.mult))
                then(nc.vector.tensor_reduce(wsum[:, 0, :], picked[:], AX.X, ALU.add))
                then(nc.vector.reciprocal(wsum[:, 1, :], wsum[:, 0, :]))
                then(nc.vector.tensor_tensor(cw[:], picked[:], bc(wsum[:, 1, :], 2, E), ALU.mult))
                nc.vector.tensor_copy(cwr[:].rearrange("p t g e i -> p (t g e) i"),
                                      bc(cw[:].rearrange("p t e -> p (t e)"), 2, UNIT)).then_inc(s_cwr, 1)

            def rank():
                rank_experts()
                rank_experts_2()

            def finish():
                add_ties()
                weights()

            routing = {-5: rank, -4: finish}
            choose_groups()

            def step(u, r):
                if live(u, r):
                    dve.wait_ge(s_silu, 4 * u + N0 + r + 1)
                    if shared(u, r):
                        if after(u, r, 2):
                            dve.wait_ge(s_hlo, 4 * u + N0 + r - 1)
                    elif not isinstance(u, int) or 4 * u + r >= 2:
                        dve.wait_ge(s_wtd, 4 * u + r - 1)
                    else:
                        dve.wait_ge(s_hlo, 4 * u + N0 + r - 1)
                    nc.vector.tensor_tensor(hu[:, r % 2, :], up[r % 2][1][:], sg[:, r % 2, :],
                                            ALU.mult).then_inc(s_gated, 1)
                q = r - 1
                if live(u, q):
                    dve.wait_ge(s_hhi, 4 * u + N0 + q + 1)
                    src = hu if shared(u, q) else hw
                    nc.vector.tensor_tensor(H[q % 2][1][:], src[:, q % 2, :], as_f32(H[q % 2][0][:]),
                                            ALU.subtract).then_inc(s_hlo, 1)
                if isinstance(u, int) and 4 * u + r in routing:
                    routing[4 * u + r]()

            run_units(dve, step, 1)
            for t in range(NT):
                dve.wait_ge(s_yt, t + 1)
                nc.vector.tensor_tensor(xn[:, t, :], up[(t // 2) % 2][t % 2][:, 0:D], X[:, t, :], ALU.add).then_inc(s_y, 1)

        @block.tensor
        def _(pe):
            def logits(h):
                for kc in range(KC):
                    last = split3(nc.tensor, acc[0][h][0:E, :], gw, xnT, (slice(None), kc),
                                  (slice(None), kc, slice(h * HALF, (h + 1) * HALF)), kc == 0, kc == KC - 1)
                last.then_inc(s_logT, 1)

            def second_half():
                for kc in range(KC):
                    for q in range(4):
                        pe.wait_ge(s_xn, q + 1)
                        last = nc.tensor.transpose(up[1][kc][:, q * P:(q + 1) * P],
                                                   xn[:, NT // 2 + q, kc * P:(kc + 1) * P], ident[:])
                    last.then_inc(s_tr, 1)
                pe.wait_ge(s_xlo, 2)
                logits(1)
                pe.wait_ge(s_lgT, 2)
                for t in range(NT):
                    last = nc.tensor.transpose(acc[1][0][:, t * E:(t + 1) * E], lgT[:, t * P:(t + 1) * P],
                                               ident[0:E, 0:E])
                last.then_inc(s_log, 1)

            logits(0)

            def step(u, r):
                if isinstance(u, int) and 4 * u + r == 1 - N0:
                    second_half()
                if isinstance(u, int) and u == 0 and r == 0:
                    pe.wait_ge(s_cwr, 1)
                    pe.wait_ge(s_gated, N0)
                    for n in range(4):
                        h, g = n // 2, n % 2
                        for x in range(4):
                            last = nc.tensor.transpose(up[h][g][:, x * P:(x + 1) * P],
                                                       cwr[:, 4 * h + x, g, :, :].rearrange("p e i -> p (e i)"), ident[:])
                        last.then_inc(s_cwt, 1)
                    pe.wait_ge(s_cw, 4)
                if live(u, r):
                    w = [x[:].rearrange("p (a k m) -> p a k m", a=2, k=KC) for x in w13[place(r)]]
                    c, h = 2 * u + NSC + r // 2, r % 2
                    if h == 0:
                        pe.wait_ge(s_13lo, c + 1)
                    if after(u, r, 2):
                        pe.wait_ge(s_gated, 4 * u + N0 + r - 1)
                    for m in range(2):
                        for kc in range(KC):
                            last = split3(nc.tensor, up[r % 2][m][:], w, xnT, (slice(None), m, kc),
                                          (slice(None), kc, slice(h * HALF, (h + 1) * HALF)), kc == 0, kc == KC - 1)
                    last.then_inc(s_up, 1)
                q = r - LAG
                if live(u, q):
                    c, h = 2 * u + NSC + q // 2, q % 2
                    if h == 0:
                        pe.wait_ge(s_2lo, c + 1)
                        if isinstance(u, int) and 4 * u + q == -N0:
                            pe.wait_ge(s_gexp, 1)
                    pe.wait_ge(s_hlo, 4 * u + N0 + q + 1)
                    first = isinstance(u, int) and 4 * u + N0 + q < 2
                    end = isinstance(u, int) and 4 * u + N0 + q >= 2 * NC - 2
                    for dc in range(KC):
                        last = split3(nc.tensor, acc[dc][h][:], w2[place(q)], H[q % 2],
                                      (slice(None), slice(dc * P, (dc + 1) * P)), (slice(None),), first, end)
                    last.then_inc(s_down, 1)

            run_units(pe, step, LAG)
            for t in range(NT):
                pe.wait_ge(s_yT, 2 * (t // 4) + 2)
                if t >= 4:
                    pe.wait_ge(s_y, t - 3)
                for dc in range(KC):
                    last = nc.tensor.transpose(up[(t // 2) % 2][t % 2][:, dc * P:(dc + 1) * P],
                                               yT[:, dc, t * P:(t + 1) * P], ident[:])
                last.then_inc(s_yt, 1)


def decoder_layer(nc, d, out):
    with ExitStack() as ctx:
        k = Kit(nc, ctx)
        X = k.sb("x", [P, NT, D])
        ident = k.sb("ident", [P, P])
        com = Common(k)
        x_d = d["x"].rearrange("(t p) c -> p t c", p=P)
        out_d = out.rearrange("(t p) c -> p t c", p=P)
        with ExitStack() as c1:
            k1 = Kit(nc, c1)
            QR = k1.sb("q_rotated", [P, 2, NT, 2 * 2 * G * SEQ])
            KR = k1.sb("k_rotated", [P, 2, NT, 2, P])
            V = k1.sb("v", [P, NT, HKV * HD])
            Q = [k1.sb(f"q_tile{i}", [P, 4 * HALF]) for i in range(2)]
            KV = [k1.sb(f"kv_blocks{i}", [P, 4 * HALF]) for i in range(2)]
            KB = [x[:, 0:2 * HALF].rearrange("p (a s b n) -> p a s b n", a=2, s=2, b=2) for x in KV]
            VB = [x[:, 2 * HALF:4 * HALF].rearrange("p (b g n) -> p b g n", b=2, g=4) for x in KV]
            staged = (Q, KV, KB, VB)
            s_qk = [k1.sem(f"qk_staged{i}") for i in range(2)]
            s_vb = [k1.sem(f"v_staged{i}") for i in range(2)]
            mask = k1.sb("mask", [P, 4, P], BF16)
            ident_b = k1.sb("ident_b", [P, P], BF16)
            qkv_phase(nc, com, X, QR, KR, V, ident, staged, s_qk, s_vb, mask, ident_b, x_d, d["wqk"], d["wv"], d["wo"],
                      d["cos_sin"], d["ident"], d["mask"])
            attention_phase(nc, com, X, QR, KR, V, ident, staged, s_qk, s_vb, mask, ident_b,
                            d["ctx"].rearrange("(t p) c -> p t c", p=P), d["wx"], d["gate"], d["wch"])
        expert_phase(nc, com, X, ident, d, out_d)



def layout(x, ctx_2048, L0_attn_Wq, L0_attn_Wk, L0_attn_Wv, L0_attn_Wo, L0_xattn_W_q, L0_xattn_W_k,
           L0_xattn_W_v, L0_xattn_W_o, L0_ffn_gate_w, L0_ffn_expert_bias, L0_ffn_w1, L0_ffn_w2, L0_ffn_w3,
           L0_ffn_sw1, L0_ffn_sw2, L0_ffn_sw3):
    a = np.ascontiguousarray
    f4 = np.float32

    def pairs(w, heads):
        w = np.asarray(w).reshape(2, 4, heads, F, 2, KC, P)
        return w.transpose(0, 2, 6, 5, 4, 1, 3).reshape(2 * heads, P, KC * 2 * P)

    wqk = np.concatenate([pairs(L0_attn_Wk, 1), pairs(L0_attn_Wq, G)], 0)
    wv = np.asarray(L0_attn_Wv).reshape(HKV * HD, KC, P).transpose(2, 1, 0)
    wo = np.asarray(L0_attn_Wo).reshape(D, 2, 2, 2, G, HD).transpose(3, 5, 2, 1, 4, 0)
    wo = wo.reshape(P, NT, HKV * HD)
    inv = (f4(1.0) / f4(10000.0) ** (np.arange(0, HD, 2, dtype=f4) / f4(HD))).astype(f4)
    ang = (np.arange(SEQ, dtype=f4)[None, :] * inv[:, None]).astype(f4)
    cs = np.stack([np.cos(ang), np.sin(ang)], 1).astype(f4)
    cs = np.tile(cs, (4, 1, 1))
    q, kk = np.arange(P)[:, None] % SEQ, np.arange(P)[None, :] % SEQ
    mask = np.where(q >= kk, 0.0, MASKED).astype(f4)
    wx = np.zeros((P, 4, P), f4)
    for n, w in enumerate((L0_xattn_W_q, L0_xattn_W_k, L0_xattn_W_v, L0_xattn_W_o)):
        for b in range(2):
            wx[b * SEQ:(b + 1) * SEQ, n, b * SEQ:(b + 1) * SEQ] = np.asarray(w).T
    def up_chunks(shared, routed):
        sh = np.zeros((D, NSC * P), f4)
        sh[:, 0:SH] = np.asarray(shared)
        sh = sh.reshape(KC, P, NSC, P).transpose(2, 1, 0, 3)
        ro = np.asarray(routed).reshape(2, EG, KC, P, NU, UNIT).transpose(4, 0, 3, 2, 1, 5)
        return np.concatenate([sh, ro.reshape(NEC, P, KC, P)], 0)

    sh2 = np.zeros((NSC * P, D), f4)
    sh2[0:SH] = np.asarray(L0_ffn_sw2)
    ro2 = np.asarray(L0_ffn_w2).reshape(2, EG, NU, UNIT, D).transpose(2, 0, 1, 3, 4).reshape(NEC, P, D)
    w2 = np.concatenate([sh2.reshape(NSC, P, D), ro2], 0)
    w13 = np.stack([up_chunks(L0_ffn_sw1, L0_ffn_w1), up_chunks(L0_ffn_sw3, L0_ffn_w3)], 2)
    wch = np.concatenate([w13.reshape(NC, P, 2 * D), w2], 2)
    gate = np.asarray(L0_ffn_gate_w).reshape(E, KC, P).transpose(2, 1, 0)
    lower = (np.arange(E)[None, :] < np.arange(E)[:, None]).astype(f4)
    return {
        "wch": a(wch), "gate": a(gate), "bias": a(np.asarray(L0_ffn_expert_bias)), "lower": lower,
        "ctx": a(np.asarray(ctx_2048).reshape(T, D)), "wx": wx,
        "x": a(np.asarray(x).reshape(T, D)), "wqk": a(wqk), "wv": a(wv), "wo": a(wo),
        "cos_sin": a(cs), "mask": a(mask), "ident": np.eye(P, dtype=f4),
    }


def kernel(**inputs):
    import concourse.bacc as _bacc
    from concourse.bass_utils import run_bass_kernel_spmd as _run

    nc = _bacc.Bacc("TRN2", target_bir_lowering=False, num_devices=1)
    arrays = {f"in_{n}": v for n, v in layout(**inputs).items()}
    d = {n[3:]: nc.dram_tensor(n, v.shape, mybir.dt.from_np(v.dtype), kind="ExternalInput").ap()
         for n, v in arrays.items()}
    out = nc.dram_tensor("out", (T, D), F32, kind="ExternalOutput").ap()
    decoder_layer(nc, d, out)
    r = _run(nc, [arrays], core_ids=[0])
    return r.results[0]["out"].reshape(B, SEQ, D)
```

```python
from contextlib import ExitStack

import numpy as np

import concourse.bass as bass
from concourse import mybir

F32 = mybir.dt.float32
F32R = mybir.dt.float32r
BF16 = mybir.dt.bfloat16
ALU = mybir.AluOpType
ACT = mybir.ActivationFunctionType
AX = mybir.AxisListType

P = 128
B, SEQ, D = 16, 64, 256
T = B * SEQ
NT = T // P
KC = D // P
HALF = 512
NHALF = T // HALF
EPS = 1e-5

HQ, HKV, HD = 32, 8, 64
G = HQ // HKV
F = HD // 2
SCALE = float(HD) ** -0.5
NPAIR = 2 * G + 2
MASKED = -1e30

XH = 8
XN = D // XH
XSCALE = float(XN) ** -0.5

E = 16
INTER = 176
GE = 4
TOPK, TOPG = 4, 2
EG = 8
UNIT = P // EG
NU = INTER // UNIT
NEC = (E // EG) * NU
SH = 2 * INTER
NSC = (SH + P - 1) // P
NC = NEC + NSC


def as_f32(ap):
    return ap.bitcast(F32)


def bc(ap, axis, n):
    a = ap.unsqueeze(axis)
    shape = list(a.shape)
    shape[axis] = n
    return a.broadcast_to(shape)


class Steps:

    def __init__(self, total, lag, head):
        self.total, self.lag, self.head = total, lag, head

    def run(self, eng, step):
        for k in range(8 * self.head):
            step(k // 8, k % 8)
        with eng.Fori(self.head, self.total // 8) as i:
            for r in range(8):
                step(i, r)
        for k in range(self.total, self.total + self.lag):
            step(k // 8, k % 8)

    def live(self, i, q):
        return not isinstance(i, int) or 0 <= 8 * i + q < self.total

    def later(self, i, q, n):
        return not isinstance(i, int) or 8 * i + q >= n


class Kit:

    def __init__(self, nc, ctx):
        self.nc, self.ctx = nc, ctx

    def sb(self, name, shape, dt=F32):
        return self.ctx.enter_context(self.nc.sbuf_tensor(name, shape, dt))

    def bank(self, name, n=1):
        shape = [P, HALF] if n == 1 else [P, n, HALF]
        return self.ctx.enter_context(self.nc.psum_tensor(name, shape, F32))

    def sem(self, name):
        return self.ctx.enter_context(self.nc.semaphore(name))


def split3(pe, out, w, x, w_sl, x_sl, first, last):
    pe.matmul(out, w[0][w_sl], x[0][x_sl], start=first, stop=False)
    pe.matmul(out, w[0][w_sl], x[1][x_sl], start=False, stop=False)
    return pe.matmul(out, w[1][w_sl], x[0][x_sl], start=False, stop=last)


class Common:

    def __init__(self, k):
        self.WO = [k.sb(f"wo_{n}", [P, 16, D], F32R) for n in ("hi", "lo")]
        flat = [x[:].rearrange("p c n -> p (c n)") for x in self.WO]
        a, b = KC * T, KC * T + 2 * D
        self.xnT = [x[:, 0:a].rearrange("p (k t) -> p k t", k=KC) for x in flat]
        self.w13 = [x[:, a:b] for x in flat]
        self.gw = [x[:, b:b + KC * E].rearrange("p (k e) -> p k e", k=KC) for x in flat]
        self.groups = [range(0, 4), range(4, 6)]
        self.mhalf = k.sb("minus_half", [P, NT // 2])
        self.st = k.sb("f_stats", [P, NT, 6])
        self.mv = k.sb("f_mean_var", [P, NT, 2])
        self.tmp = k.sb("f_norm_tmp", [P, 6, NT])
        self.s_var = k.sem("f_var")
        self.s_pow = k.sem("f_pow")
        self.s_r13 = k.sem("f_raw13_0")
        self.s_13hi = k.sem("f_w13_hi")
        self.s_13lo = k.sem("f_w13_lo")


class Chain:

    def __init__(self, eng, sem):
        self.eng, self.sem, self.n = eng, sem, 0

    def then(self, ins):
        ins.then_inc(self.sem, 1)
        self.n += 1
        self.eng.wait_ge(self.sem, self.n)


def norm_stats(nc, chain, X, tiles, st, mv, tmp, s_var, s_x=None):
    for t in tiles:
        if s_x and t % 2 == 0:
            chain.eng.wait_ge(s_x[t // 2], 16)
        last = nc.vector.bn_stats(st[:, t, :], X[:, t, :])
    chain.then(last)
    for t in tiles:
        last = nc.vector.bn_aggr(mv[:, t, :], st[:, t, :])
    chain.then(last)
    nc.vector.tensor_scalar(tmp[:, 0, tiles.start:tiles.stop], mv[:, tiles.start:tiles.stop, 1], EPS, None,
                            ALU.add).then_inc(s_var, 1)


def norm_power(nc, pool, tiles, n, mhalf, tmp, s_var, s_pow):
    part = slice(tiles.start, tiles.stop)
    pool.wait_ge(s_var, n + 1)
    nc.gpsimd.tensor_tensor(tmp[:, 1, part], tmp[:, 0, part], mhalf[:, 0:len(tiles)], ALU.pow).then_inc(s_pow, 1)


def norm_apply(nc, chain, X, xn, tiles, n, mv, tmp, s_pow, s_xn):
    part = slice(tiles.start, tiles.stop)
    v, r, a, b, c, rstd = (tmp[:, j, part] for j in range(6))
    chain.eng.wait_ge(s_pow, n + 1)
    chain.then(nc.vector.tensor_tensor(a, r, r, ALU.mult))
    chain.then(nc.vector.tensor_tensor(b, a, v, ALU.mult))
    chain.then(nc.vector.tensor_scalar(c, b, -0.5, 1.5, ALU.mult, ALU.add))
    chain.then(nc.vector.tensor_tensor(rstd, r, c, ALU.mult))
    for q, t in enumerate(tiles):
        nc.vector.tensor_scalar(xn[:, q, :], X[:, t, :], mv[:, t, 0:1], tmp[:, 5, t:t + 1],
                                ALU.subtract, ALU.mult).then_inc(s_xn, 1)


N_Q, N_K, N_V = 8, 8, 4


def stage_q(sp, QR, Q, t, sem):
    for gl in range(2):
        for a in range(2):
            for g2 in range(2):
                src = slice((2 * gl + g2) * F, (2 * gl + g2 + 1) * F)
                dst = slice(g2 * HD + a * F, g2 * HD + (a + 1) * F)
                sp.dma_start(Q[dst, gl, :], QR[src, a, bass.ds(t, 1), :].rearrange("p o n -> p (o n)")
                             ).then_inc(sem, 16)


def stage_k(sp, KR, KB, t, sem):
    for gl in range(2):
        for a in range(2):
            for g2 in range(2):
                src = slice((2 * gl + g2) * F, (2 * gl + g2 + 1) * F)
                dst = slice(g2 * HD + a * F, g2 * HD + (a + 1) * F)
                sp.dma_start(
                    KB[dst, gl, :, :, g2 * HD:(g2 + 1) * HD].rearrange("p s b t -> p (s b) t"),
                    KR[src, a, bass.ds(t, 1), :, :].rearrange("p o s (b t) -> p (o s b) t", b=2),
                ).then_inc(sem, 16)


def stage_v(sp, V, VB, t, sem):
    for b in range(2):
        for g2 in range(2):
            sp.dma_start(
                VB[g2 * HD:(g2 + 1) * HD, b, :, g2 * HD:(g2 + 1) * HD],
                V[b * SEQ:(b + 1) * SEQ, bass.ds(t, 1), :].rearrange(
                    "p o (gp g d) -> p (o gp) g d", gp=4, g=2)[:, :, g2, :],
            ).then_inc(sem, 16)


def qkv_phase(nc, com, X, QR, KR, V, ident, staged, s_qk, s_vb, mask, ident_b,
              x_d, wqk_d, wv_d, wo_d, cs_d, ident_d, mask_d):
    NW = NPAIR + KC
    NWO = 16 * D // HALF
    WO_LOADS = 2
    assert NWO == NT and HKV * HD == HALF
    with ExitStack() as ctx:
        k = Kit(nc, ctx)
        raw = [k.sb(f"w_raw{i}", [P, HALF]) for i in range(2)]
        w = [[k.sb(f"w_{n}{i}", [P, HALF], F32R) for n in ("hi", "lo")] for i in range(3)]
        xnT = [k.sb(f"xnT_{n}", [P, KC, T], F32R) for n in ("hi", "lo")]
        WO, mhalf = com.WO, com.mhalf
        halves = [range(0, NT // 2), range(NT // 2, NT)]
        Q, k_mem, v_mem, KB, VB = staged
        prod_mem = k.sb("rope_products", [P, 2 * HALF])
        prod = [[x.rearrange("p (n m) -> p n m", n=2) for x in y] for y in
                ((Q[1][:, 0:2 * HALF], Q[1][:, 2 * HALF:4 * HALF]), (v_mem[1][:], prod_mem[:]))]
        xn = Q[1][:].rearrange("p (t d) -> p t d", t=NT)
        cs = k.sb("cos_sin", [P, 2, SEQ])
        mask_f = k.sb("mask_f", [P, P])
        st = k.sb("stats", [P, NT, 6])
        mv = k.sb("mean_var", [P, NT, 2])
        tmp = k.sb("norm_tmp", [P, 6, NT])
        ps_t = k.bank("ps_transposed", 4)
        ps_v = [k.bank(f"ps_v{i}") for i in range(2)]
        proj = [ps_t[:, 2 * i:2 * i + 2, :] for i in range(2)]

        s_x = [k.sem(f"p1_x{i}") for i in range(4)]
        s_const = k.sem("p1_const")
        s_raw = [k.sem(f"p1_raw{i}") for i in range(2)]
        s_raw_o = [k.sem(f"p1_raw_o{i}") for i in range(WO_LOADS)]
        s_hi = k.sem("p1_w_hi")
        s_lo = k.sem("p1_w_lo")
        s_hi_o = k.sem("p1_wo_hi")
        s_lo_o = k.sem("p1_wo_lo")
        s_stat = k.sem("p1_stat")
        s_var = k.sem("p1_var")
        s_pow = k.sem("p1_pow")
        s_xn = k.sem("p1_xn")
        s_tr = k.sem("p1_transposed")
        s_xhi = k.sem("p1_xnT_hi")
        s_xlo = k.sem("p1_xnT_lo")
        s_vps = k.sem("p1_v_psum")
        s_vsb = k.sem("p1_v_copied")
        s_proj = k.sem("p1_projected")
        s_prod = k.sem("p1_products")
        s_rot = k.sem("p1_rotated")
        s_mask = k.sem("p1_mask")
        s_zero = k.sem("p1_zero")
        s_half = k.sem("p1_half")
        block = ctx.enter_context(nc.Block())

        def wo_dst(c):
            return [o[:, 2 * c:2 * c + 2, :].rearrange("p c n -> p (c n)") for o in WO]

        @block.sync
        def _(sp):
            for q in range(4):
                sp.dma_start(X[:, 2 * q:2 * q + 2, :], x_d[:, 2 * q:2 * q + 2, :]).then_inc(s_x[q], 16)
            sp.dma_start(ident[:], ident_d).then_inc(s_const, 16)
            for c in range(2):
                sp.dma_start(raw[c][:], wqk_d[c]).then_inc(s_raw[c], 16)
            sp.dma_start(cs[:], cs_d).then_inc(s_const, 16)
            for c in range(2, NW):
                sp.wait_ge(s_lo, c - 1)
                sp.dma_start(raw[c % 2][:], wqk_d[c] if c < NPAIR else wv_d[:, c - NPAIR, :]
                             ).then_inc(s_raw[c % 2], 16)
                if 3 <= c < 3 + WO_LOADS:
                    n = NWO // WO_LOADS
                    part = slice((c - 3) * n, (c - 2) * n)
                    sp.dma_start(V[:, part, :], wo_d[:, part, :]).then_inc(s_raw_o[c - 3], 16)
                if c in (6, 8):
                    t = (c - 6) // 2
                    sp.wait_ge(s_zero, 3)
                    sp.wait_ge(s_rot, 4)
                    stage_k(sp, KR, KB[t], t, s_qk[t])
            sp.dma_start(mask_f[:], mask_d).then_inc(s_mask, 16)
            sp.wait_ge(s_rot, 2 * NPAIR)
            stage_q(sp, QR, Q[0][:].rearrange("p (a n) -> p a n", a=2), 0, s_qk[0])
            sp.wait_ge(s_vsb, 1)
            stage_v(sp, V, VB[0], 0, s_vb[0])

        @block.gpsimd
        def _(pool):
            nc.gpsimd.memset(mhalf[:], -0.5).then_inc(s_half, 1)
            pool.wait_ge(s_half, 1)
            for h in range(2):
                norm_power(nc, pool, halves[h], h, mhalf, tmp, s_var, s_pow)
            for x in (k_mem[0], k_mem[1], v_mem[0]):
                nc.gpsimd.memset(x[:], 0.0).then_inc(s_zero, 1)
            for m in range(NPAIR):
                for h in range(2):
                    pool.wait_ge(s_prod, 2 * m + h + 1)
                    first, second = prod[h]
                    pr = [first[:, 0], first[:, 1], second[:, 0], second[:, 1]]
                    if m >= 2:
                        dst = [QR[:, a, 4 * h:4 * h + 4, :].rearrange(
                            "p t (b m s) -> p (t b) m s", b=2, s=SEQ)[:, :, m - 2, :] for a in range(2)]
                        pr = [x.rearrange("p (t s) -> p t s", s=SEQ) for x in pr]
                    else:
                        dst = [KR[:, a, 4 * h:4 * h + 4, m, :] for a in range(2)]
                        pr = [x.rearrange("p (t c) -> p t c", c=P) for x in pr]
                    nc.gpsimd.tensor_tensor(dst[0], pr[0], pr[3], ALU.subtract)
                    nc.gpsimd.tensor_tensor(dst[1], pr[1], pr[2], ALU.add).then_inc(s_rot, 1)
            pool.wait_ge(s_rot, 2 * NPAIR)
            nc.gpsimd.memset(v_mem[1][:], 0.0)

        @block.scalar
        def _(act):
            def high_half(c):
                act.wait_ge(s_raw[c % 2], 16 * (c // 2 + 1))
                nc.scalar.copy(w[2 if c == NW - 1 else c % 2][0][:], raw[c % 2][:]).then_inc(s_hi, 1)

            def high_half_o(c):
                hi, _ = wo_dst(c)
                act.wait_ge(s_raw_o[c * WO_LOADS // NWO], 16)
                nc.scalar.copy(hi, V[:, c, :]).then_inc(s_hi_o, 1)

            high_half(0)
            high_half(1)
            for n in range(KC * NHALF):
                kc, h = n % KC, n // KC
                act.wait_ge(s_tr, n + 1)
                nc.scalar.copy(xnT[0][:, kc, h * HALF:(h + 1) * HALF], ps_t[:, n, :]).then_inc(s_xhi, 1)
            for c in range(2, NW):
                if c < NW - 1:
                    act.wait_ge(s_proj, 4 * (c - 1))
                high_half(c)
                if 4 <= c < NW:
                    high_half_o(c - 4)
            for t in range(NT):
                act.wait_ge(s_vps, t + 1)
                act.wait_ge(s_lo_o, t + 1)
                nc.scalar.copy(V[:, t, :], ps_v[t % 2][:]).then_inc(s_vsb, 1)

        @block.vector
        def _(dve):
            def low_half(i, r, n):
                dve.wait_ge(s_hi, 2 * i + r + 1)
                nc.vector.tensor_tensor(w[n][1][:], raw[r % 2][:], as_f32(w[n][0][:]),
                                        ALU.subtract).then_inc(s_lo, 1)

            chain = Chain(dve, s_stat)
            for h in range(2):
                norm_stats(nc, chain, X, halves[h], st, mv, tmp, s_var, s_x)
            norm_apply(nc, chain, X, xn, halves[0], 0, mv, tmp, s_pow, s_xn)
            low_half(0, 0, 0)
            norm_apply(nc, chain, X, xn[:, NT // 2:NT], halves[1], 1, mv, tmp, s_pow, s_xn)
            for n in range(KC * NHALF):
                kc, h = n % KC, n // KC
                tok = slice(h * HALF, (h + 1) * HALF)
                dve.wait_ge(s_xhi, n + 1)
                nc.vector.tensor_tensor(xnT[1][:, kc, tok], ps_t[:, n, :], as_f32(xnT[0][:, kc, tok]),
                                        ALU.subtract).then_inc(s_xlo, 1)
            low_half(0, 1, 1)
            dve.wait_ge(s_const, 32)

            def products(i, r):
                ps, pr = proj[r % 2], prod[r % 2]
                if not isinstance(i, int) or i > 0 or r >= 2:
                    dve.wait_ge(s_rot, 4 * i + r - 1)
                for a in range(2):
                    dve.wait_ge(s_proj, 8 * i + 2 * r + a + 1)
                    last = nc.vector.tensor_tensor(
                        pr[a].rearrange("p m (b s) -> p m b s", s=SEQ),
                        bc(ps[:, a, :].rearrange("p (b s) -> p b s", s=SEQ), 1, 2),
                        bc(cs[:], 2, HALF // SEQ), ALU.mult)
                last.then_inc(s_prod, 1)

            def two_pairs(i, end=False):
                for r in range(4):
                    products(i, r)
                    if r % 2 and not end:
                        low_half(i, 2 + r // 2, r // 2)
                    if r == 1 and end:
                        low_half(i, 2, 0)
                        low_half(i, 3, 2)

            two_pairs(0)
            with dve.Fori(1, NPAIR // 2 - 1) as i:
                two_pairs(i)
            two_pairs(NPAIR // 2 - 1, end=True)
            dve.wait_ge(s_mask, 16)
            nc.vector.tensor_copy(mask[:], bc(mask_f[:], 1, 4))
            nc.vector.tensor_copy(ident_b[:], ident[:])
            for c in range(NWO):
                hi, lo = wo_dst(c)
                dve.wait_ge(s_hi_o, c + 1)
                nc.vector.tensor_tensor(lo, V[:, c, :], as_f32(hi), ALU.subtract).then_inc(s_lo_o, 1)

        @block.tensor
        def _(pe):
            pe.wait_ge(s_const, 32)
            for h in range(NHALF):
                for kc in range(KC):
                    for q in range(4):
                        t = 4 * h + q
                        pe.wait_ge(s_xn, t + 1)
                        last = nc.tensor.transpose(ps_t[:, 2 * h + kc, q * P:(q + 1) * P],
                                                   xn[:, t, kc * P:(kc + 1) * P], ident[:])
                    last.then_inc(s_tr, 1)

            def project(i, r):
                h = r % 2
                wv = [x[:].rearrange("p (k a m) -> p k a m", k=KC, a=2) for x in w[r // 2]]
                if h == 0:
                    pe.wait_ge(s_lo, 2 * i + r // 2 + 1)
                if isinstance(i, int) and r < 2:
                    pe.wait_ge(s_xlo, 2 * r + 2)
                else:
                    pe.wait_ge(s_prod, 4 * i + r - 1)
                for a in range(2):
                    for kc in range(KC):
                        last = split3(nc.tensor, proj[r % 2][:, a, :], wv, xnT, (slice(None), kc, a),
                                      (slice(None), kc, slice(h * HALF, (h + 1) * HALF)), kc == 0, kc == KC - 1)
                    last.then_inc(s_proj, 1)

            for r in range(4):
                project(0, r)
            with pe.Fori(1, NPAIR // 2) as i:
                for r in range(4):
                    project(i, r)
            pe.wait_ge(s_lo, NW)
            for t in range(NT):
                if t >= 2:
                    pe.wait_ge(s_vsb, t - 1)
                for kc in range(KC):
                    last = split3(nc.tensor, ps_v[t % 2][:], xnT, w[2 * kc], (slice(None), kc, slice(t * P, (t + 1) * P)),
                                  (slice(None),), kc == 0, kc == KC - 1)
                last.then_inc(s_vps, 1)


def attention_phase(nc, com, X, QR, KR, V, ident, staged, s_qk, s_vb, mask, ident_b, ctx_d, wx_d,
                    gate_d, wch_d):
    NUN = 4 * NT
    S_T, S_PV, S_LO, S_Y, S_ADD = 2, 3, 4, 5, 6
    X_MEAN, X_VAR, X_KV, X_NORM, X_Q, X_S, X_SUM, X_T, X_PV, X_DIFF, X_ADD = 10, 11, 11, 12, 13, 14, 15, 16, 17, 18, 19
    steps = Steps(NUN, X_ADD - 3, 2)
    with ExitStack() as ctx:
        k = Kit(nc, ctx)
        Q, _, _, KB, VB = staged
        Q = [x[:].rearrange("p (a n) -> p a n", a=2) for x in Q]
        EX = k.sb("probabilities", [P, 4, 4, P])
        PT = k.sb("probs_T", [P, 2, 2, 2 * P])
        OT = [[k.sb(f"out_T_{n}{i}", [P, 2 * G, P], F32R) for n in ("hi", "lo")] for i in range(2)]
        mx = k.sb("row_max", [P, 2, 8])
        sm = k.sb("row_sum", [P, 2, 8])
        ri = k.sb("row_inv", [P, 4, 8])
        WX = k.sb("wx", [P, 4, P])
        XQ = k.sb("xq", [P, 2, D])
        rs = k.sb("xrstd", [P, 9])
        xmx = k.sb("xrow_max", [P, XH])
        xsm = k.sb("xrow_sum", [P, XH])
        xri = k.sb("xrow_inv", [P, XH])
        kbx = QR[:, 0, 0, :].rearrange("p (c b h s) -> p c b h s", c=2, b=2, h=4)
        vbx = QR[:, 0, 1, :].rearrange("p (r h b g n) -> p r h b g n", r=2, h=4, b=2, g=2)
        C = QR[:, 1, 0, 0:2 * D].rearrange("p (r d) -> p r d", r=2)
        DF = QR[:, 1, 0, 2 * D:3 * D]
        XC = KR[:, 1, 0, :, :].rearrange("p s c -> p (s c)")
        SQ = KR[:, 0, 0, :, :].rearrange("p s c -> p (s c)")
        QT = QR[:, 1, 0, 3 * D:4 * D].rearrange("p (c m) -> p c m", c=2)
        XE = QR[:, 1, 1, 0:HALF].rearrange("p (h s) -> p h s", h=XH)
        XPT = QR[:, 1, 1, HALF:2 * HALF].rearrange("p (h m) -> p h m", h=4)
        WO = com.WO
        XN3 = [QR[:, 0, 2, :].rearrange("p (t d) -> p t d", d=D),
               QR[:, 0, 3, 2 * D:4 * D].rearrange("p (t d) -> p t d", d=D)]
        raw13 = QR[:, 0, 3, 0:2 * D]
        gate = QR[:, 1, 3, 0:KC * E].rearrange("p (k e) -> p k e", k=KC)
        ps_s = [k.bank(f"ps_scores{i}") for i in range(2)]
        ps_p = k.bank("ps_probsT")
        ps_o = k.bank("ps_outT")
        ps_y = k.bank("ps_y")
        ps_xq = k.bank("ps_x_queries")
        ps_xs = k.bank("ps_x_scores")
        ps_xo = k.bank("ps_x_out")

        s_scores = k.sem("p2_scores")
        s_max = k.sem("p2_max")
        s_shift = k.sem("p2_shifted")
        s_exp = k.sem("p2_exp")
        s_sum = k.sem("p2_sum")
        s_inv = k.sem("p2_inverse")
        s_norm = k.sem("p2_normalised")
        s_pT = k.sem("p2_probs_transposed")
        s_pTc = k.sem("p2_probsT_copied")
        s_pv = k.sem("p2_values_mixed")
        s_ohi = k.sem("p2_outT_hi")
        s_olo = k.sem("p2_outT_lo")
        s_y = k.sem("p2_out_projected")
        s_res = k.sem("p2_residual")
        x_w = k.sem("x_weights")
        x_c = [k.sem(f"x_context{i}") for i in range(2)]
        x_zero = k.sem("x_zero")
        x_kv = k.sem("x_keys_values")
        x_k = k.sem("x_keys_copied")
        x_v = k.sem("x_values_copied")
        x_stat = k.sem("x_stat")
        x_tok = k.sem("x_tokens")
        x_mean = k.sem("x_mean")
        x_sq = k.sem("x_squares")
        x_var = k.sem("x_var")
        x_pow = k.sem("x_pow")
        x_norm = k.sem("x_normed")
        x_q = k.sem("x_queries")
        x_qc = k.sem("x_queries_copied")
        x_scores = k.sem("x_scores")
        x_max = k.sem("x_max")
        x_shift = k.sem("x_shifted")
        x_exp = k.sem("x_exp")
        x_sum = k.sem("x_sum")
        x_inv = k.sem("x_inverse")
        x_prob = k.sem("x_normalised")
        x_pT = k.sem("x_probs_transposed")
        x_pTc = k.sem("x_probsT_copied")
        x_pv = k.sem("x_values_mixed")
        x_diff = k.sem("x_diff")
        x_y = k.sem("x_projected")
        x_res = k.sem("x_residual")
        f_gate = k.sem("f_gate")
        f_ghi = k.sem("f_gate_hi")
        f_stat = k.sem("f_stat")
        f_xn = k.sem("f_normed")
        f_tr = k.sem("f_transposed")
        f_xhi = k.sem("f_xnT_hi")
        block = ctx.enter_context(nc.Block())

        N_STAT, N_POW, N_APPLY, N_TR, N_HI, N_LO = (33, 40), (34, 41), (35, 44), (36, 44), (37, 45), (41, 46)
        assert all(N_STAT[g] > 4 * (tiles.stop - 1) + X_ADD for g, tiles in enumerate(com.groups))

        def transposed(g, tiles):
            n = len(tiles) * P
            places = ((ps_s[0], 0), (ps_s[1], 0)) if g == 0 else ((ps_p, 0), (ps_p, n))
            banks = [x[:, a:a + n] for x, a in places]
            tok = slice(tiles.start * P, tiles.stop * P)
            return [(banks[kc], [x[:, kc, tok] for x in com.xnT]) for kc in range(KC)]

        def at(i, r, k_):
            return isinstance(i, int) and 8 * i + r == k_

        def cross(i, r, distance):
            n, rest = divmod(r - distance, 4)
            if rest or (isinstance(i, int) and not 0 <= 2 * i + n < NT):
                return None
            return n

        @block.sync
        def _(sp):
            stage_q(sp, QR, Q[1], 1, s_qk[1])
            stage_v(sp, V, VB[1], 1, s_vb[1])
            sp.dma_start(WX[:], wx_d).then_inc(x_w, 16)

            def context(t, r, n):
                if not isinstance(n, int) or n:
                    sp.wait_ge(x_kv, n)
                sp.dma_start(C[:, r, :], ctx_d[:, bass.ds(t, 1), :].rearrange("p o d -> p (o d)")
                             ).then_inc(x_c[r], 16)

            def two_tiles(i):
                for r in range(2):
                    sp.wait_ge(s_scores, 8 * i + 4 * r - 4)
                    stage_q(sp, QR, Q[r], 2 * i + r, s_qk[r])
                    stage_k(sp, KR, KB[r], 2 * i + r, s_qk[r])
                    context(2 * i + r - 2, r, 0 if isinstance(i, int) else 2 * i + r - 3)
                    sp.wait_ge(s_pv, 8 * i + 4 * r - 4)
                    stage_v(sp, V, VB[r], 2 * i + r, s_vb[r])

            two_tiles(1)
            with sp.Fori(2, NT // 2) as i:
                two_tiles(i)
            for t in (NT - 2, NT - 1):
                context(t, t % 2, t - 1)
            sp.dma_start(raw13, wch_d[0, :, 0:2 * D]).then_inc(com.s_r13, 16)
            sp.dma_start(gate, gate_d).then_inc(f_gate, 16)

        @block.gpsimd
        def _(pool):
            def step(i, r):
                if isinstance(i, int) and 8 * i + r == X_KV - 2:
                    nc.gpsimd.memset(kbx, 0.0).then_inc(x_zero, 1)
                    nc.gpsimd.memset(vbx, 0.0).then_inc(x_zero, 1)
                q = r - 1
                if steps.live(i, q):
                    pool.wait_ge(s_inv, 8 * i + q + 1)
                    e = EX[:, q % 4, :, :].rearrange("p x (g s) -> p (x g) s", g=2)
                    nc.gpsimd.tensor_tensor(e, e, bc(ri[:, q % 4, :], 2, SEQ), ALU.mult).then_inc(s_norm, 1)
                n = cross(i, r, X_SUM)
                if n is not None:
                    pool.wait_ge(x_inv, 2 * i + n + 1)
                    nc.gpsimd.tensor_tensor(XE, XE, bc(xri[:], 2, SEQ), ALU.mult).then_inc(x_prob, 1)
                n = cross(i, r, X_VAR)
                if n is not None:
                    pool.wait_ge(x_var, 2 * i + n + 1)
                    nc.gpsimd.tensor_tensor(rs[:, 1:2], rs[:, 0:1], com.mhalf[:, 0:1], ALU.pow).then_inc(x_pow, 1)

                for g, tiles in enumerate(com.groups):
                    if at(i, r, N_POW[g]):
                        norm_power(nc, pool, tiles, g, com.mhalf, com.tmp, com.s_var, com.s_pow)
                if at(i, r, 42):
                    pool.wait_ge(com.s_13hi, 1)
                    nc.gpsimd.tensor_tensor(com.w13[1][:], raw13, as_f32(com.w13[0][:]),
                                            ALU.subtract).then_inc(com.s_13lo, 1)

            steps.run(pool, step)

        @block.scalar
        def _(act):
            def step(i, r):
                if steps.live(i, r):
                    act.wait_ge(s_shift, 8 * i + r + 1)
                    nc.scalar.activation(EX[:, r % 4, :, :], EX[:, r % 4, :, :], ACT.Exp,
                                         scale=SCALE).then_inc(s_exp, 1)
                q = r - S_T
                if steps.live(i, q):
                    act.wait_ge(s_pT, 8 * i + q + 1)
                    if steps.later(i, q, 2):
                        act.wait_ge(s_pv, 8 * i + q - 1)
                    nc.scalar.copy(PT[:, q % 2, :, :].rearrange("p a n -> p (a n)"),
                                   ps_p[:]).then_inc(s_pTc, 1)
                q = r - S_PV
                if steps.live(i, q):
                    act.wait_ge(s_pv, 8 * i + q + 1)
                    if steps.later(i, q, 4):
                        act.wait_ge(s_y, 8 * i + 2 * (q // 2) - 2)
                    b = q % 2
                    nc.scalar.copy(OT[(q // 2) % 2][0][:, :, b * SEQ:(b + 1) * SEQ],
                                   ps_o[:].rearrange("p (c s) -> p c s", s=SEQ)).then_inc(s_ohi, 1)
                n = cross(i, r, X_Q)
                if n is not None:
                    act.wait_ge(x_q, 2 * i + n + 1)
                    nc.scalar.copy(QT.rearrange("p c m -> p (c m)"), ps_xq[:, 0:D]).then_inc(x_qc, 1)
                n = cross(i, r, X_S)
                if n is not None:
                    act.wait_ge(x_shift, 2 * i + n + 1)
                    nc.scalar.activation(XE, XE, ACT.Exp, scale=XSCALE).then_inc(x_exp, 1)
                n = cross(i, r, X_T)
                if n is not None:
                    act.wait_ge(x_pT, 2 * i + n + 1)
                    nc.scalar.copy(XPT.rearrange("p h m -> p (h m)"), ps_xs[:]).then_inc(x_pTc, 1)
                n = cross(i, r, X_KV)
                if n is not None:
                    if isinstance(i, int) and 2 * i + n == 0:
                        act.wait_ge(x_zero, 2)
                    act.wait_ge(x_kv, 2 * i + n + 1)
                    for h4 in range(4):
                        rows = slice(h4 * XN, (h4 + 1) * XN)
                        last = nc.scalar.copy(kbx[rows, :, :, h4, :].rearrange("p c b s -> p (c b) s"),
                                              ps_xo[rows, 0:D].rearrange("p (m s) -> p m s", s=SEQ))
                    last.then_inc(x_k, 1)
                n = cross(i, r, X_MEAN)
                if n is not None:
                    act.wait_ge(x_mean, 2 * i + n + 1)
                    nc.scalar.activation(SQ, XC, ACT.Square, bias=rs[:, 7:8], accum_out=rs[:, 8:9]).then_inc(x_sq, 1)
                n = cross(i, r, X_NORM)
                if n is not None:
                    for b in range(2):
                        src = ps_xo[b * SEQ:(b + 1) * SEQ, D:2 * D].rearrange("p (m g n) -> p m g n", g=2, n=XN)
                        for h2 in range(2):
                            last = nc.scalar.copy(vbx[h2 * SEQ:(h2 + 1) * SEQ, n % 2, :, b, h2, :], src[:, :, h2, :])
                    last.then_inc(x_v, 1)
                if at(i, r, 38):
                    act.wait_ge(s_y, NUN)
                    act.wait_ge(f_gate, 16)
                    nc.scalar.copy(com.gw[0][:], gate).then_inc(f_ghi, 1)
                    act.wait_ge(com.s_r13, 16)
                    nc.scalar.copy(com.w13[0][:], raw13).then_inc(com.s_13hi, 1)
                for g, tiles in enumerate(com.groups):
                    if at(i, r, N_HI[g]):
                        act.wait_ge(f_tr, g + 1)
                        for kc, (src, dst) in enumerate(transposed(g, tiles)):
                            last = nc.scalar.copy(dst[0], src)
                        last.then_inc(f_xhi, 1)

            steps.run(act, step)

        @block.vector
        def _(dve):
            def tile_of(t):
                return X[:, bass.ds(t, 1), :].rearrange("p o d -> p (o d)")

            norm_chain = Chain(dve, f_stat)

            def stat(i, n, j, ins):
                ins.then_inc(x_stat, 1)
                dve.wait_ge(x_stat, 5 * (2 * i + n) + j)

            def step(i, r):
                q = r - S_LO
                if steps.live(i, q):
                    b, ot = q % 2, OT[(q // 2) % 2]
                    dve.wait_ge(s_ohi, 8 * i + q + 1)
                    hi, lo = (o[:, :, b * SEQ:(b + 1) * SEQ] for o in ot)
                    nc.vector.tensor_tensor(lo, ps_o[:].rearrange("p (c s) -> p c s", s=SEQ), as_f32(hi),
                                            ALU.subtract).then_inc(s_olo, 1)
                q = r - S_ADD
                if steps.live(i, q) and q % 4 == 3:
                    t = 2 * i + q // 4
                    dve.wait_ge(s_y, 8 * i + q + 1)
                    if not isinstance(i, int) or t >= 1:
                        dve.wait_ge(x_norm, t)
                    nc.vector.tensor_tensor(XC, ps_y[:, 0:D], tile_of(t), ALU.add).then_inc(x_tok, 1)
                    nc.vector.tensor_tensor(tile_of(t), ps_y[:, 0:D], tile_of(t), ALU.add).then_inc(s_res, 1)
                n = cross(i, r, X_ADD)
                if n is not None:
                    t = 2 * i + n
                    dve.wait_ge(x_y, t + 1)
                    nc.vector.tensor_tensor(tile_of(t), ps_xq[:, 0:D], tile_of(t), ALU.add).then_inc(x_res, 1)
                if steps.live(i, r):
                    rows = ps_s[r % 2][:].rearrange("p (x s) -> p x s", s=SEQ)
                    dve.wait_ge(s_scores, 8 * i + r + 1)
                    nc.vector.tensor_reduce(mx[:, r % 2, :], rows, AX.X, ALU.max).then_inc(s_max, 1)
                    dve.wait_ge(s_max, 8 * i + r + 1)
                    if steps.later(i, r, 4):
                        dve.wait_ge(s_pT, 8 * i + r - 3)
                    nc.vector.tensor_tensor(EX[:, r % 4, :, :].rearrange("p x (g s) -> p (x g) s", g=2), rows,
                                            bc(mx[:, r % 2, :], 2, SEQ), ALU.subtract).then_inc(s_shift, 1)
                q = r - 1
                if steps.live(i, q):
                    dve.wait_ge(s_exp, 8 * i + q + 1)
                    nc.vector.tensor_reduce(sm[:, q % 2, :], EX[:, q % 4, :, :].rearrange("p x (g s) -> p (x g) s", g=2),
                                            AX.X, ALU.add).then_inc(s_sum, 1)
                    dve.wait_ge(s_sum, 8 * i + q + 1)
                    nc.vector.reciprocal(ri[:, q % 4, :], sm[:, q % 2, :]).then_inc(s_inv, 1)
                n = cross(i, r, X_DIFF)
                if n is not None:
                    dve.wait_ge(x_pv, 2 * i + n + 1)
                    for b in range(2):
                        rows = slice(b * SEQ, (b + 1) * SEQ)
                        last = nc.vector.tensor_tensor(
                            DF[rows, :].rearrange("p (h n) -> p h n", h=4),
                            XQ[rows, n % 2, :].rearrange("p (h n) -> p h n", h=4),
                            ps_xo[rows, :].rearrange("p (h b n) -> p h b n", h=4, b=2)[:, :, b, :], ALU.subtract)
                    last.then_inc(x_diff, 1)
                n = cross(i, r, X_S)
                if n is not None:
                    rows = ps_xs[:].rearrange("p (x s) -> p x s", s=SEQ)
                    dve.wait_ge(x_scores, 2 * i + n + 1)
                    nc.vector.tensor_reduce(xmx[:], rows, AX.X, ALU.max).then_inc(x_max, 1)
                    dve.wait_ge(x_max, 2 * i + n + 1)
                    nc.vector.tensor_tensor(XE, rows, bc(xmx[:], 2, SEQ), ALU.subtract).then_inc(x_shift, 1)
                n = cross(i, r, X_SUM)
                if n is not None:
                    dve.wait_ge(x_exp, 2 * i + n + 1)
                    nc.vector.tensor_reduce(xsm[:], XE, AX.X, ALU.add).then_inc(x_sum, 1)
                    dve.wait_ge(x_sum, 2 * i + n + 1)
                    nc.vector.reciprocal(xri[:], xsm[:]).then_inc(x_inv, 1)
                n = cross(i, r, X_MEAN)
                if n is not None:
                    dve.wait_ge(x_tok, 2 * i + n + 1)
                    stat(i, n, 1, nc.vector.tensor_reduce(rs[:, 6:7], XC, AX.X, ALU.add))
                    nc.vector.tensor_scalar(rs[:, 7:8], rs[:, 6:7], -1.0 / D, None, ALU.mult).then_inc(x_mean, 1)
                n = cross(i, r, X_VAR)
                if n is not None:
                    dve.wait_ge(x_sq, 2 * i + n + 1)
                    nc.vector.tensor_scalar(rs[:, 0:1], rs[:, 8:9], 1.0 / D, EPS, ALU.mult, ALU.add
                                            ).then_inc(x_var, 1)
                n = cross(i, r, X_NORM)
                if n is not None:
                    dve.wait_ge(x_pow, 2 * i + n + 1)
                    stat(i, n, 2, nc.vector.tensor_tensor(rs[:, 2:3], rs[:, 1:2], rs[:, 1:2], ALU.mult))
                    stat(i, n, 3, nc.vector.tensor_tensor(rs[:, 3:4], rs[:, 2:3], rs[:, 0:1], ALU.mult))
                    stat(i, n, 4, nc.vector.tensor_scalar(rs[:, 4:5], rs[:, 3:4], -0.5, 1.5, ALU.mult, ALU.add))
                    stat(i, n, 5, nc.vector.tensor_tensor(rs[:, 5:6], rs[:, 1:2], rs[:, 4:5], ALU.mult))
                    nc.vector.tensor_scalar(XQ[:, n % 2, :], XC, rs[:, 7:8], rs[:, 5:6],
                                            ALU.add, ALU.mult).then_inc(x_norm, 1)
                for g, tiles in enumerate(com.groups):
                    if at(i, r, N_STAT[g]):
                        dve.wait_ge(x_res, tiles.stop)
                        norm_stats(nc, norm_chain, X, tiles, com.st, com.mv, com.tmp, com.s_var)
                    if at(i, r, N_APPLY[g]):
                        norm_apply(nc, norm_chain, X, XN3[g], tiles, g, com.mv, com.tmp, com.s_pow, f_xn)
                    if at(i, r, N_LO[g]):
                        dve.wait_ge(f_xhi, g + 1)
                        for src, dst in transposed(g, tiles):
                            nc.vector.tensor_tensor(dst[1], src, as_f32(dst[0]), ALU.subtract)
                if at(i, r, 38):
                    dve.wait_ge(f_ghi, 1)
                    nc.vector.tensor_tensor(com.gw[1][:], gate, as_f32(com.gw[0][:]), ALU.subtract)

            steps.run(dve, step)

        @block.tensor
        def _(pe):
            def step(i, r):
                if steps.live(i, r):
                    ring, gh, b = (r // 4) % 2, (r // 2) % 2, r % 2
                    if r % 4 == 0:
                        pe.wait_ge(s_qk[ring], 16 * (N_Q + N_K) * i + 16 * (N_Q + N_K))
                    if steps.later(i, r, 2):
                        pe.wait_ge(s_shift, 8 * i + r - 1)
                    nc.tensor.matmul(ps_s[r % 2][:], ident_b[:], mask[:].rearrange("p x n -> p (x n)"),
                                     start=True, stop=False)
                    for x in range(4):
                        s, m0 = x // 2, (2 * G * b + 2 * x) * SEQ
                        last = nc.tensor.matmul(ps_s[r % 2][:, x * P:(x + 1) * P],
                                                Q[ring][:, gh, m0:m0 + P],
                                                KB[ring][:, gh, s, b, :], start=False, stop=x == 3)
                    last.then_inc(s_scores, 1)
                q = r - S_T
                if steps.live(i, q):
                    pe.wait_ge(s_norm, 8 * i + q + 1)
                    if steps.later(i, q, 1):
                        pe.wait_ge(s_pTc, 8 * i + q)
                    for x in range(4):
                        last = nc.tensor.transpose(ps_p[:, x * P:(x + 1) * P], EX[:, q % 4, x, :], ident[:])
                    last.then_inc(s_pT, 1)
                q = r - S_PV
                if steps.live(i, q):
                    ring, gh, b = (q // 4) % 2, (q // 2) % 2, q % 2
                    if q % 4 == 0:
                        j = i + q // 8
                        pe.wait_ge(s_vb[ring], 16 * N_V * j + 16 * N_V)
                    pe.wait_ge(s_pTc, 8 * i + q + 1)
                    if steps.later(i, q, 1):
                        pe.wait_ge(s_olo, 8 * i + q)
                    for x in range(2):
                        last = nc.tensor.matmul(ps_o[:, x * 2 * P:(x + 1) * 2 * P],
                                                VB[ring][:, b, 2 * x + gh, :], PT[:, q % 2, x, :],
                                                start=True, stop=True)
                    last.then_inc(s_pv, 1)

                n = cross(i, r, X_Q)
                if n is not None:
                    pe.wait_ge(x_norm, 2 * i + n + 1)
                    for c in range(2):
                        last = nc.tensor.matmul(ps_xq[:, c * P:(c + 1) * P], XQ[:, n % 2, c * P:(c + 1) * P],
                                                WX[:, 0, :], start=True, stop=True)
                    last.then_inc(x_q, 1)
                n = cross(i, r, X_PV)
                if n is not None:
                    pe.wait_ge(x_pTc, 2 * i + n + 1)
                    ahead = 2 * i + n + 2
                    if isinstance(i, int):
                        ahead = min(ahead, NT)
                    pe.wait_ge(x_v, ahead)
                    for hp in range(4):
                        last = nc.tensor.matmul(ps_xo[:, hp * P:(hp + 1) * P], XPT[:, hp, :],
                                                vbx[:, n % 2, hp, :, :, :].rearrange("p b h n -> p (b h n)"),
                                                start=True, stop=True)
                    last.then_inc(x_pv, 1)
                n = cross(i, r, X_S)
                if n is not None:
                    pe.wait_ge(x_qc, 2 * i + n + 1)
                    pe.wait_ge(x_k, 2 * i + n + 1)
                    if not isinstance(i, int) or 2 * i + n >= 1:
                        pe.wait_ge(x_pTc, 2 * i + n)
                    for b in range(2):
                        for c in range(2):
                            last = nc.tensor.matmul(ps_xs[b * SEQ:(b + 1) * SEQ, c * 4 * SEQ:(c + 1) * 4 * SEQ],
                                                    QT[:, c, b * SEQ:(b + 1) * SEQ],
                                                    kbx[:, c, b, :, :].rearrange("p h s -> p (h s)"),
                                                    start=True, stop=True)
                    last.then_inc(x_scores, 1)
                n = cross(i, r, X_T)
                if n is not None:
                    pe.wait_ge(x_prob, 2 * i + n + 1)
                    for hp in range(4):
                        last = nc.tensor.transpose(ps_xs[:, hp * P:(hp + 1) * P],
                                                   XE[:, 2 * hp:2 * hp + 2, :].rearrange("p h s -> p (h s)"), ident[:])
                    last.then_inc(x_pT, 1)
                n = cross(i, r, X_KV)
                if n is not None:
                    if isinstance(i, int) and 2 * i + n == 0:
                        pe.wait_ge(x_w, 16)
                    pe.wait_ge(x_c[n % 2], 16 * (i + n // 2 + 1))
                    if not isinstance(i, int) or 2 * i + n >= 2:
                        pe.wait_ge(x_diff, 2 * i + n - 1)
                    for c in range(2):
                        nc.tensor.matmul(ps_xo[:, c * P:(c + 1) * P], C[:, n % 2, c * P:(c + 1) * P], WX[:, 1, :],
                                         start=True, stop=True)
                    nc.tensor.matmul(ps_xo[:, D:2 * D], WX[:, 2, :], C[:, n % 2, :], start=True, stop=True
                                     ).then_inc(x_kv, 1)

                q = r - S_Y
                if steps.live(i, q):
                    v, part = q // 2, q % 2
                    if part == 0:
                        pe.wait_ge(s_olo, 8 * i + 2 * v + 2)
                    if q % 4 == 0 and steps.later(i, q, 4):
                        pe.wait_ge(s_res, 2 * i + q // 4)
                    for c in range(4 * part, 4 * part + 4):
                        last = split3(nc.tensor, ps_y[:, 0:D], OT[v % 2], WO,
                                      (slice(None), c), (slice(None), 8 * (v % 2) + c),
                                      q % 4 == 0 and c == 0, q % 4 == 3 and c == 7)
                    last.then_inc(s_y, 1)
                n = cross(i, r, X_DIFF)
                if n is not None:
                    pe.wait_ge(x_diff, 2 * i + n + 1)
                    nc.tensor.matmul(ps_xq[:, 0:D], WX[:, 3, :], DF, start=True, stop=True).then_inc(x_y, 1)
                for g, tiles in enumerate(com.groups):
                    if at(i, r, N_TR[g]):
                        if g == 0:
                            pe.wait_ge(s_shift, NUN)
                        pe.wait_ge(f_xn, tiles.stop)
                        for kc, (dst, _) in enumerate(transposed(g, tiles)):
                            for q in range(len(tiles)):
                                last = nc.tensor.transpose(dst[:, q * P:(q + 1) * P],
                                                           XN3[g][:, q, kc * P:(kc + 1) * P], ident[:])
                        last.then_inc(f_tr, 1)

            steps.run(pe, step)


def expert_phase(nc, com, X, ident, d, out_d):
    LAG = 2
    UP = 2 * D
    with ExitStack() as ctx:
        k = Kit(nc, ctx)
        raw13 = [k.sb(f"raw13_{i}", [P, UP]) for i in range(2)]
        raw2 = [k.sb(f"raw2_{i}", [P, D]) for i in range(2)]
        w13 = [com.w13, [k.sb(f"w13_{n}1", [P, UP], F32R) for n in ("hi", "lo")]]
        w2 = [[k.sb(f"w2_{n}{i}", [P, D], F32R) for n in ("hi", "lo")] for i in range(2)]
        xnT, gw = com.xnT, com.gw
        xn = k.sb("f_xn", [P, NT, D])
        lgT = k.sb("logits_T", [E, T])
        bias = k.sb("bias", [P, E])
        lower_f = k.sb("lower_f", [P, E, E])
        lower = k.sb("lower", [P, E, E], BF16)
        sg = k.sb("silu", [P, 2, HALF])
        hu = k.sb("gated", [P, 2, HALF])
        hw = k.sb("weighted", [P, 2, HALF])
        H = [[k.sb(f"h_{n}{i}", [P, HALF], F32R) for n in ("hi", "lo")] for i in range(2)]
        CW = k.sb("cw_rows", [P, 2, T])
        cwr = k.sb("cw_repeated", [P, NT, 2, EG, UNIT])
        yT = k.sb("yT", [P, KC, T])
        mhalf, st, mv, tmp = com.mhalf, com.st, com.mv, com.tmp
        ex = k.sb("g_exp", [P, NT, E])
        den = k.sb("g_den", [P, NT, E])
        sc = k.sb("g_scores", [P, NT, E])
        biased = k.sb("g_biased", [P, NT, E])
        gm = k.sb("g_group_max", [P, NT, GE])
        gbeat = k.sb("g_gbeat", [P, 3, NT, GE, GE])
        gcnt = k.sb("g_gcount", [P, NT, GE])
        gsel = k.sb("g_group_sel", [P, NT, GE])
        goff = k.sb("g_group_off", [P, NT, GE])
        kept = k.sb("g_kept", [P, NT, E])
        msk = k.sb("g_masked", [P, NT, E])
        beat = k.sb("g_beat", [P, NT, E, E], BF16)
        tie = k.sb("g_tie", [P, NT, E, E], BF16)
        cnt = k.sb("g_count", [P, NT, E])
        sel = k.sb("g_selected", [P, NT, E])
        picked = k.sb("g_picked", [P, NT, E])
        wsum = k.sb("g_sum", [P, 2, NT])
        cw = k.sb("g_weight", [P, NT, E])
        acc = [[k.bank(f"acc{dc}{h}") for h in range(NHALF)] for dc in range(KC)]
        up = [[k.bank(f"up{n}{i}") for n in range(2)] for i in range(2)]

        last_tiles = range(NT - 2, NT)
        last_T = [x[:, :, T - 2 * P:T] for x in xnT]
        ps_last = up[1][0][:].rearrange("p (k t) -> p k t", k=KC)

        s_bias = k.sem("p4_bias")
        s_r13 = [com.s_r13, k.sem("p4_raw13_1")]
        s_r2 = [k.sem(f"p4_raw2_{i}") for i in range(2)]
        s_stat = k.sem("p4_stat")
        s_xn = k.sem("p4_xn")
        s_tr = k.sem("p4_transposed")
        s_xhi = k.sem("p4_xnT_hi")
        s_xlo = k.sem("p4_xnT_lo")
        s_logT = k.sem("p4_logits_T")
        s_lgT = k.sem("p4_logits_T_copied")
        s_log = k.sem("p4_logits")
        s_gexp = k.sem("p4_gate_exp")
        s_g = k.sem("p4_gating")
        s_masked = k.sem("p4_masked")
        s_weight = k.sem("p4_weights")
        s_lower = k.sem("p4_lower")
        s_cwr = k.sem("p4_cw_repeated")
        s_cwt = k.sem("p4_cw_transposed")
        s_cw = k.sem("p4_cw_rows")
        s_13hi, s_13lo = com.s_13hi, com.s_13lo
        s_2hi = k.sem("p4_w2_hi")
        s_2lo = k.sem("p4_w2_lo")
        s_up = k.sem("p4_up")
        s_silu = k.sem("p4_silu")
        s_gated = k.sem("p4_gated")
        s_wtd = k.sem("p4_weighted")
        s_hhi = k.sem("p4_h_hi")
        s_hlo = k.sem("p4_h_lo")
        s_down = k.sem("p4_down")
        s_yT = k.sem("p4_yT")
        s_yt = k.sem("p4_y_transposed")
        s_y = k.sem("p4_y")
        s_out = k.sem("p4_out")
        block = ctx.enter_context(nc.Block())

        N0 = 2 * NSC

        def run_units(eng, step, lag):
            for n in range(N0 + 4):
                step((n - N0) // 4, (n - N0) % 4)
            with eng.Fori(1, NU - 1) as u:
                for r in range(4):
                    step(u, r)
            for r in range(4 + lag):
                step(NU - 1, r)

        def live(u, q):
            return not isinstance(u, int) or 0 <= 4 * u + N0 + q < 2 * NC

        def after(u, q, n):
            return not isinstance(u, int) or 4 * u + N0 + q >= n

        def shared(u, q):
            return isinstance(u, int) and 4 * u + q < 0

        def place(q):
            return (NSC + q // 2) % 2

        @block.sync
        def _(sp):
            def load13(u, q):
                c, i = 2 * u + NSC + q // 2, place(q)
                if after(u, q, 4):
                    sp.wait_ge(s_13lo, c - 1)
                sp.dma_start(raw13[i][:], d["wch"][bass.ds(c, 1), :, 0:UP].rearrange("o p n -> (o p) n")
                             ).then_inc(s_r13[i], 16)

            def load2(u, q):
                c, i = 2 * u + NSC + q // 2, place(q)
                if after(u, q, 4):
                    sp.wait_ge(s_2lo, c - 1)
                sp.dma_start(raw2[i][:], d["wch"][bass.ds(c, 1), :, UP:UP + D].rearrange("o p n -> (o p) n")
                             ).then_inc(s_r2[i], 16)

            load13(-1, 0)
            load2(-2, 2)
            sp.dma_start(bias[:], d["bias"].partition_broadcast(P)).then_inc(s_bias, 16)
            sp.dma_start(lower_f[:], d["lower"].partition_broadcast(P)).then_inc(s_bias, 16)

            def step(u, r):
                if r % 2 == 0:
                    if live(u, r + 4):
                        load13(u, r + 4)
                    if live(u, r + 2):
                        load2(u, r + 2)

            run_units(sp, step, 0)
            for q in range(2):
                sp.wait_ge(s_y, 4 * (q + 1))
                sp.dma_start(out_d[:, 4 * q:4 * q + 4, :], xn[:, 4 * q:4 * q + 4, :]).then_inc(s_out, 16)
            sp.wait_ge(s_out, 32)

        @block.gpsimd
        def _(pool):
            def low13(u, q):
                c, i = 2 * u + NSC + q // 2, place(q)
                pool.wait_ge(s_13hi, c + 1)
                nc.gpsimd.tensor_tensor(w13[i][1][:], raw13[i][:], as_f32(w13[i][0][:]),
                                        ALU.subtract).then_inc(s_13lo, 1)

            def low2(u, q):
                c, i = 2 * u + NSC + q // 2, place(q)
                pool.wait_ge(s_2hi, c + 1)
                nc.gpsimd.tensor_tensor(w2[i][1][:], raw2[i][:], as_f32(w2[i][0][:]), ALU.subtract).then_inc(s_2lo, 1)

            norm_power(nc, pool, last_tiles, len(com.groups), mhalf, tmp, com.s_var, com.s_pow)

            def step(u, r):
                q = r - 1
                if live(u, q) and shared(u, q):
                    pool.wait_ge(s_hhi, 4 * u + N0 + q + 1)
                    if after(u, q, 2):
                        pool.wait_ge(s_down, 4 * u + N0 + q - 1)
                    nc.gpsimd.tensor_tensor(H[q % 2][1][:], hu[:, q % 2, :], as_f32(H[q % 2][0][:]),
                                            ALU.subtract).then_inc(s_hlo, 1)
                if r % 2 == 0:
                    if live(u, r + 2):
                        low13(u, r + 2)
                    if live(u, r):
                        low2(u, r)
                if live(u, r) and not shared(u, r):
                    if isinstance(u, int) and u == 0 and r < 2:
                        pool.wait_ge(s_cw, 2 * r + 2)
                    pool.wait_ge(s_gated, 4 * u + N0 + r + 1)
                    if not isinstance(u, int) or 4 * u + r >= 2:
                        pool.wait_ge(s_hlo, 4 * u + N0 + r - 1)
                    h = r % 2
                    nc.gpsimd.tensor_tensor(hw[:, h, :], hu[:, h, :], CW[:, r // 2, h * HALF:(h + 1) * HALF],
                                            ALU.mult).then_inc(s_wtd, 1)

            run_units(pool, step, 0)

        @block.scalar
        def _(act):
            def high13(u, q):
                c, i = 2 * u + NSC + q // 2, place(q)
                act.wait_ge(s_r13[i], 16 * (u + (NSC + q // 2) // 2 + 1))
                if after(u, q, 4):
                    act.wait_ge(s_up, 2 * c - 2)
                nc.scalar.copy(w13[i][0][:], raw13[i][:]).then_inc(s_13hi, 1)

            def high2(u, q):
                c, i = 2 * u + NSC + q // 2, place(q)
                act.wait_ge(s_r2[i], 16 * (u + (NSC + q // 2) // 2 + 1))
                if after(u, q, 4):
                    act.wait_ge(s_down, 2 * c - 2)
                nc.scalar.copy(w2[i][0][:], raw2[i][:]).then_inc(s_2hi, 1)

            def weight_rows_out(h):
                for g in range(2):
                    act.wait_ge(s_cwt, 2 * h + g + 1)
                    nc.scalar.copy(CW[:, g, h * HALF:(h + 1) * HALF], up[1][g][:]).then_inc(s_cw, 1)

            def silu(u, r):
                act.wait_ge(s_up, 4 * u + N0 + r + 1)
                if after(u, r, 2):
                    act.wait_ge(s_gated, 4 * u + N0 + r - 1)
                nc.scalar.activation(sg[:, r % 2, :], up[r % 2][0][:], ACT.Silu).then_inc(s_silu, 1)

            def logits_out(h):
                act.wait_ge(s_logT, h + 1)
                nc.scalar.copy(lgT[:, h * HALF:(h + 1) * HALF], acc[0][h][0:E, :]).then_inc(s_lgT, 1)

            logits_out(0)
            high13(-1, 0)
            act.wait_ge(s_tr, 1)
            nc.scalar.copy(last_T[0], ps_last).then_inc(s_xhi, 1)
            silu(-2, 2)
            logits_out(1)
            act.wait_ge(s_log, 1)
            nc.scalar.activation(ex[:].rearrange("p t e -> p (t e)"), acc[1][0][:, 0:NT * E], ACT.Exp,
                                 scale=-1.0).then_inc(s_gexp, 1)

            def step(u, r):
                if r % 2 == 0:
                    if live(u, r):
                        high2(u, r)
                    if live(u, r + 2) and after(u, r, 1):
                        high13(u, r + 2)
                if isinstance(u, int) and u == 0 and r == 1:
                    weight_rows_out(1)
                if live(u, r) and after(u, r, 1):
                    silu(u, r)
                q = r - 1
                if live(u, q):
                    if shared(u, q):
                        act.wait_ge(s_gated, 4 * u + N0 + q + 1)
                    else:
                        act.wait_ge(s_wtd, 4 * u + q + 1)
                    if after(u, q, 2):
                        act.wait_ge(s_down, 4 * u + N0 + q - 1)
                    src = hu if shared(u, q) else hw
                    nc.scalar.copy(H[q % 2][0][:], src[:, q % 2, :]).then_inc(s_hhi, 1)
                if isinstance(u, int) and u == 0 and r == 0:
                    weight_rows_out(0)
                if isinstance(u, int) and 4 * u + r == -1:
                    act.wait_ge(s_weight, 1)
                    for h in range(2):
                        tiles = slice(h * NT // 2, (h + 1) * NT // 2)
                        nc.scalar.copy(cwr[:, tiles].rearrange("p t g e i -> p (t g e) i"),
                                       bc(cw[:, tiles].rearrange("p t e -> p (t e)"), 2, UNIT)).then_inc(s_cwr, 1)

            run_units(act, step, 1)
            for n in range(4):
                dc, h = n % 2, n // 2
                act.wait_ge(s_down, 2 * NC - 1 + h)
                nc.scalar.copy(yT[:, dc, h * HALF:(h + 1) * HALF], acc[dc][h][:]).then_inc(s_yT, 1)

        @block.vector
        def _(dve):
            routing_chain = Chain(dve, s_g)
            then = routing_chain.then
            chain = Chain(dve, s_stat)
            norm_stats(nc, chain, X, last_tiles, st, mv, tmp, com.s_var)
            norm_apply(nc, chain, X, xn, last_tiles, len(com.groups), mv, tmp, com.s_pow, s_xn)
            dve.wait_ge(s_xhi, 1)
            nc.vector.tensor_tensor(last_T[1], ps_last, as_f32(last_T[0]), ALU.subtract).then_inc(s_xlo, 1)

            dve.wait_ge(s_bias, 32)

            def choose_groups():
                nc.vector.tensor_copy(lower[:], lower_f[:]).then_inc(s_lower, 1)
                dve.wait_ge(s_lower, 1)
                dve.wait_ge(s_gexp, 1)
                then(nc.vector.tensor_scalar(den[:], ex[:], 1.0, None, ALU.add))
                then(nc.vector.reciprocal(sc[:], den[:]))
                then(nc.vector.tensor_tensor(biased[:], sc[:], bc(bias[:], 1, NT), ALU.add))
                grouped = biased[:].rearrange("p t (g e) -> p t g e", g=GE)
                then(nc.vector.tensor_reduce(gm[:], grouped, AX.X, ALU.max))

            def mask_groups():
                grouped = biased[:].rearrange("p t (g e) -> p t g e", g=GE)
                other, own = bc(gm[:], 2, GE), bc(gm[:], 3, GE)
                nc.vector.tensor_tensor(gbeat[:, 0], other, own, ALU.is_gt)
                then(nc.vector.tensor_tensor(gbeat[:, 1], other, own, ALU.is_equal))
                then(nc.vector.tensor_tensor(gbeat[:, 2], gbeat[:, 1], bc(lower[:, 0:GE, 0:GE], 1, NT), ALU.mult))
                then(nc.vector.tensor_tensor(gbeat[:, 1], gbeat[:, 0], gbeat[:, 2], ALU.add))
                then(nc.vector.tensor_reduce(gcnt[:], gbeat[:, 1], AX.X, ALU.add))
                then(nc.vector.tensor_scalar(gsel[:], gcnt[:], TOPG - 0.5, None, ALU.is_lt))
                nc.vector.tensor_scalar(goff[:], gsel[:], 1.0, -MASKED, ALU.subtract, ALU.mult)
                then(nc.vector.tensor_tensor(kept[:].rearrange("p t (g e) -> p t g e", g=GE), grouped,
                                             bc(gsel[:], 3, E // GE), ALU.mult))
                nc.vector.tensor_tensor(msk[:].rearrange("p t (g e) -> p t g e", g=GE),
                                        kept[:].rearrange("p t (g e) -> p t g e", g=GE),
                                        bc(goff[:], 3, E // GE), ALU.add).then_inc(s_masked, 1)

            def find_ties():
                dve.wait_ge(s_masked, 1)
                then(nc.vector.tensor_tensor(tie[:], bc(msk[:], 2, E), bc(msk[:], 3, E), ALU.is_equal))

            def find_greater():
                nc.vector.tensor_tensor(beat[:], bc(msk[:], 2, E), bc(msk[:], 3, E), ALU.is_gt)
                then(nc.vector.tensor_tensor(tie[:], tie[:], bc(lower[:], 1, NT), ALU.mult))

            def count_better():
                then(nc.vector.tensor_tensor(beat[:], beat[:], tie[:], ALU.add))
                then(nc.vector.tensor_reduce(cnt[:], beat[:], AX.X, ALU.add))

            def weights():
                then(nc.vector.tensor_scalar(sel[:], cnt[:], TOPK - 0.5, None, ALU.is_lt))
                then(nc.vector.tensor_tensor(picked[:], sc[:], sel[:], ALU.mult))
                then(nc.vector.tensor_reduce(wsum[:, 0, :], picked[:], AX.X, ALU.add))
                then(nc.vector.reciprocal(wsum[:, 1, :], wsum[:, 0, :]))
                nc.vector.tensor_tensor(cw[:], picked[:], bc(wsum[:, 1, :], 2, E), ALU.mult).then_inc(s_weight, 1)

            routing = {-6: mask_groups, -5: find_ties, -4: find_greater, -3: count_better, -2: weights}

            def gate_unit(u, r):
                dve.wait_ge(s_silu, 4 * u + N0 + r + 1)
                if shared(u, r):
                    if after(u, r, 2):
                        dve.wait_ge(s_hlo, 4 * u + N0 + r - 1)
                elif not isinstance(u, int) or 4 * u + r >= 2:
                    dve.wait_ge(s_wtd, 4 * u + r - 1)
                else:
                    dve.wait_ge(s_hlo, 4 * u + N0 + r - 1)
                nc.vector.tensor_tensor(hu[:, r % 2, :], up[r % 2][1][:], sg[:, r % 2, :],
                                        ALU.mult).then_inc(s_gated, 1)

            def step(u, r):
                if live(u, r) and after(u, r, 1):
                    gate_unit(u, r)
                q = r - 1
                if live(u, q) and not shared(u, q):
                    dve.wait_ge(s_hhi, 4 * u + N0 + q + 1)
                    nc.vector.tensor_tensor(H[q % 2][1][:], hw[:, q % 2, :], as_f32(H[q % 2][0][:]),
                                            ALU.subtract).then_inc(s_hlo, 1)
                if isinstance(u, int) and 4 * u + r in routing:
                    routing[4 * u + r]()

            gate_unit(-2, 2)
            choose_groups()
            run_units(dve, step, 1)
            for t in range(NT):
                dve.wait_ge(s_yt, t + 1)
                nc.vector.tensor_tensor(xn[:, t, :], up[(t // 2) % 2][t % 2][:, 0:D], X[:, t, :],
                                        ALU.add).then_inc(s_y, 1)

        @block.tensor
        def _(pe):
            def logits(h):
                for kc in range(KC):
                    last = split3(nc.tensor, acc[0][h][0:E, :], gw, xnT, (slice(None), kc),
                                  (slice(None), kc, slice(h * HALF, (h + 1) * HALF)), kc == 0, kc == KC - 1)
                last.then_inc(s_logT, 1)

            def weight_rows(h):
                pe.wait_ge(s_cwr, h + 1)
                if h == 0:
                    pe.wait_ge(s_gated, N0)
                else:
                    pe.wait_ge(s_cw, 2)
                for g in range(2):
                    for x in range(4):
                        last = nc.tensor.transpose(up[1][g][:, x * P:(x + 1) * P],
                                                   cwr[:, 4 * h + x, g, :, :].rearrange("p e i -> p (e i)"), ident[:])
                    last.then_inc(s_cwt, 1)

            def transpose_last():
                for q in range(2):
                    pe.wait_ge(s_xn, q + 1)
                    for kc in range(KC):
                        last = nc.tensor.transpose(ps_last[:, kc, q * P:(q + 1) * P], xn[:, q, kc * P:(kc + 1) * P],
                                                   ident[:])
                last.then_inc(s_tr, 1)

            def logits_back():
                pe.wait_ge(s_lgT, 2)
                for t in range(NT):
                    last = nc.tensor.transpose(acc[1][0][:, t * E:(t + 1) * E], lgT[:, t * P:(t + 1) * P],
                                               ident[0:E, 0:E])
                last.then_inc(s_log, 1)

            logits(0)

            def step(u, r):
                if isinstance(u, int) and 4 * u + r == 1 - N0:
                    pe.wait_ge(s_xlo, 1)
                    logits(1)
                if isinstance(u, int) and u == 0 and r == 1:
                    down(u, r - LAG)
                    weight_rows(1)
                    pe.wait_ge(s_cw, 4)
                if live(u, r):
                    w = [x[:].rearrange("p (a k m) -> p a k m", a=2, k=KC) for x in w13[place(r)]]
                    c, h = 2 * u + NSC + r // 2, r % 2
                    if h == 0:
                        pe.wait_ge(s_13lo, c + 1)
                    if after(u, r, 2):
                        pe.wait_ge(s_gated, 4 * u + N0 + r - 1)
                    for m in range(2):
                        for kc in range(KC):
                            last = split3(nc.tensor, up[r % 2][m][:], w, xnT, (slice(None), m, kc),
                                          (slice(None), kc, slice(h * HALF, (h + 1) * HALF)), kc == 0, kc == KC - 1)
                        if m == 0 and isinstance(u, int) and 4 * u + r == -N0:
                            transpose_last()
                        if m == 0 and isinstance(u, int) and 4 * u + r == 1 - N0:
                            logits_back()
                    last.then_inc(s_up, 1)
                if not (isinstance(u, int) and u == 0 and r == 1):
                    down(u, r - LAG)
                if isinstance(u, int) and u == 0 and r == 0:
                    weight_rows(0)

            def down(u, q):
                if live(u, q):
                    c, h = 2 * u + NSC + q // 2, q % 2
                    if h == 0:
                        pe.wait_ge(s_2lo, c + 1)
                        if isinstance(u, int) and 4 * u + q == -N0:
                            pe.wait_ge(s_gexp, 1)
                    pe.wait_ge(s_hlo, 4 * u + N0 + q + 1)
                    first = isinstance(u, int) and 4 * u + N0 + q < 2
                    end = isinstance(u, int) and 4 * u + N0 + q >= 2 * NC - 2
                    for dc in range(KC):
                        last = split3(nc.tensor, acc[dc][h][:], w2[place(q)], H[q % 2],
                                      (slice(None), slice(dc * P, (dc + 1) * P)), (slice(None),), first, end)
                    last.then_inc(s_down, 1)

            run_units(pe, step, LAG)
            for t in range(NT):
                pe.wait_ge(s_yT, 2 * (t // 4) + 2)
                if t >= 4:
                    pe.wait_ge(s_y, t - 3)
                for dc in range(KC):
                    last = nc.tensor.transpose(up[(t // 2) % 2][t % 2][:, dc * P:(dc + 1) * P],
                                               yT[:, dc, t * P:(t + 1) * P], ident[:])
                last.then_inc(s_yt, 1)


def decoder_layer(nc, d, out):
    with ExitStack() as ctx:
        k = Kit(nc, ctx)
        X = k.sb("x", [P, NT, D])
        ident = k.sb("ident", [P, P])
        com = Common(k)
        x_d = d["x"].rearrange("(t p) c -> p t c", p=P)
        out_d = out.rearrange("(t p) c -> p t c", p=P)
        with ExitStack() as c1:
            k1 = Kit(nc, c1)
            QR = k1.sb("q_rotated", [P, 2, NT, 2 * 2 * G * SEQ])
            KR = k1.sb("k_rotated", [P, 2, NT, 2, P])
            V = k1.sb("v", [P, NT, HKV * HD])
            Q = [k1.sb(f"q_tile{i}", [P, 4 * HALF]) for i in range(2)]
            k_mem = [k1.sb(f"k_blocks{i}", [P, 2 * HALF]) for i in range(2)]
            v_mem = [k1.sb(f"v_blocks{i}", [P, 2 * HALF]) for i in range(2)]
            KB = [x[:].rearrange("p (a s b n) -> p a s b n", a=2, s=2, b=2) for x in k_mem]
            VB = [x[:].rearrange("p (b g n) -> p b g n", b=2, g=4) for x in v_mem]
            staged = (Q, k_mem, v_mem, KB, VB)
            s_qk = [k1.sem(f"qk_staged{i}") for i in range(2)]
            s_vb = [k1.sem(f"v_staged{i}") for i in range(2)]
            mask = k1.sb("mask", [P, 4, P], BF16)
            ident_b = k1.sb("ident_b", [P, P], BF16)
            qkv_phase(nc, com, X, QR, KR, V, ident, staged, s_qk, s_vb, mask, ident_b, x_d, d["wqk"], d["wv"], d["wo"],
                      d["cos_sin"], d["ident"], d["mask"])
            attention_phase(nc, com, X, QR, KR, V, ident, staged, s_qk, s_vb, mask, ident_b,
                            d["ctx"].rearrange("(t p) c -> p t c", p=P), d["wx"], d["gate"], d["wch"])
        expert_phase(nc, com, X, ident, d, out_d)



def layout(x, ctx_2048, L0_attn_Wq, L0_attn_Wk, L0_attn_Wv, L0_attn_Wo, L0_xattn_W_q, L0_xattn_W_k,
           L0_xattn_W_v, L0_xattn_W_o, L0_ffn_gate_w, L0_ffn_expert_bias, L0_ffn_w1, L0_ffn_w2, L0_ffn_w3,
           L0_ffn_sw1, L0_ffn_sw2, L0_ffn_sw3):
    a = np.ascontiguousarray
    f4 = np.float32

    def pairs(w, heads):
        w = np.asarray(w).reshape(2, 4, heads, F, 2, KC, P)
        return w.transpose(0, 2, 6, 5, 4, 1, 3).reshape(2 * heads, P, KC * 2 * P)

    wqk = np.concatenate([pairs(L0_attn_Wk, 1), pairs(L0_attn_Wq, G)], 0)
    wv = np.asarray(L0_attn_Wv).reshape(HKV * HD, KC, P).transpose(2, 1, 0)
    wo = np.asarray(L0_attn_Wo).reshape(D, 2, 2, 2, G, HD).transpose(3, 5, 2, 1, 4, 0)
    wo = wo.reshape(P, NT, HKV * HD)
    inv = (f4(1.0) / f4(10000.0) ** (np.arange(0, HD, 2, dtype=f4) / f4(HD))).astype(f4)
    ang = (np.arange(SEQ, dtype=f4)[None, :] * inv[:, None]).astype(f4)
    cs = np.stack([np.cos(ang), np.sin(ang)], 1).astype(f4)
    cs = np.tile(cs, (4, 1, 1))
    q, kk = np.arange(P)[:, None] % SEQ, np.arange(P)[None, :] % SEQ
    mask = np.where(q >= kk, 0.0, MASKED).astype(f4)
    wx = np.zeros((P, 4, P), f4)
    for n, w in enumerate((L0_xattn_W_q, L0_xattn_W_k, L0_xattn_W_v, L0_xattn_W_o)):
        for b in range(2):
            wx[b * SEQ:(b + 1) * SEQ, n, b * SEQ:(b + 1) * SEQ] = np.asarray(w).T
    def up_chunks(shared, routed):
        sh = np.zeros((D, NSC * P), f4)
        sh[:, 0:SH] = np.asarray(shared)
        sh = sh.reshape(KC, P, NSC, P).transpose(2, 1, 0, 3)
        ro = np.asarray(routed).reshape(2, EG, KC, P, NU, UNIT).transpose(4, 0, 3, 2, 1, 5)
        return np.concatenate([sh, ro.reshape(NEC, P, KC, P)], 0)

    sh2 = np.zeros((NSC * P, D), f4)
    sh2[0:SH] = np.asarray(L0_ffn_sw2)
    ro2 = np.asarray(L0_ffn_w2).reshape(2, EG, NU, UNIT, D).transpose(2, 0, 1, 3, 4).reshape(NEC, P, D)
    w2 = np.concatenate([sh2.reshape(NSC, P, D), ro2], 0)
    w13 = np.stack([up_chunks(L0_ffn_sw1, L0_ffn_w1), up_chunks(L0_ffn_sw3, L0_ffn_w3)], 2)
    wch = np.concatenate([w13.reshape(NC, P, 2 * D), w2], 2)
    gate = np.asarray(L0_ffn_gate_w).reshape(E, KC, P).transpose(2, 1, 0)
    lower = (np.arange(E)[None, :] < np.arange(E)[:, None]).astype(f4)
    return {
        "wch": a(wch), "gate": a(gate), "bias": a(np.asarray(L0_ffn_expert_bias)), "lower": lower,
        "ctx": a(np.asarray(ctx_2048).reshape(T, D)), "wx": wx,
        "x": a(np.asarray(x).reshape(T, D)), "wqk": a(wqk), "wv": a(wv), "wo": a(wo),
        "cos_sin": a(cs), "mask": a(mask), "ident": np.eye(P, dtype=f4),
    }


def kernel(**inputs):
    import concourse.bacc as _bacc
    from concourse.bass_utils import run_bass_kernel_spmd as _run

    nc = _bacc.Bacc("TRN2", target_bir_lowering=False, num_devices=1)
    arrays = {f"in_{n}": v for n, v in layout(**inputs).items()}
    d = {n[3:]: nc.dram_tensor(n, v.shape, mybir.dt.from_np(v.dtype), kind="ExternalInput").ap()
         for n, v in arrays.items()}
    out = nc.dram_tensor("out", (T, D), F32, kind="ExternalOutput").ap()
    decoder_layer(nc, d, out)
    r = _run(nc, [arrays], core_ids=[0])
    return r.results[0]["out"].reshape(B, SEQ, D)
```
